# Optimizing a Trainium2 kernel written in Bass

```python
import numpy as np
import jax
import jax.numpy as jnp

def _softmax(x, axis=-1):
    return jax.nn.softmax(x, axis=axis)

def _gelu(x):
    return jax.nn.gelu(x, approximate=True)

def _silu(x):
    return jax.nn.silu(x)

def _sigmoid(x):
    return jax.nn.sigmoid(x)

def _layernorm(x, axis=-1, eps=1e-05):
    m = jnp.mean(x, axis=axis, keepdims=True)
    v = jnp.var(x, axis=axis, keepdims=True)
    return (x - m) / jnp.sqrt(v + eps)

def _scatter_add(tgt, idx, src, axis=0):
    return tgt.at[idx].add(src)

def _segment_sum(src, seg, n):
    return jax.ops.segment_sum(src, seg, n)
kernel_name = 'mk_decoder_postln_d4_seqx_r4_a3b4cc'

def setup_inputs(seed: int=0):
    np.random.seed(seed)
    _w = jnp.asarray

    def _rec_inputs():
        import jax
        import jax.numpy as jnp
        _rk = jax.random.key(seed)
        x = -0.0003929 + 0.9999 * jax.random.normal(jax.random.fold_in(_rk, 1), (2, 512, 256), jnp.float32)
        _lenS = 512 - jax.random.randint(jax.random.fold_in(_rk, 7), (2,), 0, max(1, 512 // 4) + 1, jnp.int32)
        _lenS2 = 1024 - jax.random.randint(jax.random.fold_in(_rk, 8), (2,), 0, max(1, 1024 // 4) + 1, jnp.int32)
        _ctx_768P = jax.random.normal(jax.random.fold_in(_rk, 11), (2, 16, 192), jnp.float32)
        _ctx_768c = jax.random.dirichlet(jax.random.fold_in(_rk, 511), 0.3 * jnp.ones((16,), jnp.float32), (2, 1024))
        _ctx_768t = jnp.einsum('bsk,bkd->bsd', _ctx_768c, _ctx_768P)
        _ctx_768t = _ctx_768t * jax.lax.rsqrt(jnp.mean(jnp.square(_ctx_768t)) + 1e-12) * 0.953939
        ctx_768 = 2.09791e-05 + 1.00001 * (_ctx_768t + 0.3 * jax.random.normal(jax.random.fold_in(_rk, 611), (2, 1024, 192), jnp.float32))
        _validS = jnp.arange(512)[None, :] < _lenS[:, None]
        _validS2 = jnp.arange(1024)[None, :] < _lenS2[:, None]
        _causal = jnp.tril(jnp.ones((512, 512), dtype=bool))
        mask_BxS2_bk0 = jnp.logical_not(jnp.broadcast_to(_validS2[:, :], (2, 1024)))
        return (x, ctx_768, mask_BxS2_bk0)
    x, ctx_768, mask_BxS2_bk0 = _rec_inputs()

    def _L0_attn_setup():
        import jax, jax.numpy as jnp
        import numpy as np
        D = 256
        H = 16
        KVH = 4
        HD = D // H
        LAT = 64
        WIN = 64
        B, S = (1, 512)
        BASE_G, BASE_L = (1000000.0, 10000.0)
        EPS = 1e-06

        def rmsnorm(x, w):
            return x * jax.lax.rsqrt(jnp.mean(x * x, axis=-1, keepdims=True) + EPS) * w

        def qk_norm(x):
            return x * jax.lax.rsqrt(jnp.mean(x * x, axis=-1, keepdims=True) + EPS)

        def rope(x, base):
            s, hd = (x.shape[-2], x.shape[-1])
            inv_freq = 1.0 / base ** (jnp.arange(0, hd, 2, dtype=jnp.float32) / hd)
            freqs = jnp.arange(s, dtype=jnp.float32)[:, None] * inv_freq[None, :]
            cos, sin = (jnp.cos(freqs), jnp.sin(freqs))
            xe, xo = (x[..., ::2], x[..., 1::2])
            out = jnp.stack([xe * cos - xo * sin, xe * sin + xo * cos], axis=-1)
            return out.reshape(x.shape)

        def split_heads(x, n_heads):
            b, s, _ = x.shape
            return x.reshape(b, s, n_heads, HD).transpose(0, 2, 1, 3)

        def repeat_kv(x):
            return jnp.repeat(x, H // KVH, axis=1)

        def sdpa(q, k, v, mask):
            scores = jnp.einsum('bhqd,bhkd->bhqk', q, k) / np.sqrt(HD).astype(np.float32)
            scores = jnp.where(mask, scores, jnp.float32(-1e+30))
            probs = jax.nn.softmax(scores, axis=-1)
            return jnp.einsum('bhqk,bhkd->bhqd', probs, v)

        def merge_heads(x):
            b, h, s, hd = x.shape
            return x.transpose(0, 2, 1, 3).reshape(b, s, h * hd)

        def global_latent_attn(x, wq, w_kv_down, w_k_up, w_v_up, wo):
            q = split_heads(x @ wq, H)
            latent = x @ w_kv_down
            k = split_heads(latent @ w_k_up, KVH)
            v = split_heads(latent @ w_v_up, KVH)
            q, k = (rope(q, BASE_G), rope(k, BASE_G))
            q, k = (qk_norm(q), qk_norm(k))
            k, v = (repeat_kv(k), repeat_kv(v))
            i = jnp.arange(x.shape[1])
            causal = i[:, None] >= i[None, :]
            return merge_heads(sdpa(q, k, v, causal)) @ wo

        def local_gqa_attn(x, wq, wk, wv, wo):
            q = split_heads(x @ wq, H)
            k = split_heads(x @ wk, KVH)
            v = split_heads(x @ wv, KVH)
            q, k = (rope(q, BASE_L), rope(k, BASE_L))
            q, k = (qk_norm(q), qk_norm(k))
            k, v = (repeat_kv(k), repeat_kv(v))
            i = jnp.arange(x.shape[1])
            diff = i[:, None] - i[None, :]
            mask = (diff >= 0) & (diff < WIN)
            return merge_heads(sdpa(q, k, v, mask)) @ wo
        key = jax.random.key(seed)
        ks = jax.random.split(key, 12)
        std = 0.02
        return {'hidden': jax.random.normal(ks[0], (B, S, D), dtype=jnp.float32), 'norm1_w': jnp.ones((D,), jnp.float32), 'norm2_w': jnp.ones((D,), jnp.float32), 'g_wq': jax.random.normal(ks[1], (D, H * HD), jnp.float32) * std, 'g_kv_down': jax.random.normal(ks[2], (D, LAT), jnp.float32) * std, 'g_k_up': jax.random.normal(ks[3], (LAT, KVH * HD), jnp.float32) * std, 'g_v_up': jax.random.normal(ks[4], (LAT, KVH * HD), jnp.float32) * std, 'g_wo': jax.random.normal(ks[5], (D, D), jnp.float32) * std, 'l_wq': jax.random.normal(ks[6], (D, H * HD), jnp.float32) * std, 'l_wk': jax.random.normal(ks[7], (D, KVH * HD), jnp.float32) * std, 'l_wv': jax.random.normal(ks[8], (D, KVH * HD), jnp.float32) * std, 'l_wo': jax.random.normal(ks[9], (D, D), jnp.float32) * std}
    _L0_attn_all = _L0_attn_setup()
    _L0_attn_in = {k: v for k, v in _L0_attn_all.items() if k in ('norm1_w', 'norm2_w', 'g_wq', 'g_kv_down', 'g_k_up', 'g_v_up', 'g_wo', 'l_wq', 'l_wk', 'l_wv', 'l_wo')}
    del _L0_attn_all

    def _L0_xattn_setup():
        import jax, jax.numpy as jnp
        import numpy as np
        QUERY_DIM = 256
        KEY_DIM = 192
        NUM_HEADS = 16
        HEAD_DIM = QUERY_DIM // NUM_HEADS
        SCALE = HEAD_DIM ** (-0.5)
        key = jax.random.key(seed)
        ks = jax.random.split(key, 11)
        B, Nq, Nk = (4, 1024, 256)
        s_q = QUERY_DIM ** (-0.5)
        s_k = KEY_DIM ** (-0.5)
        return {'query': jax.random.normal(ks[0], (B, Nq, QUERY_DIM), jnp.float32), 'key': jax.random.normal(ks[1], (B, Nk, KEY_DIM), jnp.float32), 'value': jax.random.normal(ks[2], (B, Nk, KEY_DIM), jnp.float32), 'Wq': jax.random.normal(ks[3], (QUERY_DIM, QUERY_DIM), jnp.float32) * s_q, 'bq': jnp.zeros((QUERY_DIM,), jnp.float32), 'Wk': jax.random.normal(ks[4], (KEY_DIM, QUERY_DIM), jnp.float32) * s_k, 'bk': jnp.zeros((QUERY_DIM,), jnp.float32), 'Wv': jax.random.normal(ks[5], (KEY_DIM, QUERY_DIM), jnp.float32) * s_k, 'bv': jnp.zeros((QUERY_DIM,), jnp.float32), 'Wo': jax.random.normal(ks[6], (QUERY_DIM, QUERY_DIM), jnp.float32) * s_q, 'bo': jnp.zeros((QUERY_DIM,), jnp.float32)}
    _L0_xattn_all = _L0_xattn_setup()
    _L0_xattn_in = {k: v for k, v in _L0_xattn_all.items() if k in ('Wq', 'bq', 'Wk', 'bk', 'Wv', 'bv', 'Wo', 'bo')}
    del _L0_xattn_all

    def _L0_ffn_setup():
        import jax, jax.numpy as jnp
        import numpy as np
        DIM = 256
        DEPTH = 6
        HEADS = 16
        DIM_HEAD = 64
        WINDOW = 64
        INNER = HEADS * DIM_HEAD
        DIM_INNER = int(DIM * 4 * 2 / 3)
        QK_SCALE = 8.0

        def shift_tokens(t):
            a, s = jnp.split(t, 2, -1)
            s = jnp.pad(s, ((0, 0), (1, 0), (0, 0)))[:, :-1]
            return jnp.concatenate([a, s], -1)

        def l2norm(t):
            return t / jnp.maximum(jnp.linalg.norm(t, axis=-1, keepdims=True), 1e-12)

        def rotate_half(x):
            x1, x2 = jnp.split(x, 2, -1)
            return jnp.concatenate([-x2, x1], -1)

        def rotary_tables(n):
            half = jnp.arange(0, DIM_HEAD, 2, dtype=jnp.float32)
            inv_freq = 1.0 / 10000.0 ** (half / DIM_HEAD)
            t = jnp.arange(n, dtype=jnp.float32)
            freqs = t[:, None] * inv_freq[None, :]
            freqs = jnp.concatenate([freqs, freqs], -1)
            base_scale = (half + 0.4 * DIM_HEAD) / (1.4 * DIM_HEAD)
            power = (t - n // 2) / (WINDOW // 2)
            scale = base_scale[None, :] ** power[:, None]
            scale = jnp.concatenate([scale, scale], -1)
            return (freqs, scale)

        def local_attention(q, k, v):
            b, h, n, d = q.shape
            w = WINDOW
            nw = n // w
            bq = q.reshape(b, h, nw, w, d)
            bk = k.reshape(b, h, nw, w, d)
            bv = v.reshape(b, h, nw, w, d)

            def look(t):
                p = jnp.pad(t, ((0, 0), (0, 0), (1, 0), (0, 0), (0, 0)))
                return jnp.concatenate([p[:, :, :nw], p[:, :, 1:]], axis=3)
            bk2, bv2 = (look(bk), look(bv))
            seq = jnp.arange(n).reshape(nw, w)
            seq_p = jnp.pad(seq, ((1, 0), (0, 0)), constant_values=-1)
            jt = jnp.concatenate([seq_p[:nw], seq_p[1:]], axis=1)
            it = seq[:, :, None]
            jb = jt[:, None, :]
            mask = (it < jb) | (it > jb + w) | (jb == -1)
            sim = jnp.einsum('bhwie,bhwje->bhwij', bq, bk2) * QK_SCALE
            sim = jnp.where(mask, -jnp.finfo(sim.dtype).max, sim)
            attn = jax.nn.softmax(sim, -1)
            out = jnp.einsum('bhwij,bhwje->bhwie', attn, bv2)
            return out.reshape(b, h, n, d)

        def attn_layer(x, Wqkv, qs, ksc, Wo):
            b, n, _ = x.shape
            qkv = x @ Wqkv
            q, k, v = jnp.split(qkv, 3, -1)
            sh = lambda t: t.reshape(b, n, HEADS, DIM_HEAD).transpose(0, 2, 1, 3)
            q, k, v = (sh(q), sh(k), sh(v))
            q = l2norm(q) * qs
            k = l2norm(k) * ksc
            freqs, scale = rotary_tables(n)
            cos, sin = (jnp.cos(freqs), jnp.sin(freqs))
            q = q * cos * scale + rotate_half(q) * sin * scale
            inv = 1.0 / scale
            k = k * cos * inv + rotate_half(k) * sin * inv
            out = local_attention(q, k, v)
            out = out.transpose(0, 2, 1, 3).reshape(b, n, INNER)
            return out @ Wo

        def ffn_layer(x, g, bln, W1, b1, W2, b2):
            mu = x.mean(-1, keepdims=True)
            var = ((x - mu) ** 2).mean(-1, keepdims=True)
            xn = (x - mu) / jnp.sqrt(var + 1e-05) * g + bln
            hg = xn @ W1 + b1
            a, gate = jnp.split(hg, 2, -1)
            return a * jax.nn.gelu(gate, approximate=False) @ W2 + b2
        key = jax.random.key(seed)
        ks = jax.random.split(key, 8)
        B, N = (2, 512)
        init = lambda k, shape: jax.random.normal(k, shape, jnp.float32) * 0.02
        return {'x': jax.random.normal(ks[0], (B, N, DIM), jnp.float32), 'Wqkv': init(ks[1], (DEPTH, DIM, 3 * INNER)), 'q_scale': jnp.ones((DEPTH, DIM_HEAD), jnp.float32), 'k_scale': jnp.ones((DEPTH, DIM_HEAD), jnp.float32), 'Wo': init(ks[2], (DEPTH, INNER, DIM)), 'ln_g': jnp.ones((DEPTH, DIM), jnp.float32), 'ln_b': jnp.zeros((DEPTH, DIM), jnp.float32), 'W1': init(ks[3], (DEPTH, DIM, 2 * DIM_INNER)), 'b1': jnp.zeros((DEPTH, 2 * DIM_INNER), jnp.float32), 'W2': init(ks[4], (DEPTH, DIM_INNER, DIM)), 'b2': jnp.zeros((DEPTH, DIM), jnp.float32)}
    _L0_ffn_all = _L0_ffn_setup()
    _L0_ffn_in = {k: v for k, v in _L0_ffn_all.items() if k in ('Wqkv', 'q_scale', 'k_scale', 'Wo', 'ln_g', 'ln_b', 'W1', 'b1', 'W2', 'b2')}
    del _L0_ffn_all

    def _L1_attn_setup():
        import jax, jax.numpy as jnp
        import numpy as np
        import math
        EPS = 1e-06
        H = 16

        def favorplus_features(x, proj, eps=EPS):
            xw = jnp.einsum('bhtd,hmd->bhtm', x, proj)
            xw = xw - jnp.max(xw, axis=-1, keepdims=True)
            exp_part = jnp.exp(xw)
            x_norm_sq = jnp.sum(x * x, axis=-1, keepdims=True)
            base = jnp.exp(-0.5 * x_norm_sq)
            return exp_part * base + eps
        key = jax.random.key(seed)
        ks = jax.random.split(key, 7)
        B, T, d = (4, 1024, 256)
        h, m = (H, 64)
        dk = d // h
        s = 1.0 / math.sqrt(d)
        return {'x': jax.random.normal(ks[0], (B, T, d), jnp.float32), 'Wq': jax.random.normal(ks[1], (d, d), jnp.float32) * s, 'Wk': jax.random.normal(ks[2], (d, d), jnp.float32) * s, 'Wv': jax.random.normal(ks[3], (d, d), jnp.float32) * s, 'Wo': jax.random.normal(ks[4], (d, d), jnp.float32) * s, 'bo': jnp.zeros((d,), jnp.float32), 'proj': jax.random.normal(ks[5], (h, m, dk), jnp.float32)}
    _L1_attn_all = _L1_attn_setup()
    _L1_attn_in = {k: v for k, v in _L1_attn_all.items() if k in ('Wq', 'Wk', 'Wv', 'Wo', 'bo', 'proj')}
    del _L1_attn_all

    def _L1_xattn_setup():
        import jax, jax.numpy as jnp
        import numpy as np
        HEADS = 16
        DIM_HEAD = 64
        key = jax.random.key(seed)
        ks = jax.random.split(key, 7)
        b, n, m = (2, 512, 256)
        query_dim, context_dim = (256, 192)
        inner = HEADS * DIM_HEAD
        s_q = 1.0 / np.sqrt(query_dim)
        s_c = 1.0 / np.sqrt(context_dim)
        s_i = 1.0 / np.sqrt(inner)
        return {'x': jax.random.normal(ks[0], (b, n, query_dim), jnp.float32), 'context': jax.random.normal(ks[1], (b, m, context_dim), jnp.float32), 'Wq': jax.random.normal(ks[2], (query_dim, inner), jnp.float32) * s_q, 'Wk': jax.random.normal(ks[3], (context_dim, inner), jnp.float32) * s_c, 'Wv': jax.random.normal(ks[4], (context_dim, inner), jnp.float32) * s_c, 'Wo': jax.random.normal(ks[5], (inner, query_dim), jnp.float32) * s_i, 'bo': jax.random.normal(ks[6], (query_dim,), jnp.float32) * 0.01}
    _L1_xattn_all = _L1_xattn_setup()
    _L1_xattn_in = {k: v for k, v in _L1_xattn_all.items() if k in ('Wq', 'Wk', 'Wv', 'Wo', 'bo')}
    del _L1_xattn_all

    def _L1_ffn_setup():
        import jax, jax.numpy as jnp
        import numpy as np
        BLOCK = 32
        W_BITS = 4
        ACT_BITS = 16

        def act_qdq(x):
            qmax = 2.0 ** (ACT_BITS - 1) - 1.0
            scale = jnp.maximum(jnp.max(jnp.abs(x)) / qmax, 1e-12)
            return jnp.clip(jnp.round(x / scale), -qmax - 1.0, qmax) * scale

        def fixed_qdq_u16(x):
            scale = 1.0 / 65536.0
            return jnp.clip(jnp.round(x / scale), 0.0, 65535.0) * scale

        def lpbq_dequant(w):
            O, I = w.shape
            qmax = 2.0 ** (W_BITS - 1) - 1.0
            wb = w.reshape(O, I // BLOCK, BLOCK)
            s = jnp.maximum(jnp.max(jnp.abs(wb), axis=-1, keepdims=True) / qmax, 1e-12)
            wq = jnp.clip(jnp.round(wb / s), -qmax - 1.0, qmax) * s
            return wq.reshape(O, I)
        key = jax.random.key(seed)
        k1, k2, k3, k4 = jax.random.split(key, 4)
        B, S, H, I = (2, 1024, 256, 768)
        x = jax.random.normal(k1, (B, S, H), jnp.float32)
        w_gate = jax.random.normal(k2, (I, H), jnp.float32) * 0.02
        w_up = jax.random.normal(k3, (I, H), jnp.float32) * 0.02
        w_down = jax.random.normal(k4, (H, I), jnp.float32) * 0.02
        return {'x': x, 'w_gate': w_gate, 'w_up': w_up, 'w_down': w_down}
    _L1_ffn_all = _L1_ffn_setup()
    _L1_ffn_in = {k: v for k, v in _L1_ffn_all.items() if k in ('w_gate', 'w_up', 'w_down')}
    del _L1_ffn_all

    def _L2_attn_setup():
        import jax, jax.numpy as jnp
        import numpy as np
        D_MODEL = 256
        N_QK = 32
        D_QK = 32
        N_OV = 512
        D_OV = 1
        SEQ = 256
        BATCH = 2
        VKV = 16
        ROT_DIM = 32
        ROT_BASE = 10000.0
        SCALE = D_QK ** 0.5

        def _kaiming(k, shape, fan_in):
            return jax.random.normal(k, shape, jnp.float32) * np.sqrt(2.0 / fan_in)

        def _rotary_sin_cos(n_ctx, rd, base):
            pos = jnp.arange(n_ctx, dtype=jnp.float32)
            dim = jnp.arange(rd // 2, dtype=jnp.float32)
            freq = base ** (dim / (rd / 2))
            freq = jnp.concatenate([freq, freq])
            angles = pos[:, None] / freq[None, :]
            return (jnp.sin(angles), jnp.cos(angles))

        def _apply_rotary(x, sin, cos, rd):
            s = x.shape[1]
            x_rot, x_pass = (x[..., :rd], x[..., rd:])
            flip = jnp.concatenate([-x_rot[..., rd // 2:], x_rot[..., :rd // 2]], axis=-1)
            rot = x_rot * cos[None, :s, None, :] + flip * sin[None, :s, None, :]
            return jnp.concatenate([rot, x_pass], axis=-1)
        key = jax.random.key(seed)
        ks = jax.random.split(key, 7)
        return {'resid': jax.random.normal(ks[0], (BATCH, SEQ, D_MODEL), jnp.float32), 'W_Q': _kaiming(ks[1], (N_QK, D_MODEL, D_QK), D_MODEL * D_QK), 'W_K': _kaiming(ks[2], (N_QK, D_MODEL, D_QK), D_MODEL * D_QK), 'W_V': _kaiming(ks[3], (N_OV, D_MODEL, D_OV), D_MODEL * D_OV), 'W_O': _kaiming(ks[4], (N_OV, D_OV, D_MODEL), D_OV * D_MODEL), 'b_Q': jnp.zeros((N_QK, D_QK), jnp.float32), 'b_K': jnp.zeros((N_QK, D_QK), jnp.float32), 'b_V': jnp.zeros((N_OV, D_OV), jnp.float32), 'virtual_k': _kaiming(ks[5], (VKV, N_QK, D_QK), N_QK * D_QK), 'virtual_v': jnp.zeros((VKV, N_OV, D_OV), jnp.float32)}
    _L2_attn_all = _L2_attn_setup()
    _L2_attn_in = {k: v for k, v in _L2_attn_all.items() if k in ('W_Q', 'W_K', 'W_V', 'W_O', 'b_Q', 'b_K', 'b_V', 'virtual_k', 'virtual_v')}
    del _L2_attn_all

    def _L2_xattn_setup():
        import jax, jax.numpy as jnp
        import numpy as np
        DIM_IN, DIM_LAT, DIM_HEAD = (192, 256, 64)
        INNER = max(DIM_LAT, DIM_IN)
        HEADS = INNER // DIM_HEAD
        SCALE = DIM_HEAD ** (-0.5)
        RMS_EPS = 1e-08
        LN_EPS = 1e-05

        def layernorm(x, g, b):
            mu = jnp.mean(x, axis=-1, keepdims=True)
            var = jnp.mean((x - mu) ** 2, axis=-1, keepdims=True)
            return (x - mu) * jax.lax.rsqrt(var + LN_EPS) * g + b

        def rmsnorm(x, gamma):
            norm = jnp.sqrt(jnp.sum(x * x, axis=-1, keepdims=True)) * x.shape[-1] ** (-0.5)
            return x / jnp.maximum(norm, RMS_EPS) * gamma
        key = jax.random.key(seed)
        ks = jax.random.split(key, 12)
        b, n, m = (4, 1024, 128)
        x = jax.random.normal(ks[0], (b, n, DIM_IN), jnp.float32)
        latents = jax.random.normal(ks[1], (b, m, DIM_LAT), jnp.float32)
        mask = jax.random.randint(ks[2], (b, n), 0, 2).astype(bool)
        s = lambda k, sh, fan: jax.random.normal(k, sh, jnp.float32) * fan ** (-0.5)
        return {'x': x, 'latents': latents, 'mask': mask, 'ln_x_g': jnp.ones((DIM_IN,), jnp.float32), 'ln_x_b': jnp.zeros((DIM_IN,), jnp.float32), 'ln_l_g': jnp.ones((DIM_LAT,), jnp.float32), 'ln_l_b': jnp.zeros((DIM_LAT,), jnp.float32), 'qn_g': jnp.ones((DIM_HEAD,), jnp.float32), 'kn_g': jnp.ones((DIM_HEAD,), jnp.float32), 'Wq': s(ks[3], (INNER, DIM_LAT), DIM_LAT), 'Wkv': s(ks[4], (2 * INNER, DIM_IN), DIM_IN), 'Wlkv': s(ks[5], (2 * INNER, DIM_LAT), DIM_LAT), 'Wo': s(ks[6], (DIM_LAT, INNER), INNER), 'bo': jnp.zeros((DIM_LAT,), jnp.float32)}
    _L2_xattn_all = _L2_xattn_setup()
    _L2_xattn_in = {k: v for k, v in _L2_xattn_all.items() if k in ('ln_x_g', 'ln_x_b', 'ln_l_g', 'ln_l_b', 'qn_g', 'kn_g', 'Wq', 'Wkv', 'Wlkv', 'Wo', 'bo')}
    del _L2_xattn_all

    def _L2_ffn_setup():
        import jax, jax.numpy as jnp
        import numpy as np
        E = 16
        G = 4
        EPG = E // G
        K = 4
        TOPK_GROUP = 2
        PER_GROUP_K = K // TOPK_GROUP

        def _route(xf, router_w, correction_bias):
            S = xf.shape[0]
            logits = xf @ router_w.T
            scores = jax.nn.sigmoid(logits)
            sb = scores + correction_bias
            grp_top = jax.lax.top_k(sb.reshape(S, G, EPG), PER_GROUP_K)[0]
            group_scores = grp_top.sum(axis=-1)
            _, group_idx = jax.lax.top_k(group_scores, TOPK_GROUP)
            group_mask = jnp.zeros((S, G), sb.dtype).at[jnp.arange(S)[:, None], group_idx].set(1.0)
            score_mask = jnp.broadcast_to(group_mask[:, :, None], (S, G, EPG)).reshape(S, E)
            masked = jnp.where(score_mask > 0, sb, -jnp.inf)
            _, topk_idx = jax.lax.top_k(masked, K)
            w = jnp.take_along_axis(scores, topk_idx, axis=1)
            w = w / (w.sum(axis=-1, keepdims=True) + 1e-20)
            return (topk_idx, w, scores)
        key = jax.random.key(seed)
        ks = jax.random.split(key, 9)
        B, T, C, H, HS = (2, 256, 256, 64, 512)
        std = 0.02
        return {'x': jax.random.normal(ks[0], (B, T, C), jnp.float32), 'router_w': jax.random.normal(ks[1], (E, C), jnp.float32) * std, 'correction_bias': jnp.zeros((E,), jnp.float32), 'gate_w': jax.random.normal(ks[2], (E, C, H), jnp.float32) * std, 'up_w': jax.random.normal(ks[3], (E, C, H), jnp.float32) * std, 'down_w': jax.random.normal(ks[4], (E, H, C), jnp.float32) * std, 'shared_gate_w': jax.random.normal(ks[5], (HS, C), jnp.float32) * std, 'shared_up_w': jax.random.normal(ks[6], (HS, C), jnp.float32) * std, 'shared_down_w': jax.random.normal(ks[7], (C, HS), jnp.float32) * std}
    _L2_ffn_all = _L2_ffn_setup()
    _L2_ffn_in = {k: v for k, v in _L2_ffn_all.items() if k in ('router_w', 'correction_bias', 'gate_w', 'up_w', 'down_w', 'shared_gate_w', 'shared_up_w', 'shared_down_w')}
    del _L2_ffn_all

    def _L3_attn_setup():
        import jax, jax.numpy as jnp
        import numpy as np
        B, T, D, H = (4, 512, 256, 16)
        HEAD_DIM = D // H
        LOCAL_WINDOW = 128

        def _rotate_half(t):
            t1, t2 = jnp.split(t, 2, axis=-1)
            return jnp.concatenate([-t2, t1], axis=-1)

        def _apply_rope(q, k):
            Tq, d = (q.shape[2], q.shape[3])
            half = d // 2
            theta = 1.0 / 10000.0 ** (jnp.arange(half, dtype=jnp.float32) / half)
            pos = jnp.arange(Tq, dtype=jnp.float32)
            freqs = pos[:, None] * theta[None, :]
            freqs = jnp.concatenate([freqs, freqs], axis=-1)
            cos = jnp.cos(freqs)[None, None]
            sin = jnp.sin(freqs)[None, None]
            q = q * cos + _rotate_half(q) * sin
            k = k * cos + _rotate_half(k) * sin
            return (q, k)
        key = jax.random.key(seed)
        k1, k2, k3 = jax.random.split(key, 3)
        x = jax.random.normal(k1, (B, T, D), dtype=jnp.float32)
        Wqkv = jax.random.normal(k2, (D, 3 * D), dtype=jnp.float32) * 0.02
        Wout = jax.random.normal(k3, (D, D), dtype=jnp.float32) * 0.02
        return {'x': x, 'Wqkv': Wqkv, 'Wout': Wout}
    _L3_attn_all = _L3_attn_setup()
    _L3_attn_in = {k: v for k, v in _L3_attn_all.items() if k in ('Wqkv', 'Wout')}
    del _L3_attn_all

    def _L3_xattn_setup():
        import jax, jax.numpy as jnp
        import numpy as np
        NUM_HEADS = 16
        CLAMP = 10000.0
        key = jax.random.key(seed)
        ks = jax.random.split(key, 8)
        B, Nq, Nkv, Cq, Ckv = (4, 512, 512, 256, 192)
        s_q = 1.0 / np.sqrt(Cq)
        s_kv = 1.0 / np.sqrt(Ckv)
        return {'query': jax.random.normal(ks[0], (B, Nq, Cq), jnp.float32), 'key_value': jax.random.normal(ks[1], (B, Nkv, Ckv), jnp.float32), 'Wq': jax.random.normal(ks[2], (Cq, Cq), jnp.float32) * s_q, 'bq': jnp.zeros((Cq,), jnp.float32), 'Wk': jax.random.normal(ks[3], (Ckv, Cq), jnp.float32) * s_kv, 'bk': jnp.zeros((Cq,), jnp.float32), 'Wv': jax.random.normal(ks[4], (Ckv, Cq), jnp.float32) * s_kv, 'bv': jnp.zeros((Cq,), jnp.float32), 'Wo': jax.random.normal(ks[5], (Cq, Cq), jnp.float32) * s_q, 'bo': jnp.zeros((Cq,), jnp.float32)}
    _L3_xattn_all = _L3_xattn_setup()
    _L3_xattn_in = {k: v for k, v in _L3_xattn_all.items() if k in ('Wq', 'bq', 'Wk', 'bk', 'Wv', 'bv', 'Wo', 'bo')}
    del _L3_xattn_all

    def _L3_ffn_setup():
        import jax, jax.numpy as jnp
        import numpy as np
        B, S, H = (2, 512, 256)
        I = 128
        E_R, E_Z = (32, 8)
        E_T = E_R + E_Z
        K = 6
        SCALE = 2.5
        W_INIT = 0.02
        key = jax.random.key(seed)
        k0, k1, k2, k3 = jax.random.split(key, 4)
        return {'hidden_states': jax.random.normal(k0, (B, S, H), jnp.float32), 'classifier_weight': jax.random.normal(k1, (E_T, H), jnp.float32) * W_INIT, 'e_score_correction_bias': jnp.zeros((E_T,), jnp.float32), 'gate_up_proj': jax.random.normal(k2, (E_T, 2 * I, H), jnp.float32) * W_INIT, 'down_proj': jax.random.normal(k3, (E_R, H, I), jnp.float32) * W_INIT}
    _L3_ffn_all = _L3_ffn_setup()
    _L3_ffn_in = {k: v for k, v in _L3_ffn_all.items() if k in ('classifier_weight', 'e_score_correction_bias', 'gate_up_proj', 'down_proj')}
    del _L3_ffn_all
    return {'x': x, 'ctx_768': ctx_768, 'mask_BxS2_bk0': mask_BxS2_bk0, 'L0_attn_norm1_w': _L0_attn_in['norm1_w'], 'L0_attn_norm2_w': _L0_attn_in['norm2_w'], 'L0_attn_g_wq': _L0_attn_in['g_wq'], 'L0_attn_g_kv_down': _L0_attn_in['g_kv_down'], 'L0_attn_g_k_up': _L0_attn_in['g_k_up'], 'L0_attn_g_v_up': _L0_attn_in['g_v_up'], 'L0_attn_g_wo': _L0_attn_in['g_wo'], 'L0_attn_l_wq': _L0_attn_in['l_wq'], 'L0_attn_l_wk': _L0_attn_in['l_wk'], 'L0_attn_l_wv': _L0_attn_in['l_wv'], 'L0_attn_l_wo': _L0_attn_in['l_wo'], 'L0_xattn_Wq': _L0_xattn_in['Wq'], 'L0_xattn_bq': _L0_xattn_in['bq'], 'L0_xattn_Wk': _L0_xattn_in['Wk'], 'L0_xattn_bk': _L0_xattn_in['bk'], 'L0_xattn_Wv': _L0_xattn_in['Wv'], 'L0_xattn_bv': _L0_xattn_in['bv'], 'L0_xattn_Wo': _L0_xattn_in['Wo'], 'L0_xattn_bo': _L0_xattn_in['bo'], 'L0_ffn_Wqkv': _L0_ffn_in['Wqkv'], 'L0_ffn_q_scale': _L0_ffn_in['q_scale'], 'L0_ffn_k_scale': _L0_ffn_in['k_scale'], 'L0_ffn_Wo': _L0_ffn_in['Wo'], 'L0_ffn_ln_g': _L0_ffn_in['ln_g'], 'L0_ffn_ln_b': _L0_ffn_in['ln_b'], 'L0_ffn_W1': _L0_ffn_in['W1'], 'L0_ffn_b1': _L0_ffn_in['b1'], 'L0_ffn_W2': _L0_ffn_in['W2'], 'L0_ffn_b2': _L0_ffn_in['b2'], 'L1_attn_Wq': _L1_attn_in['Wq'], 'L1_attn_Wk': _L1_attn_in['Wk'], 'L1_attn_Wv': _L1_attn_in['Wv'], 'L1_attn_Wo': _L1_attn_in['Wo'], 'L1_attn_bo': _L1_attn_in['bo'], 'L1_attn_proj': _L1_attn_in['proj'], 'L1_xattn_Wq': _L1_xattn_in['Wq'], 'L1_xattn_Wk': _L1_xattn_in['Wk'], 'L1_xattn_Wv': _L1_xattn_in['Wv'], 'L1_xattn_Wo': _L1_xattn_in['Wo'], 'L1_xattn_bo': _L1_xattn_in['bo'], 'L1_ffn_w_gate': _L1_ffn_in['w_gate'], 'L1_ffn_w_up': _L1_ffn_in['w_up'], 'L1_ffn_w_down': _L1_ffn_in['w_down'], 'L2_attn_W_Q': _L2_attn_in['W_Q'], 'L2_attn_W_K': _L2_attn_in['W_K'], 'L2_attn_W_V': _L2_attn_in['W_V'], 'L2_attn_W_O': _L2_attn_in['W_O'], 'L2_attn_b_Q': _L2_attn_in['b_Q'], 'L2_attn_b_K': _L2_attn_in['b_K'], 'L2_attn_b_V': _L2_attn_in['b_V'], 'L2_attn_virtual_k': _L2_attn_in['virtual_k'], 'L2_attn_virtual_v': _L2_attn_in['virtual_v'], 'L2_xattn_ln_x_g': _L2_xattn_in['ln_x_g'], 'L2_xattn_ln_x_b': _L2_xattn_in['ln_x_b'], 'L2_xattn_ln_l_g': _L2_xattn_in['ln_l_g'], 'L2_xattn_ln_l_b': _L2_xattn_in['ln_l_b'], 'L2_xattn_qn_g': _L2_xattn_in['qn_g'], 'L2_xattn_kn_g': _L2_xattn_in['kn_g'], 'L2_xattn_Wq': _L2_xattn_in['Wq'], 'L2_xattn_Wkv': _L2_xattn_in['Wkv'], 'L2_xattn_Wlkv': _L2_xattn_in['Wlkv'], 'L2_xattn_Wo': _L2_xattn_in['Wo'], 'L2_xattn_bo': _L2_xattn_in['bo'], 'L2_ffn_router_w': _L2_ffn_in['router_w'], 'L2_ffn_correction_bias': _L2_ffn_in['correction_bias'], 'L2_ffn_gate_w': _L2_ffn_in['gate_w'], 'L2_ffn_up_w': _L2_ffn_in['up_w'], 'L2_ffn_down_w': _L2_ffn_in['down_w'], 'L2_ffn_shared_gate_w': _L2_ffn_in['shared_gate_w'], 'L2_ffn_shared_up_w': _L2_ffn_in['shared_up_w'], 'L2_ffn_shared_down_w': _L2_ffn_in['shared_down_w'], 'L3_attn_Wqkv': _L3_attn_in['Wqkv'], 'L3_attn_Wout': _L3_attn_in['Wout'], 'L3_xattn_Wq': _L3_xattn_in['Wq'], 'L3_xattn_bq': _L3_xattn_in['bq'], 'L3_xattn_Wk': _L3_xattn_in['Wk'], 'L3_xattn_bk': _L3_xattn_in['bk'], 'L3_xattn_Wv': _L3_xattn_in['Wv'], 'L3_xattn_bv': _L3_xattn_in['bv'], 'L3_xattn_Wo': _L3_xattn_in['Wo'], 'L3_xattn_bo': _L3_xattn_in['bo'], 'L3_ffn_classifier_weight': _L3_ffn_in['classifier_weight'], 'L3_ffn_e_score_correction_bias': _L3_ffn_in['e_score_correction_bias'], 'L3_ffn_gate_up_proj': _L3_ffn_in['gate_up_proj'], 'L3_ffn_down_proj': _L3_ffn_in['down_proj']}

def reference(x, ctx_768, mask_BxS2_bk0, L0_attn_norm1_w, L0_attn_norm2_w, L0_attn_g_wq, L0_attn_g_kv_down, L0_attn_g_k_up, L0_attn_g_v_up, L0_attn_g_wo, L0_attn_l_wq, L0_attn_l_wk, L0_attn_l_wv, L0_attn_l_wo, L0_xattn_Wq, L0_xattn_bq, L0_xattn_Wk, L0_xattn_bk, L0_xattn_Wv, L0_xattn_bv, L0_xattn_Wo, L0_xattn_bo, L0_ffn_Wqkv, L0_ffn_q_scale, L0_ffn_k_scale, L0_ffn_Wo, L0_ffn_ln_g, L0_ffn_ln_b, L0_ffn_W1, L0_ffn_b1, L0_ffn_W2, L0_ffn_b2, L1_attn_Wq, L1_attn_Wk, L1_attn_Wv, L1_attn_Wo, L1_attn_bo, L1_attn_proj, L1_xattn_Wq, L1_xattn_Wk, L1_xattn_Wv, L1_xattn_Wo, L1_xattn_bo, L1_ffn_w_gate, L1_ffn_w_up, L1_ffn_w_down, L2_attn_W_Q, L2_attn_W_K, L2_attn_W_V, L2_attn_W_O, L2_attn_b_Q, L2_attn_b_K, L2_attn_b_V, L2_attn_virtual_k, L2_attn_virtual_v, L2_xattn_ln_x_g, L2_xattn_ln_x_b, L2_xattn_ln_l_g, L2_xattn_ln_l_b, L2_xattn_qn_g, L2_xattn_kn_g, L2_xattn_Wq, L2_xattn_Wkv, L2_xattn_Wlkv, L2_xattn_Wo, L2_xattn_bo, L2_ffn_router_w, L2_ffn_correction_bias, L2_ffn_gate_w, L2_ffn_up_w, L2_ffn_down_w, L2_ffn_shared_gate_w, L2_ffn_shared_up_w, L2_ffn_shared_down_w, L3_attn_Wqkv, L3_attn_Wout, L3_xattn_Wq, L3_xattn_bq, L3_xattn_Wk, L3_xattn_bk, L3_xattn_Wv, L3_xattn_bv, L3_xattn_Wo, L3_xattn_bo, L3_ffn_classifier_weight, L3_ffn_e_score_correction_bias, L3_ffn_gate_up_proj, L3_ffn_down_proj):
    import jax
    import jax.numpy as jnp

    def _L0_attn_ref(hidden, norm1_w, norm2_w, g_wq, g_kv_down, g_k_up, g_v_up, g_wo, l_wq, l_wk, l_wv, l_wo):
        import jax, jax.numpy as jnp
        import numpy as np
        D = 256
        H = 16
        KVH = 4
        HD = D // H
        LAT = 64
        WIN = 64
        B, S = (1, 512)
        BASE_G, BASE_L = (1000000.0, 10000.0)
        EPS = 1e-06

        def rmsnorm(x, w):
            return x * jax.lax.rsqrt(jnp.mean(x * x, axis=-1, keepdims=True) + EPS) * w

        def qk_norm(x):
            return x * jax.lax.rsqrt(jnp.mean(x * x, axis=-1, keepdims=True) + EPS)

        def rope(x, base):
            s, hd = (x.shape[-2], x.shape[-1])
            inv_freq = 1.0 / base ** (jnp.arange(0, hd, 2, dtype=jnp.float32) / hd)
            freqs = jnp.arange(s, dtype=jnp.float32)[:, None] * inv_freq[None, :]
            cos, sin = (jnp.cos(freqs), jnp.sin(freqs))
            xe, xo = (x[..., ::2], x[..., 1::2])
            out = jnp.stack([xe * cos - xo * sin, xe * sin + xo * cos], axis=-1)
            return out.reshape(x.shape)

        def split_heads(x, n_heads):
            b, s, _ = x.shape
            return x.reshape(b, s, n_heads, HD).transpose(0, 2, 1, 3)

        def repeat_kv(x):
            return jnp.repeat(x, H // KVH, axis=1)

        def sdpa(q, k, v, mask):
            scores = jnp.einsum('bhqd,bhkd->bhqk', q, k) / np.sqrt(HD).astype(np.float32)
            scores = jnp.where(mask, scores, jnp.float32(-1e+30))
            probs = jax.nn.softmax(scores, axis=-1)
            return jnp.einsum('bhqk,bhkd->bhqd', probs, v)

        def merge_heads(x):
            b, h, s, hd = x.shape
            return x.transpose(0, 2, 1, 3).reshape(b, s, h * hd)

        def global_latent_attn(x, wq, w_kv_down, w_k_up, w_v_up, wo):
            q = split_heads(x @ wq, H)
            latent = x @ w_kv_down
            k = split_heads(latent @ w_k_up, KVH)
            v = split_heads(latent @ w_v_up, KVH)
            q, k = (rope(q, BASE_G), rope(k, BASE_G))
            q, k = (qk_norm(q), qk_norm(k))
            k, v = (repeat_kv(k), repeat_kv(v))
            i = jnp.arange(x.shape[1])
            causal = i[:, None] >= i[None, :]
            return merge_heads(sdpa(q, k, v, causal)) @ wo

        def local_gqa_attn(x, wq, wk, wv, wo):
            q = split_heads(x @ wq, H)
            k = split_heads(x @ wk, KVH)
            v = split_heads(x @ wv, KVH)
            q, k = (rope(q, BASE_L), rope(k, BASE_L))
            q, k = (qk_norm(q), qk_norm(k))
            k, v = (repeat_kv(k), repeat_kv(v))
            i = jnp.arange(x.shape[1])
            diff = i[:, None] - i[None, :]
            mask = (diff >= 0) & (diff < WIN)
            return merge_heads(sdpa(q, k, v, mask)) @ wo
        x = hidden
        x = x + global_latent_attn(rmsnorm(x, norm1_w), g_wq, g_kv_down, g_k_up, g_v_up, g_wo)
        x = x + local_gqa_attn(rmsnorm(x, norm2_w), l_wq, l_wk, l_wv, l_wo)
        return x

    def _L0_xattn_ref(query, key, value, Wq, bq, Wk, bk, Wv, bv, Wo, bo):
        import jax, jax.numpy as jnp
        import numpy as np
        QUERY_DIM = 256
        KEY_DIM = 192
        NUM_HEADS = 16
        HEAD_DIM = QUERY_DIM // NUM_HEADS
        SCALE = HEAD_DIM ** (-0.5)
        B, Nq, _ = query.shape
        Nk = key.shape[1]
        q = (query @ Wq + bq).reshape(B, Nq, NUM_HEADS, HEAD_DIM).transpose(0, 2, 1, 3)
        k = (key @ Wk + bk).reshape(B, Nk, NUM_HEADS, HEAD_DIM).transpose(0, 2, 1, 3)
        v = (value @ Wv + bv).reshape(B, Nk, NUM_HEADS, HEAD_DIM).transpose(0, 2, 1, 3)
        attn = jnp.einsum('bhqd,bhkd->bhqk', q, k) * SCALE
        attn = jax.nn.softmax(attn, axis=-1)
        out = jnp.einsum('bhqk,bhkd->bhqd', attn, v)
        out = out.transpose(0, 2, 1, 3).reshape(B, Nq, QUERY_DIM)
        return out @ Wo + bo

    def _L0_ffn_ref(x, Wqkv, q_scale, k_scale, Wo, ln_g, ln_b, W1, b1, W2, b2):
        import jax, jax.numpy as jnp
        import numpy as np
        DIM = 256
        DEPTH = 6
        HEADS = 16
        DIM_HEAD = 64
        WINDOW = 64
        INNER = HEADS * DIM_HEAD
        DIM_INNER = int(DIM * 4 * 2 / 3)
        QK_SCALE = 8.0

        def shift_tokens(t):
            a, s = jnp.split(t, 2, -1)
            s = jnp.pad(s, ((0, 0), (1, 0), (0, 0)))[:, :-1]
            return jnp.concatenate([a, s], -1)

        def l2norm(t):
            return t / jnp.maximum(jnp.linalg.norm(t, axis=-1, keepdims=True), 1e-12)

        def rotate_half(x):
            x1, x2 = jnp.split(x, 2, -1)
            return jnp.concatenate([-x2, x1], -1)

        def rotary_tables(n):
            half = jnp.arange(0, DIM_HEAD, 2, dtype=jnp.float32)
            inv_freq = 1.0 / 10000.0 ** (half / DIM_HEAD)
            t = jnp.arange(n, dtype=jnp.float32)
            freqs = t[:, None] * inv_freq[None, :]
            freqs = jnp.concatenate([freqs, freqs], -1)
            base_scale = (half + 0.4 * DIM_HEAD) / (1.4 * DIM_HEAD)
            power = (t - n // 2) / (WINDOW // 2)
            scale = base_scale[None, :] ** power[:, None]
            scale = jnp.concatenate([scale, scale], -1)
            return (freqs, scale)

        def local_attention(q, k, v):
            b, h, n, d = q.shape
            w = WINDOW
            nw = n // w
            bq = q.reshape(b, h, nw, w, d)
            bk = k.reshape(b, h, nw, w, d)
            bv = v.reshape(b, h, nw, w, d)

            def look(t):
                p = jnp.pad(t, ((0, 0), (0, 0), (1, 0), (0, 0), (0, 0)))
                return jnp.concatenate([p[:, :, :nw], p[:, :, 1:]], axis=3)
            bk2, bv2 = (look(bk), look(bv))
            seq = jnp.arange(n).reshape(nw, w)
            seq_p = jnp.pad(seq, ((1, 0), (0, 0)), constant_values=-1)
            jt = jnp.concatenate([seq_p[:nw], seq_p[1:]], axis=1)
            it = seq[:, :, None]
            jb = jt[:, None, :]
            mask = (it < jb) | (it > jb + w) | (jb == -1)
            sim = jnp.einsum('bhwie,bhwje->bhwij', bq, bk2) * QK_SCALE
            sim = jnp.where(mask, -jnp.finfo(sim.dtype).max, sim)
            attn = jax.nn.softmax(sim, -1)
            out = jnp.einsum('bhwij,bhwje->bhwie', attn, bv2)
            return out.reshape(b, h, n, d)

        def attn_layer(x, Wqkv, qs, ksc, Wo):
            b, n, _ = x.shape
            qkv = x @ Wqkv
            q, k, v = jnp.split(qkv, 3, -1)
            sh = lambda t: t.reshape(b, n, HEADS, DIM_HEAD).transpose(0, 2, 1, 3)
            q, k, v = (sh(q), sh(k), sh(v))
            q = l2norm(q) * qs
            k = l2norm(k) * ksc
            freqs, scale = rotary_tables(n)
            cos, sin = (jnp.cos(freqs), jnp.sin(freqs))
            q = q * cos * scale + rotate_half(q) * sin * scale
            inv = 1.0 / scale
            k = k * cos * inv + rotate_half(k) * sin * inv
            out = local_attention(q, k, v)
            out = out.transpose(0, 2, 1, 3).reshape(b, n, INNER)
            return out @ Wo

        def ffn_layer(x, g, bln, W1, b1, W2, b2):
            mu = x.mean(-1, keepdims=True)
            var = ((x - mu) ** 2).mean(-1, keepdims=True)
            xn = (x - mu) / jnp.sqrt(var + 1e-05) * g + bln
            hg = xn @ W1 + b1
            a, gate = jnp.split(hg, 2, -1)
            return a * jax.nn.gelu(gate, approximate=False) @ W2 + b2
        for i in range(DEPTH):
            x = attn_layer(shift_tokens(x), Wqkv[i], q_scale[i], k_scale[i], Wo[i]) + x
            x = ffn_layer(shift_tokens(x), ln_g[i], ln_b[i], W1[i], b1[i], W2[i], b2[i]) + x
        return x

    def _L1_attn_ref(x, Wq, Wk, Wv, Wo, bo, proj):
        import jax, jax.numpy as jnp
        import numpy as np
        import math
        EPS = 1e-06
        H = 16

        def favorplus_features(x, proj, eps=EPS):
            xw = jnp.einsum('bhtd,hmd->bhtm', x, proj)
            xw = xw - jnp.max(xw, axis=-1, keepdims=True)
            exp_part = jnp.exp(xw)
            x_norm_sq = jnp.sum(x * x, axis=-1, keepdims=True)
            base = jnp.exp(-0.5 * x_norm_sq)
            return exp_part * base + eps
        B, T, d = x.shape
        h = H
        dk = d // h
        m = proj.shape[1]

        def heads(W):
            return (x @ W.T).reshape(B, T, h, dk).transpose(0, 2, 1, 3)
        Q, K, V = (heads(Wq), heads(Wk), heads(Wv))
        scale = 1.0 / math.sqrt(dk)
        phiQ = favorplus_features(Q * scale, proj) / math.sqrt(m)
        phiK = favorplus_features(K * scale, proj) / math.sqrt(m)
        KV = jnp.einsum('bhtm,bhtd->bhmd', phiK, V)
        Ksum = jnp.sum(phiK, axis=2)
        num = jnp.einsum('bhtm,bhmd->bhtd', phiQ, KV)
        den = jnp.einsum('bhtm,bhm->bht', phiQ, Ksum)[..., None] + EPS
        out_heads = num / den
        merged = out_heads.transpose(0, 2, 1, 3).reshape(B, T, h * dk)
        return merged @ Wo.T + bo

    def _L1_xattn_ref(x, context, Wq, Wk, Wv, Wo, bo):
        import jax, jax.numpy as jnp
        import numpy as np
        HEADS = 16
        DIM_HEAD = 64
        b, n, _ = x.shape
        h, d = (HEADS, DIM_HEAD)
        scale = d ** (-0.5)
        q = (x @ Wq).reshape(b, n, h, d).transpose(0, 2, 1, 3)
        k = (context @ Wk).reshape(b, -1, h, d).transpose(0, 2, 1, 3)
        v = (context @ Wv).reshape(b, -1, h, d).transpose(0, 2, 1, 3)
        sim = jnp.einsum('bhid,bhjd->bhij', q, k) * scale
        attn = jax.nn.softmax(sim, axis=-1)
        out = jnp.einsum('bhij,bhjd->bhid', attn, v)
        out = out.transpose(0, 2, 1, 3).reshape(b, n, h * d)
        return out @ Wo + bo

    def _L1_ffn_ref(x, w_gate, w_up, w_down):
        import jax, jax.numpy as jnp
        import numpy as np
        BLOCK = 32
        W_BITS = 4
        ACT_BITS = 16

        def act_qdq(x):
            qmax = 2.0 ** (ACT_BITS - 1) - 1.0
            scale = jnp.maximum(jnp.max(jnp.abs(x)) / qmax, 1e-12)
            return jnp.clip(jnp.round(x / scale), -qmax - 1.0, qmax) * scale

        def fixed_qdq_u16(x):
            scale = 1.0 / 65536.0
            return jnp.clip(jnp.round(x / scale), 0.0, 65535.0) * scale

        def lpbq_dequant(w):
            O, I = w.shape
            qmax = 2.0 ** (W_BITS - 1) - 1.0
            wb = w.reshape(O, I // BLOCK, BLOCK)
            s = jnp.maximum(jnp.max(jnp.abs(wb), axis=-1, keepdims=True) / qmax, 1e-12)
            wq = jnp.clip(jnp.round(wb / s), -qmax - 1.0, qmax) * s
            return wq.reshape(O, I)
        x = act_qdq(x)
        up = act_qdq(x @ lpbq_dequant(w_up).T)
        gate = act_qdq(x @ lpbq_dequant(w_gate).T)
        sig = fixed_qdq_u16(jax.nn.sigmoid(gate))
        gate = act_qdq(gate * sig)
        o = act_qdq(gate * up)
        return o @ lpbq_dequant(w_down).T

    def _L2_attn_ref(resid, W_Q, W_K, W_V, W_O, b_Q, b_K, b_V, virtual_k, virtual_v):
        import jax, jax.numpy as jnp
        import numpy as np
        D_MODEL = 256
        N_QK = 32
        D_QK = 32
        N_OV = 512
        D_OV = 1
        SEQ = 256
        BATCH = 2
        VKV = 16
        ROT_DIM = 32
        ROT_BASE = 10000.0
        SCALE = D_QK ** 0.5

        def _kaiming(k, shape, fan_in):
            return jax.random.normal(k, shape, jnp.float32) * np.sqrt(2.0 / fan_in)

        def _rotary_sin_cos(n_ctx, rd, base):
            pos = jnp.arange(n_ctx, dtype=jnp.float32)
            dim = jnp.arange(rd // 2, dtype=jnp.float32)
            freq = base ** (dim / (rd / 2))
            freq = jnp.concatenate([freq, freq])
            angles = pos[:, None] / freq[None, :]
            return (jnp.sin(angles), jnp.cos(angles))

        def _apply_rotary(x, sin, cos, rd):
            s = x.shape[1]
            x_rot, x_pass = (x[..., :rd], x[..., rd:])
            flip = jnp.concatenate([-x_rot[..., rd // 2:], x_rot[..., :rd // 2]], axis=-1)
            rot = x_rot * cos[None, :s, None, :] + flip * sin[None, :s, None, :]
            return jnp.concatenate([rot, x_pass], axis=-1)
        b, s, _ = resid.shape
        q = jnp.einsum('bsm,hmd->bshd', resid, W_Q) + b_Q
        k = jnp.einsum('bsm,hmd->bshd', resid, W_K) + b_K
        v = jnp.einsum('bsm,hmd->bshd', resid, W_V) + b_V
        sin, cos = _rotary_sin_cos(s, ROT_DIM, ROT_BASE)
        q = _apply_rotary(q, sin, cos, ROT_DIM)
        k = _apply_rotary(k, sin, cos, ROT_DIM)
        k = jnp.concatenate([k, jnp.broadcast_to(virtual_k[None], (b,) + virtual_k.shape)], axis=1)
        v = jnp.concatenate([v, jnp.broadcast_to(virtual_v[None], (b,) + virtual_v.shape)], axis=1)
        kv_len = s + VKV
        scores = jnp.einsum('bqhd,bkhd->bhqk', q, k) / SCALE
        mask = jnp.arange(kv_len)[None, :] <= jnp.arange(s)[:, None] + VKV
        scores = jnp.where(mask[None, None], scores, -jnp.inf)
        pattern = jax.nn.softmax(scores, axis=-1)
        pattern = jnp.where(jnp.isnan(pattern), 0.0, pattern)
        ratio = N_OV // N_QK
        v_g = v.reshape(b, kv_len, N_QK, ratio * D_OV)
        z = jnp.einsum('bhqk,bkhr->bqhr', pattern, v_g)
        z = z.reshape(b, s, N_OV, D_OV)
        out = jnp.einsum('bqhd,hdm->bqm', z, W_O)
        return out

    def _L2_xattn_ref(x, latents, mask, ln_x_g, ln_x_b, ln_l_g, ln_l_b, qn_g, kn_g, Wq, Wkv, Wlkv, Wo, bo):
        import jax, jax.numpy as jnp
        import numpy as np
        DIM_IN, DIM_LAT, DIM_HEAD = (192, 256, 64)
        INNER = max(DIM_LAT, DIM_IN)
        HEADS = INNER // DIM_HEAD
        SCALE = DIM_HEAD ** (-0.5)
        RMS_EPS = 1e-08
        LN_EPS = 1e-05

        def layernorm(x, g, b):
            mu = jnp.mean(x, axis=-1, keepdims=True)
            var = jnp.mean((x - mu) ** 2, axis=-1, keepdims=True)
            return (x - mu) * jax.lax.rsqrt(var + LN_EPS) * g + b

        def rmsnorm(x, gamma):
            norm = jnp.sqrt(jnp.sum(x * x, axis=-1, keepdims=True)) * x.shape[-1] ** (-0.5)
            return x / jnp.maximum(norm, RMS_EPS) * gamma
        b, n, _ = x.shape
        m = latents.shape[1]
        xn = layernorm(x, ln_x_g, ln_x_b)
        ln = layernorm(latents, ln_l_g, ln_l_b)
        q = ln @ Wq.T
        kv = jnp.concatenate([xn @ Wkv.T, ln @ Wlkv.T], axis=1)
        k, v = (kv[..., :INNER], kv[..., INNER:])
        split_heads = lambda t: t.reshape(t.shape[0], t.shape[1], HEADS, DIM_HEAD).transpose(0, 2, 1, 3)
        q, k, v = (split_heads(q), split_heads(k), split_heads(v))
        qn = rmsnorm(q, qn_g) * SCALE
        kn = rmsnorm(k, kn_g)
        attn = jnp.einsum('bhid,bhjd->bhij', qn, kn)
        full_mask = jnp.pad(mask, ((0, 0), (0, m)), constant_values=True)
        attn = jnp.where(full_mask[:, None, None, :], attn, -jnp.finfo(attn.dtype).max)
        attn = jax.nn.softmax(attn, axis=-1)
        out = jnp.einsum('bhij,bhjd->bhid', attn, v)
        out = out.transpose(0, 2, 1, 3).reshape(b, m, INNER)
        return out @ Wo.T + bo

    def _L2_ffn_ref(x, router_w, correction_bias, gate_w, up_w, down_w, shared_gate_w, shared_up_w, shared_down_w):
        import jax, jax.numpy as jnp
        import numpy as np
        E = 16
        G = 4
        EPG = E // G
        K = 4
        TOPK_GROUP = 2
        PER_GROUP_K = K // TOPK_GROUP

        def _route(xf, router_w, correction_bias):
            S = xf.shape[0]
            logits = xf @ router_w.T
            scores = jax.nn.sigmoid(logits)
            sb = scores + correction_bias
            grp_top = jax.lax.top_k(sb.reshape(S, G, EPG), PER_GROUP_K)[0]
            group_scores = grp_top.sum(axis=-1)
            _, group_idx = jax.lax.top_k(group_scores, TOPK_GROUP)
            group_mask = jnp.zeros((S, G), sb.dtype).at[jnp.arange(S)[:, None], group_idx].set(1.0)
            score_mask = jnp.broadcast_to(group_mask[:, :, None], (S, G, EPG)).reshape(S, E)
            masked = jnp.where(score_mask > 0, sb, -jnp.inf)
            _, topk_idx = jax.lax.top_k(masked, K)
            w = jnp.take_along_axis(scores, topk_idx, axis=1)
            w = w / (w.sum(axis=-1, keepdims=True) + 1e-20)
            return (topk_idx, w, scores)
        B, T, C = x.shape
        S = B * T
        xf = x.reshape(S, C)
        sg = xf @ shared_gate_w.T
        su = xf @ shared_up_w.T
        shared_out = jax.nn.silu(sg) * su @ shared_down_w.T
        topk_idx, w, _scores = _route(xf, router_w, correction_bias)
        combine = jnp.zeros((S, E), xf.dtype).at[jnp.arange(S)[:, None], topk_idx].add(w)
        g = jnp.einsum('sc,ech->esh', xf, gate_w)
        u = jnp.einsum('sc,ech->esh', xf, up_w)
        h = jax.nn.silu(g) * u
        hw = h * combine.T[:, :, None]
        routed = jnp.einsum('esh,ehc->sc', hw, down_w)
        return (shared_out + routed).reshape(B, T, C)

    def _L3_attn_ref(x, Wqkv, Wout):
        import jax, jax.numpy as jnp
        import numpy as np
        B, T, D, H = (4, 512, 256, 16)
        HEAD_DIM = D // H
        LOCAL_WINDOW = 128

        def _rotate_half(t):
            t1, t2 = jnp.split(t, 2, axis=-1)
            return jnp.concatenate([-t2, t1], axis=-1)

        def _apply_rope(q, k):
            Tq, d = (q.shape[2], q.shape[3])
            half = d // 2
            theta = 1.0 / 10000.0 ** (jnp.arange(half, dtype=jnp.float32) / half)
            pos = jnp.arange(Tq, dtype=jnp.float32)
            freqs = pos[:, None] * theta[None, :]
            freqs = jnp.concatenate([freqs, freqs], axis=-1)
            cos = jnp.cos(freqs)[None, None]
            sin = jnp.sin(freqs)[None, None]
            q = q * cos + _rotate_half(q) * sin
            k = k * cos + _rotate_half(k) * sin
            return (q, k)
        Bx, Tx, C = x.shape
        h, d, w = (H, HEAD_DIM, LOCAL_WINDOW)
        qkv = x @ Wqkv
        q, k, v = jnp.split(qkv, 3, axis=-1)
        q = q.reshape(Bx, Tx, h, d).transpose(0, 2, 1, 3)
        k = k.reshape(Bx, Tx, h, d).transpose(0, 2, 1, 3)
        v = v.reshape(Bx, Tx, h, d).transpose(0, 2, 1, 3)
        q, k = _apply_rope(q, k)
        idx = jnp.arange(Tx)
        dist = idx[None, :] - idx[:, None]
        allowed = (dist <= 0) & (dist >= -(w - 1))
        scores = jnp.einsum('bhqd,bhkd->bhqk', q, k) / jnp.sqrt(jnp.float32(d))
        scores = jnp.where(allowed[None, None], scores, -jnp.inf)
        weights = jax.nn.softmax(scores, axis=-1)
        out = jnp.einsum('bhqk,bhkd->bhqd', weights, v)
        out = out.transpose(0, 2, 1, 3).reshape(Bx, Tx, C)
        return out @ Wout

    def _L3_xattn_ref(query, key_value, Wq, bq, Wk, bk, Wv, bv, Wo, bo):
        import jax, jax.numpy as jnp
        import numpy as np
        NUM_HEADS = 16
        CLAMP = 10000.0
        B, Nq, Cq = query.shape
        Nkv = key_value.shape[1]
        H = NUM_HEADS
        D = Cq // H
        scale = D ** (-0.5)
        q = (query @ Wq + bq).reshape(B, Nq, H, D).transpose(0, 2, 1, 3)
        k = (key_value @ Wk + bk).reshape(B, Nkv, H, D).transpose(0, 2, 1, 3)
        v = (key_value @ Wv + bv).reshape(B, Nkv, H, D).transpose(0, 2, 1, 3)
        attn = jnp.einsum('bhqd,bhkd->bhqk', q, k) * scale
        attn = jnp.clip(attn, -CLAMP, CLAMP)
        attn = jax.nn.softmax(attn, axis=-1)
        attn = jnp.where(jnp.any(jnp.isnan(attn)), jnp.asarray(1.0 / Nkv, attn.dtype), attn)
        x = jnp.einsum('bhqk,bhkd->bqhd', attn, v).reshape(B, Nq, Cq)
        return x @ Wo + bo

    def _L3_ffn_ref(hidden_states, classifier_weight, e_score_correction_bias, gate_up_proj, down_proj):
        import jax, jax.numpy as jnp
        import numpy as np
        B, S, H = (2, 512, 256)
        I = 128
        E_R, E_Z = (32, 8)
        E_T = E_R + E_Z
        K = 6
        SCALE = 2.5
        W_INIT = 0.02
        orig_shape = hidden_states.shape
        x = hidden_states.reshape(-1, H).astype(jnp.float32)
        T = x.shape[0]
        logits = x @ classifier_weight.T
        scores = jax.nn.softmax(logits, axis=-1)
        _, topk_idx = jax.lax.top_k(scores + e_score_correction_bias[None, :], K)
        topk_w = jnp.take_along_axis(scores, topk_idx, axis=1) * SCALE
        w_full = jnp.zeros((T, E_T), jnp.float32).at[jnp.arange(T)[:, None], topk_idx].add(topk_w)
        zero_w = w_full[:, E_R:].sum(axis=-1, keepdims=True)
        out0 = x * zero_w
        routed_w = w_full[:, :E_R].T

        def body(out, xs):
            Wgu, Wd, we = xs
            gate, up = jnp.split(x @ Wgu.T, 2, axis=-1)
            y = jax.nn.silu(gate) * up @ Wd.T
            return (out + we[:, None] * y, None)
        out, _ = jax.lax.scan(body, out0, (gate_up_proj[:E_R], down_proj, routed_w))
        return out.reshape(orig_shape).astype(hidden_states.dtype)
    x = _layernorm(x + _L0_attn_ref(x, L0_attn_norm1_w, L0_attn_norm2_w, L0_attn_g_wq, L0_attn_g_kv_down, L0_attn_g_k_up, L0_attn_g_v_up, L0_attn_g_wo, L0_attn_l_wq, L0_attn_l_wk, L0_attn_l_wv, L0_attn_l_wo), axis=-1)
    x = _layernorm(x + _L0_xattn_ref(x, ctx_768, ctx_768, L0_xattn_Wq, L0_xattn_bq, L0_xattn_Wk, L0_xattn_bk, L0_xattn_Wv, L0_xattn_bv, L0_xattn_Wo, L0_xattn_bo), axis=-1)
    x = _layernorm(x + _L0_ffn_ref(x, L0_ffn_Wqkv, L0_ffn_q_scale, L0_ffn_k_scale, L0_ffn_Wo, L0_ffn_ln_g, L0_ffn_ln_b, L0_ffn_W1, L0_ffn_b1, L0_ffn_W2, L0_ffn_b2), axis=-1)
    x = _layernorm(x + _L1_attn_ref(x, L1_attn_Wq, L1_attn_Wk, L1_attn_Wv, L1_attn_Wo, L1_attn_bo, L1_attn_proj), axis=-1)
    x = _layernorm(x + _L1_xattn_ref(x, ctx_768, L1_xattn_Wq, L1_xattn_Wk, L1_xattn_Wv, L1_xattn_Wo, L1_xattn_bo), axis=-1)
    x = _layernorm(x + _L1_ffn_ref(x, L1_ffn_w_gate, L1_ffn_w_up, L1_ffn_w_down), axis=-1)
    x = _layernorm(x + _L2_attn_ref(x, L2_attn_W_Q, L2_attn_W_K, L2_attn_W_V, L2_attn_W_O, L2_attn_b_Q, L2_attn_b_K, L2_attn_b_V, L2_attn_virtual_k, L2_attn_virtual_v), axis=-1)
    x = _layernorm(x + _L2_xattn_ref(ctx_768, x, mask_BxS2_bk0, L2_xattn_ln_x_g, L2_xattn_ln_x_b, L2_xattn_ln_l_g, L2_xattn_ln_l_b, L2_xattn_qn_g, L2_xattn_kn_g, L2_xattn_Wq, L2_xattn_Wkv, L2_xattn_Wlkv, L2_xattn_Wo, L2_xattn_bo), axis=-1)
    x = _layernorm(x + _L2_ffn_ref(x, L2_ffn_router_w, L2_ffn_correction_bias, L2_ffn_gate_w, L2_ffn_up_w, L2_ffn_down_w, L2_ffn_shared_gate_w, L2_ffn_shared_up_w, L2_ffn_shared_down_w), axis=-1)
    x = _layernorm(x + _L3_attn_ref(x, L3_attn_Wqkv, L3_attn_Wout), axis=-1)
    x = _layernorm(x + _L3_xattn_ref(x, ctx_768, L3_xattn_Wq, L3_xattn_bq, L3_xattn_Wk, L3_xattn_bk, L3_xattn_Wv, L3_xattn_bv, L3_xattn_Wo, L3_xattn_bo), axis=-1)
    x = _layernorm(x + _L3_ffn_ref(x, L3_ffn_classifier_weight, L3_ffn_e_score_correction_bias, L3_ffn_gate_up_proj, L3_ffn_down_proj), axis=-1)
    return x

_drawn_inputs = setup_inputs


def setup_inputs(seed=0):
    import zlib

    import numpy as np

    out = dict(_drawn_inputs(seed))
    spreads = {'L0_attn_norm1_w': (1.0, 0.6),
     'L0_attn_norm2_w': (1.0, 0.6),
     'L0_xattn_bq': (0.0, 0.337),
     'L0_xattn_bk': (0.0, 2.0),
     'L0_xattn_bv': (0.0, 0.1),
     'L0_xattn_bo': (0.0, 0.1),
     'L0_ffn_q_scale': (1.0, 0.6),
     'L0_ffn_k_scale': (1.0, 0.6),
     'L0_ffn_ln_g': (1.0, 0.6),
     'L0_ffn_ln_b': (0.0, 0.8),
     'L0_ffn_b1': (0.0, 0.579),
     'L0_ffn_b2': (0.0, 0.1),
     'L1_attn_bo': (0.0, 0.1),
     'L2_attn_b_Q': (0.0, 0.8),
     'L2_attn_b_K': (0.0, 0.8),
     'L2_attn_b_V': (0.0, 0.1),
     'L2_attn_virtual_v': (0.0, 2.0),
     'L2_xattn_ln_x_g': (1.0, 0.566),
     'L2_xattn_ln_x_b': (0.0, 0.31),
     'L2_xattn_ln_l_g': (1.0, 0.2),
     'L2_xattn_ln_l_b': (0.0, 0.1),
     'L2_xattn_qn_g': (1.0, 0.549),
     'L2_xattn_kn_g': (1.0, 0.2),
     'L2_xattn_bo': (0.0, 0.1),
     'L2_ffn_correction_bias': (0.0, 0.8),
     'L3_xattn_bq': (0.0, 0.388),
     'L3_xattn_bk': (0.0, 2.0),
     'L3_xattn_bv': (0.0, 0.1),
     'L3_xattn_bo': (0.0, 0.1),
     'L3_ffn_e_score_correction_bias': (0.0, 0.8)}
    factors = {'L0_attn_g_wq': 8.0,
     'L0_attn_g_kv_down': 8.0,
     'L0_attn_g_k_up': 8.0,
     'L0_attn_g_v_up': 8.0,
     'L0_attn_g_wo': 8.0,
     'L0_attn_l_wq': 8.0,
     'L0_attn_l_wk': 8.0,
     'L0_attn_l_wv': 8.0,
     'L0_attn_l_wo': 8.0,
     'L1_attn_Wq': 6.19,
     'L1_attn_proj': 5.228,
     'L1_xattn_bo': 4.56,
     'L2_attn_W_Q': 8.0,
     'L2_attn_W_K': 8.0,
     'L2_attn_virtual_k': 64.0,
     'L2_ffn_router_w': 8.0,
     'L2_ffn_gate_w': 8.0,
     'L2_ffn_up_w': 8.0,
     'L2_ffn_down_w': 8.0,
     'L3_ffn_classifier_weight': 8.0,
     'L3_ffn_gate_up_proj': 8.0,
     'L3_ffn_down_proj': 8.0}
    for name, (base, spread) in spreads.items():
        noise = np.random.default_rng([zlib.crc32(name.encode()), seed]).standard_normal(out[name].shape)
        drawn = base * np.exp(spread * noise) if base else spread * noise
        out[name] = jnp.asarray(drawn.astype(out[name].dtype))
    for name, factor in factors.items():
        out[name] = (out[name] * factor).astype(out[name].dtype)
    return out
```

```python
import concourse.bass as bass
from concourse import mybir
from concourse.alu_op_type import AluOpType as ALU

F32 = mybir.dt.float32
BF16 = mybir.dt.bfloat16
U8 = mybir.dt.uint8
ACT = mybir.ActivationFunctionType
AX = mybir.AxisListType.X

P = 128
B, S, D = 2, 512, 256
SC, DC = 1024, 192
NT = S // P
BANK = 512
BIG = 1.0e30

STAGES = {
    "start": ["inputs_loaded", "constants_set"],
    "norm": ["gains_loaded", "summed", "mean_ready", "centered", "squared", "var_ready", "var_kept",
             "root_ready", "order"],
    "linear": ["weights_loaded", "product_ready", "product_used"],
    "project": ["weights_loaded", "product_ready", "product_kept", "sums_ready", "roots_ready", "order"],
    "turn": ["turned", "kept_by_dve", "kept_by_act"],
    "maxima": ["scores_ready", "max_taken"],
    "attend": ["scores_ready", "probs_ready", "values_ready", "heads_kept", "shift_ready",
               "shift_kept", "clipped", "exp_ready", "order"],
    "gated": ["bias_loaded", "slot0_loaded", "slot1_loaded", "slot2_loaded", "slot3_loaded",
              "gate_ready", "up_ready", "gate_acted", "hidden_ready", "tile_done", "sum_ready",
              "order"],
    "features": ["cleared", "squares_ready", "logits_ready", "shifted_ready", "exp_ready",
                 "phi_ready", "order"],
    "quantize": ["row_max", "all_max", "sigmoid_ready", "order"],
    "route": ["shifted_ready", "scores_ready", "order"],
    "small": ["weights_loaded", "pe_done", "act_done", "dve_done", "pool_done", "order"],
}


class Signals:

    def __init__(self, nc, names, stage):
        self.of = {n: nc.alloc_semaphore(f"{stage}_{n}") for n in names}
        nums = [s.num for s in self.of.values()]
        self.lo, self.hi = min(nums), max(nums) + 1

    def __getitem__(self, name):
        return self.of[name]


class Order:

    def __init__(self, eng, sem):
        self.eng, self.sem, self.n = eng, sem, 0

    def __call__(self, ins):
        self.n += 1
        ins.then_inc(self.sem, 1)
        self.eng.wait_ge(self.sem, self.n)


class Chip:

    def __init__(self, nc):
        self.nc = nc
        self.signals = {k: Signals(nc, v, k) for k, v in STAGES.items()}
        self.lo = min(s.lo for s in self.signals.values())
        self.hi = max(s.hi for s in self.signals.values())
        self.last = None
        self.psum = nc.alloc_psum_tensor("psum", [P, 8, BANK], F32)
        sb = nc.alloc_sbuf_tensor
        self.state = sb("state", [P, 2, B * S], F32)
        self.inner = sb("inner", [P, 2, B * S], F32)
        self.normed = sb("normed", [P, 2, B * S], F32)
        self.ctx = sb("ctx", [P, 2, B * SC], F32)
        self.ident = sb("ident", [P, P], F32)
        self.ident_bf = sb("ident_bf", [P, P], BF16)
        self.mean_w = sb("mean_w", [P, 2, P], F32)
        self.ones = sb("ones", [1, P], F32)
        self.masks = sb("masks", [P, 2 * 256], BF16)
        self.w_in = sb("w_in", [P, 2, 768], F32)
        self.w_bias = sb("w_bias", [1, SC], F32)
        self.w_out = sb("w_out", [P, 8, D], F32)
        self.cols = sb("cols", [P, 64], F32)
        self.roots = sb("roots", [P, 64], F32)
        self.pick_max = sb("pick_max", [P, P], F32)
        self.gains = sb("gains", [P, 160], F32)
        self.mask_cols = sb("mask_cols", [P, B * SC // P], U8)
        self.table_mem = sb("table_mem", [P, 4 * NT * 64], F32)
        self.mask_row = self.table_mem[0:1, 0:B * SC // 4].bitcast(U8)
        self.arena = sb("arena", [P, 36032], F32)

    def carve(self, at, *shape):
        n = 1
        for s in shape:
            n *= s
        assert at + n <= self.arena.shape[1], (at, n)
        v = self.arena[:, at:at + n]
        if len(shape) == 1:
            return v
        if len(shape) == 2:
            return v.rearrange("p (a b) -> p a b", b=shape[1])
        return v.rearrange("p (a b c) -> p a b c", b=shape[1], c=shape[2])

    def tables(self, hd, n=0):
        at = n * 2 * NT * 64
        return [self.table_mem[:, at + i * NT * hd:at + (i + 1) * NT * hd].rearrange(
            "p (t e) -> p t e", e=hd) for i in range(2)]

    def stage(self, kind):
        if self.last == kind:
            with self.nc.Block() as block:
                @block.gpsimd
                def _(pool):
                    pool.sem_clear(range(self.lo, self.hi))
        self.last = kind
        return self.signals[kind]

    def reset_others(self, pool, own):
        if own.lo > self.lo:
            pool.sem_clear(range(self.lo, own.lo))
        if own.hi < self.hi:
            pool.sem_clear(range(own.hi, self.hi))


def start_stage(chip, loads):
    nc, sig = chip.nc, chip.stage("start")
    with nc.Block() as block:
        @block.sync
        def _(sp):
            for dst, src in loads:
                sp.dma_start(dst, src).then_inc(sig["inputs_loaded"], 16)
            sp.wait_ge(sig["inputs_loaded"], 16 * len(loads))

        @block.vector
        def _(dve):
            dve.memset(chip.ones[:, :], 1.0)
            dve.memset(chip.mean_w[:, 0, :], 1.0 / D)
            dve.memset(chip.mean_w[:, 1, :], 1.0 / DC).then_inc(sig["constants_set"], 1)
            dve.wait_ge(sig["constants_set"], 1)


def load_stage(chip, loads):
    nc, sig = chip.nc, chip.stage("start")
    with nc.Block() as block:
        @block.gpsimd
        def _(pool):
            chip.reset_others(pool, sig)

        @block.sync
        def _(sp):
            for dst, src in loads:
                sp.dma_start(dst, src).then_inc(sig["inputs_loaded"], 16)
            sp.wait_ge(sig["inputs_loaded"], 16 * len(loads))


def norm_stage(chip, src, dst, sizes, width, eps, center=True, gain=None, shift=None, add=None,
               loads=()):
    nc, sig = chip.nc, chip.stage("norm")
    halves = width // BANK
    mean_w = chip.mean_w[:, 0 if sum(sizes) == D else 1, :]
    work = chip.carve(0, 2, 2, BANK)
    centred = chip.carve(2048, 2, 2, BANK)
    squares = chip.carve(4096, 2, 2, BANK)
    spread = chip.carve(6144, 2, BANK)
    root = chip.carve(7168, 2, BANK)
    mean_ps, var_ps = chip.psum[:, 0:2, :], chip.psum[:, 2:4, :]
    chunks = list(enumerate(sizes))
    with nc.Block() as block:
        @block.gpsimd
        def _(pool):
            chip.reset_others(pool, sig)

        @block.sync
        def _(sp):
            for to, frm in loads:
                sp.dma_start(to, frm).then_inc(sig["gains_loaded"], 16)

        @block.vector
        def _(dve):
            order = Order(dve, sig["order"])

            def begin(h):
                n, cols = h % 2, slice(h * BANK, (h + 1) * BANK)
                if h >= 2:
                    dve.wait_ge(sig["squared"], h - 1)
                for c, rows in chunks:
                    if add is not None:
                        ins = dve.tensor_tensor(work[:rows, n, c], src[:rows, c, cols],
                                                add[:rows, c, cols], ALU.add)
                    else:
                        ins = dve.tensor_copy(work[:rows, n, c], src[:rows, c, cols])
                    ins.then_inc(sig["summed"], 1)
                if center:
                    dve.wait_ge(sig["mean_ready"], h + 1)
                dve.wait_ge(sig["summed"], 2 * h + 2)
                for c, rows in chunks:
                    if center:
                        ins = dve.tensor_tensor(centred[:rows, n, c], work[:rows, n, c],
                                                mean_ps[:rows, n], ALU.subtract)
                    else:
                        ins = dve.tensor_copy(centred[:rows, n, c], work[:rows, n, c])
                    ins.then_inc(sig["centered"], 1)

            def end(h):
                n = h % 2
                dve.wait_ge(sig["var_ready"], h + 1)
                dve.tensor_scalar(spread[:, n], var_ps[:, n], eps, None,
                                  ALU.add).then_inc(sig["var_kept"], 1)
                dve.wait_ge(sig["root_ready"], h + 1)
                order(dve.reciprocal(spread[:, n], root[:, n]))
                for c, rows in chunks:
                    out = dst[:rows, c, h * BANK:(h + 1) * BANK]
                    order(dve.tensor_tensor(out, centred[:rows, n, c], spread[:rows, n], ALU.mult))
                    if gain is not None and shift is None:
                        order(dve.tensor_scalar(out, out, gain[:rows, c:c + 1], None, ALU.mult))
                    elif gain is not None:
                        order(dve.tensor_scalar(out, out, gain[:rows, c:c + 1],
                                                shift[:rows, c:c + 1], ALU.mult, ALU.add))

            if loads:
                dve.wait_ge(sig["gains_loaded"], 16 * len(loads))
            begin(0)
            for h in range(halves):
                if h + 1 < halves:
                    begin(h + 1)
                end(h)

        @block.scalar
        def _(act):
            for h in range(halves):
                n = h % 2
                act.wait_ge(sig["centered"], 2 * h + 2)
                if h >= 2:
                    act.wait_ge(sig["var_ready"], h - 1)
                for c, rows in chunks:
                    ins = act.activation(squares[:rows, n, c], centred[:rows, n, c], ACT.Square)
                ins.then_inc(sig["squared"], 1)
                act.wait_ge(sig["var_kept"], h + 1)
                act.activation(root[:, n], spread[:, n], ACT.Sqrt).then_inc(sig["root_ready"], 1)

        @block.tensor
        def _(pe):
            def mean(h):
                if not center:
                    return
                n = h % 2
                pe.wait_ge(sig["summed"], 2 * h + 2)
                if h >= 2:
                    pe.wait_ge(sig["centered"], 2 * (h - 1))
                for c, rows in chunks:
                    mm = pe.matmul(mean_ps[:, n], mean_w[:rows, :], work[:rows, n, c],
                                   start=c == 0, stop=c == 1)
                mm.then_inc(sig["mean_ready"], 1)

            mean(0)
            for h in range(halves):
                if h + 1 < halves:
                    mean(h + 1)
                n = h % 2
                pe.wait_ge(sig["squared"], h + 1)
                if h >= 2:
                    pe.wait_ge(sig["var_kept"], h - 1)
                for c, rows in chunks:
                    mm = pe.matmul(var_ps[:, n], mean_w[:rows, :], squares[:rows, n, c],
                                   start=c == 0, stop=c == 1)
                mm.then_inc(sig["var_ready"], 1)


def linear_stage(chip, loads, jobs):
    nc, sig = chip.nc, chip.stage("linear")
    with nc.Block() as block:
        @block.gpsimd
        def _(pool):
            chip.reset_others(pool, sig)

        @block.sync
        def _(sp):
            for dst, src in loads:
                sp.dma_start(dst, src).then_inc(sig["weights_loaded"], 16)

        @block.tensor
        def _(pe):
            if loads:
                pe.wait_ge(sig["weights_loaded"], 16 * len(loads))
            for j, (out, pairs, bias, addend) in enumerate(jobs):
                if j >= 8:
                    pe.wait_ge(sig["product_used"], j - 7)
                rows, cols = out.shape
                for i, (lhs, rhs) in enumerate(pairs):
                    mm = pe.matmul(chip.psum[:rows, j % 8, :cols], lhs, rhs, start=i == 0,
                                   stop=i == len(pairs) - 1)
                mm.then_inc(sig["product_ready"], 1)

        @block.vector
        def _(dve):
            if loads:
                dve.wait_ge(sig["weights_loaded"], 16 * len(loads))
            for j, (out, pairs, bias, addend) in enumerate(jobs):
                rows, cols = out.shape
                made = chip.psum[:rows, j % 8, :cols]
                dve.wait_ge(sig["product_ready"], j + 1)
                if addend is not None and bias is not None:
                    ins = dve.scalar_tensor_tensor(out, made, bias, addend, ALU.add, ALU.add)
                elif addend is not None:
                    ins = dve.tensor_tensor(out, made, addend, ALU.add)
                elif bias is not None:
                    ins = dve.tensor_scalar(out, made, bias, None, ALU.add)
                else:
                    ins = dve.tensor_copy(out, made)
                ins.then_inc(sig["product_used"], 1)


def turn_stage(chip, groups):
    nc, sig = chip.nc, chip.stage("turn")

    def kept(eng, g):
        eng.wait_ge(sig["kept_by_act" if g % 2 else "kept_by_dve"], g // 2 + 1)

    with nc.Block() as block:
        @block.gpsimd
        def _(pool):
            chip.reset_others(pool, sig)

        @block.tensor
        def _(pe):
            for g, (parts, dst) in enumerate(groups):
                if g >= 8:
                    kept(pe, g - 8)
                for src, at in parts:
                    rows, cols = src.shape
                    mm = pe.transpose(chip.psum[:cols, g % 8, at:at + rows], src,
                                      chip.ident[:rows, :rows])
                mm.then_inc(sig["turned"], 1)

        @block.vector
        def _(dve):
            for g, (parts, dst) in enumerate(groups):
                if g % 2 == 0:
                    dve.wait_ge(sig["turned"], g + 1)
                    dve.tensor_copy(dst, chip.psum[:dst.shape[0], g % 8, :dst.shape[1]]
                                    ).then_inc(sig["kept_by_dve"], 1)

        @block.scalar
        def _(act):
            for g, (parts, dst) in enumerate(groups):
                if g % 2 == 1:
                    act.wait_ge(sig["turned"], g + 1)
                    act.copy(dst, chip.psum[:dst.shape[0], g % 8, :dst.shape[1]]
                             ).then_inc(sig["kept_by_act"], 1)


class Attention:

    def __init__(self, chip, hd, vd, key_tiles, scale, mask=None, last_keys=P):
        self.hd, self.vd, self.scale, self.mask = hd, vd, scale, mask
        self.heads = D // hd
        self.slot = {16: 32, 32: 64, 64: 128}[hd]
        self.per = P // self.slot
        self.key_tiles, self.last_keys = key_tiles, last_keys
        self.keys = (key_tiles - 1) * P + last_keys
        self.q = chip.carve(0, NT, 4, P)
        self.k = chip.carve(2048, 12, 4, P)
        self.v = chip.carve(8192, 12, 272)[:, :, :self.heads * (vd + 1)].rearrange(
            "p t (h e) -> p t h e", e=vd + 1)
        self.qT = chip.carve(11456, 4, BANK)
        self.kT = chip.carve(13504, 4, 12 * P)
        self.raw_q = chip.carve(19648, NT * D)
        self.raw_k = chip.carve(20672, NT * D)
        self.tmp = chip.carve(21696, NT * D)
        self.tmp2 = chip.carve(22720, NT * D)
        self.out = chip.carve(23744, NT, 1024)
        self.tmp_rows = chip.carve(19648, 2, BANK)
        self.clip_rows = chip.carve(20672, 4, BANK)
        self.nbuf = 2 if key_tiles <= 8 else 1
        self.probs = [chip.carve(27840 + 4096 * i, 8, BANK) for i in range(2)] \
            if self.nbuf == 2 else [chip.carve(27840, key_tiles, BANK)]

    def carve_outT(self, chip):
        return chip.carve(27840, 8, BANK)

    def slots(self, t, tiles):
        return t[:, :tiles].rearrange("p t b (h w) -> p (t b h) w", w=self.slot)

    def rows(self, h, n):
        at = (h % self.per) * self.slot
        return slice(at, at + n)

    def width(self, kt):
        return self.last_keys if kt == self.key_tiles - 1 else P

    def keys_of(self, qt):
        if self.mask == "causal":
            return 0, qt + 1
        if self.mask == "band":
            return max(qt - 1, 0), qt + 1
        if self.mask == "ahead":
            return 0, qt + 2
        return 0, self.key_tiles

    def masks_of(self, qt, lo, hi):
        if self.mask == "causal":
            found = [(0, P, qt * P)]
        elif self.mask == "band":
            found = [(0, P, (qt - 1) * P)] * (qt > 0) + [(P, 2 * P, qt * P)]
        else:
            found = [(0, P, qt * P), (P, P + self.width(qt + 1), (qt + 1) * P)]
        return [m for m in found if lo <= m[2] < hi]

    def masks_of_keys(self, kt):
        if self.mask == "causal":
            return [(0, P, 0)]
        if self.mask == "band":
            return [(0, P, 0)] + [(P, 2 * P, P)] * (kt + 1 < NT)
        if kt == 0:
            return [(P, 2 * P, 0)]
        return [(0, P, 0)] + [(P, 2 * P, P)] * (kt < NT)

    def queries_of(self, kt):
        seen = [qt for qt in range(NT) if self.keys_of(qt)[0] <= kt < self.keys_of(qt)[1]]
        return seen[0], seen[-1] + 1


def fill_slots_stage(chip, at):
    nc, sig = chip.nc, chip.stage("small")
    with nc.Block() as block:
        @block.gpsimd
        def _(pool):
            chip.reset_others(pool, sig)
            pool.memset(at.v, 1.0).then_inc(sig["pool_done"], 1)

        @block.vector
        def _(dve):
            order = Order(dve, sig["order"])
            dve.memset(at.q, 0.0).then_inc(sig["dve_done"], 1)
            order(dve.memset(at.k, 0.0))
            order(dve.memset(at.slots(at.k, 12)[:, :, at.hd:at.hd + 1], 1.0))


def project_stage(chip, at, loads, jobs, q_post=None, k_post=None):
    nc, sig = chip.nc, chip.stage("project")
    posts = [p for p in (q_post, k_post) if p is not None]
    with nc.Block() as block:
        @block.gpsimd
        def _(pool):
            chip.reset_others(pool, sig)

        @block.sync
        def _(sp):
            for dst, src in loads:
                sp.dma_start(dst, src).then_inc(sig["weights_loaded"], 16)

        @block.tensor
        def _(pe):
            if loads:
                pe.wait_ge(sig["weights_loaded"], 16 * len(loads))
            for j, (products, copies) in enumerate(jobs):
                if j >= 4:
                    pe.wait_ge(sig["product_kept"], j - 3)
                two = chip.psum[:, 2 * (j % 4):2 * (j % 4) + 2, :].rearrange("p a b -> p (a b)")
                for lhs, rhs, first, start, stop in products:
                    mm = pe.matmul(two[:lhs.shape[1], first:first + rhs.shape[1]], lhs, rhs,
                                   start=start, stop=stop)
                mm.then_inc(sig["product_ready"], 1)

        @block.scalar
        def _(act):
            for j, (products, copies) in enumerate(jobs):
                act.wait_ge(sig["product_ready"], j + 1)
                two = chip.psum[:, 2 * (j % 4):2 * (j % 4) + 2, :].rearrange("p a b -> p (a b)")
                for dst, src in copies:
                    ins = act.copy(dst, src(two))
                ins.then_inc(sig["product_kept"], 1)
            n = 0
            for post in posts:
                if post.norm:
                    n += 1
                    act.wait_ge(sig["sums_ready"], n)
                    act.activation(post.root, post.sums, ACT.Sqrt).then_inc(sig["roots_ready"], 1)

        @block.vector
        def _(dve):
            if not posts:
                return
            order = Order(dve, sig["order"])
            if loads:
                dve.wait_ge(sig["weights_loaded"], 16 * len(loads))
            dve.wait_ge(sig["product_kept"], len(jobs))
            n = 0
            for post in posts:
                t, tmp = post.raw, post.tmp
                if post.norm:
                    mult, eps, floor, scale = post.norm
                    order(dve.tensor_tensor(tmp, t, t, ALU.mult))
                    order(dve.tensor_reduce(post.sums, tmp, AX, ALU.add))
                    dve.tensor_scalar(post.sums, post.sums, mult, eps, ALU.mult,
                                      ALU.add).then_inc(sig["sums_ready"], 1)
                    n += 1
                    dve.wait_ge(sig["roots_ready"], n)
                    order(dve.tensor_scalar(post.root, post.root, floor, 1.0 / scale, ALU.max,
                                            ALU.mult))
                    order(dve.reciprocal(post.root, post.root))
                    last = post.gain is None and post.cos is None
                    order(dve.tensor_tensor(post.dst if last else t, t,
                                            post.root.to_broadcast(t.shape), ALU.mult))
                    if last:
                        continue
                if post.gain is not None:
                    out = post.dst if post.cos is None else t
                    order(dve.tensor_tensor(out, t, post.gain.unsqueeze(1).to_broadcast(t.shape), ALU.mult))
                    if post.cos is None:
                        continue
                order(dve.tensor_tensor(post.by_tile(tmp), post.by_tile(t), post.table(post.cos),
                                        ALU.mult))
                for dst_part, src_part in post.partners:
                    ins = dve.tensor_tensor(post.by_tile(post.tmp2)[:, :, :, dst_part],
                                            post.by_tile(t)[:, :, :, src_part],
                                            post.table(post.sin)[:, :, :, dst_part], ALU.mult)
                    order(ins)
                if post.copies == 1:
                    order(dve.tensor_tensor(post.dst, tmp, post.tmp2, ALU.add))
                else:
                    order(dve.tensor_tensor(tmp, tmp, post.tmp2, ALU.add))
                    for r in range(post.copies):
                        order(dve.tensor_copy(post.dst_copy(r), tmp))


class HeadPost:

    def __init__(self, chip, at, raw, slots, tiles, heads, norm=None, gain=None, cos=None,
                 sin=None, pairs=False, copies=1):
        hd = at.hd
        n = tiles * heads
        self.tiles, self.heads, self.hd, self.copies = tiles, heads, hd, copies
        self.raw = raw[:, :n * hd].rearrange("p (n e) -> p n e", e=hd)
        self.tmp = at.tmp[:, :n * hd].rearrange("p (n e) -> p n e", e=hd)
        self.tmp2 = at.tmp2[:, :n * hd].rearrange("p (n e) -> p n e", e=hd)
        self.sums = chip.cols[:, 0:n]
        self.root = chip.roots[:, 0:n]
        self.norm, self.cos, self.sin = norm, cos, sin
        self.gain = gain
        self.slots = at.slots(slots, tiles)[:, :, :hd]
        self.dst = self.slots if copies == 1 else None
        if pairs:
            self.partners = [(slice(0, hd, 2), slice(1, hd, 2)), (slice(1, hd, 2), slice(0, hd, 2))]
        else:
            self.partners = [(slice(0, hd // 2), slice(hd // 2, hd)),
                             (slice(hd // 2, hd), slice(0, hd // 2))]

    def by_tile(self, t):
        return t.rearrange("p (t h) e -> p t h e", h=self.heads)

    def table(self, t):
        return t.unsqueeze(2).to_broadcast([P, self.tiles, self.heads, self.hd])

    def dst_copy(self, r):
        return self.slots.rearrange("p (n r) e -> p n r e", r=self.copies)[:, :, r]


def maxima_stage(chip, at, mask=None, key_bias=None, clip=None):
    nc, sig = chip.nc, chip.stage("maxima")
    units = [(h, qt) for h in range(at.heads) for qt in range(NT)]
    minus = at.q.rearrange("p t b (h w) -> p t b h w", w=at.slot)
    with nc.Block() as block:
        @block.gpsimd
        def _(pool):
            chip.reset_others(pool, sig)

        @block.tensor
        def _(pe):
            for u, (h, qt) in enumerate(units):
                if u >= 2:
                    pe.wait_ge(sig["max_taken"], u - 1)
                banks = chip.psum[:, 4 * (u % 2):4 * (u % 2) + 4, :].rearrange("p a b -> p (a b)")
                k0, k1 = at.keys_of(qt)
                first, end = k0 * P, min(k1 * P, at.keys)
                r = at.rows(h, at.hd)
                for lo in range(first, end, BANK):
                    n = min(BANK, end - lo)
                    masks = at.masks_of(qt, lo, lo + n) if mask is not None else []
                    biased = key_bias is not None and lo < key_bias.shape[1]
                    mm = pe.matmul(banks[:, lo - first:lo - first + n],
                                   at.qT[r, h // at.per, qt * P:(qt + 1) * P],
                                   at.kT[r, h // at.per, lo:lo + n], start=True,
                                   stop=not masks and not biased)
                    for i, (m0, m1, col) in enumerate(masks):
                        mm = pe.matmul(banks[:, col - first:col - first + m1 - m0],
                                       chip.ident_bf[:, :], mask[0][:, m0:m1], start=False,
                                       stop=i == len(masks) - 1)
                    if biased:
                        mm = pe.matmul(banks[:, lo - first:lo - first + n], chip.ones[0:1, 0:P],
                                       key_bias[:, lo:lo + n], start=False, stop=True)
                mm.then_inc(sig["scores_ready"], 1)

        @block.vector
        def _(dve):
            for u, (h, qt) in enumerate(units):
                dve.wait_ge(sig["scores_ready"], u + 1)
                banks = chip.psum[:, 4 * (u % 2):4 * (u % 2) + 4, :].rearrange("p a b -> p (a b)")
                k0, k1 = at.keys_of(qt)
                n = min(k1 * P, at.keys) - k0 * P
                dve.tensor_reduce(minus[:, qt, h // at.per, h % at.per, at.hd:at.hd + 1],
                                  banks[:, :n], AX, ALU.max,
                                  negate=True).then_inc(sig["max_taken"], 1)
            if clip is not None:
                dve.wait_ge(sig["max_taken"], len(units))
                col = at.slots(at.q, NT)[:, :, at.hd:at.hd + 1]
                dve.tensor_scalar(col, col, -clip, clip, ALU.max,
                                  ALU.min).then_inc(sig["max_taken"], 1)


def attend_stage(chip, at, out_col, mask=None, key_bias=None):
    nc, sig = chip.nc, chip.stage("attend")
    units = [(h, kt, *at.queries_of(kt)) for h in range(at.heads) for kt in range(at.key_tiles)]
    per_head = at.key_tiles
    RING = 4
    e = at.vd + 1

    def values_bank(h):
        return chip.psum[:, 4 + h % 4, :NT * e].rearrange("p (t e) -> p t e", e=e)

    with nc.Block() as block:
        @block.gpsimd
        def _(pool):
            chip.reset_others(pool, sig)

        @block.tensor
        def _(pe):
            def scores(h):
                for u in range(h * per_head, (h + 1) * per_head):
                    _, kt, q0, q1 = units[u]
                    if u >= RING:
                        pe.wait_ge(sig["probs_ready"], u - RING + 1)
                    r, w, n = at.rows(h, at.hd + 1), at.width(kt), (q1 - q0) * P
                    ps = chip.psum[:w, u % RING, :n]
                    masks = at.masks_of_keys(kt) if mask is not None else []
                    mm = pe.matmul(ps, at.kT[r, h // at.per, kt * P:kt * P + w],
                                   at.qT[r, h // at.per, q0 * P:q1 * P], start=True,
                                   stop=not masks)
                    for i, (m0, m1, col) in enumerate(masks):
                        mm = pe.matmul(ps[:, col:col + m1 - m0], chip.ident_bf[:, :w],
                                       mask[1][:, m0:m1], start=False, stop=i == len(masks) - 1)
                    mm.then_inc(sig["scores_ready"], 1)

            def values(h):
                pe.wait_ge(sig["probs_ready"], (h + 1) * per_head)
                if h >= 4:
                    pe.wait_ge(sig["heads_kept"], h - 3)
                probs = at.probs[h % at.nbuf]
                for qt in range(NT):
                    k0, k1 = at.keys_of(qt)
                    for kt in range(k0, k1):
                        w = at.width(kt)
                        mm = pe.matmul(values_bank(h)[:, qt], probs[:w, kt, qt * P:(qt + 1) * P],
                                       at.v[:w, kt, h], start=kt == k0, stop=kt == k1 - 1)
                mm.then_inc(sig["values_ready"], 1)

            scores(0)
            for h in range(at.heads):
                if at.nbuf == 2 and h + 1 < at.heads:
                    scores(h + 1)
                values(h)
                if at.nbuf == 1 and h + 1 < at.heads:
                    scores(h + 1)

        @block.scalar
        def _(act):
            for u, (h, kt, q0, q1) in enumerate(units):
                act.wait_ge(sig["scores_ready"], u + 1)
                if kt == 0 and h >= at.nbuf:
                    act.wait_ge(sig["values_ready"], h - at.nbuf + 1)
                w, n = at.width(kt), (q1 - q0) * P
                bias = key_bias[:w, kt:kt + 1] if key_bias is not None else 0.0
                act.activation(at.probs[h % at.nbuf][:w, kt, q0 * P:q1 * P],
                               chip.psum[:w, u % RING, :n], ACT.Exp, bias=bias,
                               scale=at.scale).then_inc(sig["probs_ready"], 1)

        @block.vector
        def _(dve):
            order = Order(dve, sig["order"])
            for h in range(at.heads):
                dve.wait_ge(sig["values_ready"], h + 1)
                made = values_bank(h)
                sums = chip.roots[:, 0:NT].unsqueeze(2)
                order(dve.reciprocal(sums, made[:, :, at.vd:at.vd + 1]))
                out = at.out[:, :, bass.ds(out_col + h * at.vd, at.vd)]
                dve.tensor_tensor(out, made[:, :, 0:at.vd], sums.to_broadcast([P, NT, at.vd]),
                                  ALU.mult).then_inc(sig["heads_kept"], 1)
                dve.wait_ge(sig["heads_kept"], h + 1)


def attend_clipped_stage(chip, at, out_col, clip):
    nc, sig = chip.nc, chip.stage("attend")
    units = [(h, kt) for h in range(at.heads) for kt in range(at.key_tiles)]
    per_head, RING, e = at.key_tiles, 3, at.vd + 1
    minus_max = at.tmp_rows
    clipped = at.clip_rows

    def values_bank(h):
        return chip.psum[:, 4 + h % 4, :NT * e].rearrange("p (t e) -> p t e", e=e)

    with nc.Block() as block:
        @block.tensor
        def _(pe):
            def scores(h):
                if h >= 1:
                    pe.wait_ge(sig["shift_kept"], h)
                r = at.rows(h, at.hd + 1)
                pe.matmul(chip.psum[:, 3], chip.pick_max[r, :], at.qT[r, h // at.per, :],
                          start=True, stop=True).then_inc(sig["shift_ready"], 1)
                r = at.rows(h, at.hd)
                for u in range(h * per_head, (h + 1) * per_head):
                    kt = units[u][1]
                    if u >= RING:
                        pe.wait_ge(sig["clipped"], u - RING + 1)
                    pe.matmul(chip.psum[:, u % RING], at.kT[r, h // at.per, kt * P:(kt + 1) * P],
                              at.qT[r, h // at.per, :], start=True,
                              stop=True).then_inc(sig["scores_ready"], 1)

            def values(h):
                pe.wait_ge(sig["probs_ready"], (h + 1) * per_head)
                if h >= 4:
                    pe.wait_ge(sig["heads_kept"], h - 3)
                for qt in range(NT):
                    for kt in range(per_head):
                        mm = pe.matmul(values_bank(h)[:, qt],
                                       at.probs[h % 2][:, kt, qt * P:(qt + 1) * P],
                                       at.v[:, kt, h], start=kt == 0, stop=kt == per_head - 1)
                mm.then_inc(sig["values_ready"], 1)

            scores(0)
            for h in range(at.heads):
                if h + 1 < at.heads:
                    scores(h + 1)
                values(h)

        @block.scalar
        def _(act):
            for u, (h, kt) in enumerate(units):
                if kt == 0:
                    act.wait_ge(sig["shift_ready"], h + 1)
                    if h >= 2:
                        act.wait_ge(sig["clipped"], (h - 1) * per_head)
                    act.copy(minus_max[:, h % 2], chip.psum[:, 3]).then_inc(sig["shift_kept"], 1)
                    if h >= 2:
                        act.wait_ge(sig["values_ready"], h - 1)
                act.wait_ge(sig["clipped"], u + 1)
                act.activation(at.probs[h % 2][:, kt, :], clipped[:, u % 4], ACT.Exp,
                               scale=at.scale).then_inc(sig["exp_ready"], 1)

        @block.gpsimd
        def _(pool):
            chip.reset_others(pool, sig)
            for u, (h, kt) in enumerate(units):
                pool.wait_ge(sig["exp_ready"], u + 1)
                probs = at.probs[h % 2][:, kt, :]
                pool.tensor_scalar(probs, probs, 1.0, None, ALU.min).then_inc(sig["probs_ready"], 1)

        @block.vector
        def _(dve):
            order = Order(dve, sig["order"])

            def keep(h):
                dve.wait_ge(sig["values_ready"], h + 1)
                made = values_bank(h)
                sums = chip.roots[:, 0:NT].unsqueeze(2)
                order(dve.reciprocal(sums, made[:, :, at.vd:at.vd + 1]))
                out = at.out[:, :, out_col + h * at.vd:out_col + (h + 1) * at.vd]
                dve.tensor_tensor(out, made[:, :, 0:at.vd], sums.to_broadcast([P, NT, at.vd]),
                                  ALU.mult).then_inc(sig["heads_kept"], 1)
                dve.wait_ge(sig["heads_kept"], h + 1)

            for u, (h, kt) in enumerate(units):
                dve.wait_ge(sig["scores_ready"], u + 1)
                if kt == 0:
                    dve.wait_ge(sig["shift_kept"], h + 1)
                if u >= 4:
                    dve.wait_ge(sig["exp_ready"], u - 3)
                dve.scalar_tensor_tensor(clipped[:, u % 4], chip.psum[:, u % RING], -clip,
                                         minus_max[:, h % 2], ALU.max,
                                         ALU.add).then_inc(sig["clipped"], 1)
                if kt == per_head - 1 and h >= 1:
                    keep(h - 1)
            keep(at.heads - 1)


def turn_groups(at, which, tiles):
    src, dst = (at.q, at.qT) if which == "q" else (at.k, at.kT)
    groups = []
    for b in range(4):
        for t0 in range(0, tiles, 4):
            parts, end = [], 0
            for t in range(t0, min(t0 + 4, tiles)):
                w = P if which == "q" else at.width(t)
                parts.append((src[:w, t, b, :], end))
                end += w
            groups.append((parts, dst[:, b, t0 * P:t0 * P + end]))
    return groups


def out_stages(chip, at, b, inner_width, loads, bias, addend, dst):
    chunks = inner_width // P
    outT = at.carve_outT(chip)
    turn_stage(chip, [([(at.out[:, t, c * P:(c + 1) * P], t * P) for t in range(NT)], outT[:, c])
                      for c in range(chunks)])
    cols = slice(b * S, (b + 1) * S)
    jobs = [(dst[:, m, cols], [(chip.w_out[:, c, m * P:(m + 1) * P], outT[:, c])
                               for c in range(chunks)],
             None if bias is None else bias[:, m:m + 1],
             None if addend is None else addend[:, m, cols]) for m in range(2)]
    linear_stage(chip, loads, jobs)


def attention_core(chip, at, out_col, mask=None, key_row=None, key_col=None, clip=None):
    turn_stage(chip, turn_groups(at, "q", NT) + turn_groups(at, "k", at.key_tiles))
    maxima_stage(chip, at, mask, key_row, clip)
    turn_stage(chip, turn_groups(at, "q", NT))
    if clip is None:
        attend_stage(chip, at, out_col, mask, key_col)
    else:
        attend_clipped_stage(chip, at, out_col, clip)


def rope_tables(hd, base, pairs, theta=None):
    import numpy as np
    half = hd // 2
    f32 = np.float32
    if theta is None:
        theta = f32(1.0) / (f32(base) ** (np.arange(0, hd, 2, dtype=f32) / f32(hd)))
    angle = np.arange(S, dtype=f32)[:, None] * theta[None, :].astype(f32)
    c, s = np.cos(angle), np.sin(angle)
    if pairs:
        cos, sin = np.repeat(c, 2, -1), np.repeat(s, 2, -1)
        sin[:, 0::2] *= -1
    else:
        cos, sin = np.concatenate([c, c], -1), np.concatenate([-s, s], -1)
    return cos.astype(f32), sin.astype(f32)


def by_partition(table):
    import numpy as np
    return np.ascontiguousarray(table.reshape(NT, P, -1).transpose(1, 0, 2).reshape(P, -1))


def band_masks(lowest, highest, other):
    import numpy as np
    i, j = np.arange(P)[:, None], np.arange(P)[None, :]

    def tile(distance):
        return np.where((distance >= lowest) & (distance <= highest), 0.0, -BIG)

    diag_q, diag_k = tile(i - j), tile(j - i)
    side_q, side_k = tile(i - j - other * P), tile(j - i - other * P)
    if other == -1:
        return np.concatenate([side_q, diag_q, diag_k, side_k], 1)
    if other == 1:
        return np.concatenate([diag_q, side_q, side_k, diag_k], 1)
    return np.concatenate([diag_q, diag_q, diag_k, diag_k], 1)


def constants():
    import numpy as np
    bf16 = mybir.dt.np(BF16)
    out = {"ident": np.eye(P, dtype=np.float32), "ident_bf": np.eye(P).astype(bf16)}
    for name, args in (("causal", (0, 10 ** 6, 0)), ("band64", (0, 63, -1)), ("band65", (0, 64, -1)),
                       ("band128", (0, 127, -1)), ("ahead", (-16, 10 ** 6, 1))):
        out["mask_" + name] = band_masks(*args).astype(bf16)
    for name, args in (("rope_l0g", (16, 1e6, True)), ("rope_l0l", (16, 1e4, True)),
                       ("rope_l2", (32, 1e4, False)), ("rope_l3", (16, 1e4, False))):
        cos, sin = rope_tables(*args)
        out[name + "_cos"], out[name + "_sin"] = by_partition(cos), by_partition(sin)
    out["pick_max"] = np.zeros((P, P), np.float32)
    out["pick_max"][16::32] = 1.0
    out["head_sum"] = np.repeat(np.eye(8, dtype=np.float32), 16, 0)
    for n in (4, 16, 40):
        out[f"ties{n}"] = np.tril(np.ones((n, n), np.float32), -1).reshape(1, n * n)
    sel = np.zeros((17, 12, P), np.float32)
    for f in range(8):
        sel[2 * f, f, :64] = 1.0
        sel[2 * f + 1, f, 64:] = 1.0
    sel[16, 8:] = 1.0
    out["sel_l2"] = sel
    sel = np.zeros((40, 33, P), np.float32)
    for f in range(32):
        sel[f, f] = 1.0
    sel[32:, 32] = 1.0
    out["sel_l3"] = sel
    cos, sin = rope_tables(64, 1e4, False)
    f32 = np.float32
    half = np.arange(0, 64, 2, dtype=f32)
    base = (half + f32(0.4 * 64)) / f32(1.4 * 64)
    power = (np.arange(S, dtype=f32) - S // 2) / f32(32)
    scale = base[None, :] ** power[:, None]
    scale = np.concatenate([scale, scale], -1).astype(f32)
    for name, s in (("xpos_q", scale), ("xpos_k", f32(1.0) / scale)):
        out[name + "_cos"], out[name + "_sin"] = by_partition(cos * s), by_partition(sin * s)
    return out


def fm(w):
    return w.rearrange("(c p) n -> p c n", p=P)


def ctx_loads(dst, w, cols=slice(None)):
    return [(dst[:, 0], w[0:P, cols]), (dst[:DC - P, 1], w[P:DC, cols])]


def layer0_attention(chip, a):
    h = chip.inner
    for kind, table, mask_name in (("g", "rope_l0g", "causal"), ("l", "rope_l0l", "band64")):
        src = chip.state if kind == "g" else h
        gains = chip.gains[:, 0:2]
        norm_name = "L0_attn_norm1_w" if kind == "g" else "L0_attn_norm2_w"
        norm_stage(chip, src, chip.normed, (P, P), B * S, 1e-6, center=False, gain=gains,
                   loads=[(gains, a[norm_name + "_col"])])
        at = Attention(chip, 16, 16, NT, 0.25, "causal" if kind == "g" else "band")
        fill_slots_stage(chip, at)
        cos, sin = chip.tables(16)
        load_stage(chip, [(cos, a[table + "_cos"].rearrange("p (t e) -> p t e", t=NT)),
                          (sin, a[table + "_sin"].rearrange("p (t e) -> p t e", t=NT)),
                          (chip.masks[:, :], a["mask_" + mask_name]),
                          (chip.w_in[:, :, 0:D], fm(a[f"L0_attn_{kind}_wq"])),
                          (chip.w_out[:, 0:2, :], fm(a[f"L0_attn_{kind}_wo"]))]
                   + ([(chip.w_in[:, :, 256:320], fm(a["L0_attn_g_kv_down"])),
                       (chip.w_in[:64, 0, 384:448], a["L0_attn_g_k_up"]),
                       (chip.w_in[:64, 0, 448:512], a["L0_attn_g_v_up"])] if kind == "g" else
                      [(chip.w_in[:, :, 256:320], fm(a["L0_attn_l_wk"])),
                       (chip.w_in[:, :, 320:384], fm(a["L0_attn_l_wv"]))]))
        masks = (chip.masks[:, 0:256], chip.masks[:, 256:512])
        latent = chip.carve(31936, BANK)[:64]
        for b in range(B):
            cols = slice(b * S, (b + 1) * S)
            if kind == "g":
                linear_stage(chip, [], [(latent, [(chip.w_in[:, c, 256:320],
                                                   chip.normed[:, c, cols]) for c in range(2)],
                                         None, None)])
            jobs = []
            for t in range(NT):
                tok = slice(b * S + t * P, b * S + (t + 1) * P)
                x = [chip.normed[:, c, tok] for c in range(2)]
                if kind == "g":
                    products = [(x[0], chip.w_in[:, 0, 0:D], 0, True, False),
                                (x[1], chip.w_in[:, 1, 0:D], 0, False, True),
                                (latent[:, t * P:(t + 1) * P], chip.w_in[:64, 0, 384:512], BANK,
                                 True, True)]
                    k_at = BANK
                else:
                    products = [(x[0], chip.w_in[:, 0, 0:384], 0, True, False),
                                (x[1], chip.w_in[:, 1, 0:384], 0, False, True)]
                    k_at = D
                copies = [(at.raw_q[:, t * D:(t + 1) * D], lambda ps: ps[:, 0:D]),
                          (at.raw_k[:, t * 64:(t + 1) * 64],
                           lambda ps, k=k_at: ps[:, k:k + 64])]
                for r in range(4):
                    copies.append((at.v[:, t].rearrange("p (n r) e -> p n r e", r=4)[:, :, r, 0:16],
                                   lambda ps, k=k_at: ps[:, k + 64:k + 128].rearrange(
                                       "p (n e) -> p n e", e=16)))
                jobs.append((products, copies))
            norm = (1.0 / 16, 1e-6, 0.0, 1.0)
            q_post = HeadPost(chip, at, at.raw_q, at.q, NT, 16, norm, None, cos, sin, True)
            k_post = HeadPost(chip, at, at.raw_k, at.k, NT, 4, norm, None, cos, sin, True, 4)
            project_stage(chip, at, [], jobs, q_post, k_post)
            attention_core(chip, at, 0, masks)
            out_stages(chip, at, b, D, [], None, src, h)
    norm_stage(chip, chip.state, chip.state, (P, P), B * S, 1e-5, add=h)


def cross_attention(chip, a, pre, hd, biased, clip=None):
    at = Attention(chip, hd, hd, SC // P, hd ** -0.5)
    heads_wide = 256 if hd == 16 else 1024
    fill_slots_stage(chip, at)
    bo = chip.gains[:, 0:2]
    loads = [(chip.w_out[:, 0:heads_wide // P, :], fm(a[pre + "Wo"])), (bo, a[pre + "bo_col"])]
    if biased:
        for i, n in enumerate("qkv"):
            loads.append((chip.w_bias[:, i * D:(i + 1) * D], a[pre + "b" + n].unsqueeze(0)))
    load_stage(chip, loads)

    def group(b, g):
        cols = bass.ds(g * D, D)
        w_q, w_k, w_v = (chip.w_in[:, :, i * D:(i + 1) * D] for i in range(3))
        loads = ([(w_q, fm(a[pre + "Wq"])[:, :, cols])] + ctx_loads(w_k, a[pre + "Wk"], cols)
                 + ctx_loads(w_v, a[pre + "Wv"], cols))
        jobs = []
        for t in range(NT):
            tok = slice(b * S + t * P, b * S + (t + 1) * P)
            products = [(chip.state[:, c, tok], w_q[:, c], 0, c == 0, c == 1 and not biased)
                        for c in range(2)]
            if biased:
                products.append((chip.ones[:, 0:P], chip.w_bias[:, 0:D], 0, False, True))
            jobs.append((products, [(at.q[:, t].rearrange("p b (h w) -> p (b h) w", w=at.slot)
                                     [:, :, 0:hd],
                                     lambda ps: ps[:, 0:D].rearrange("p (h e) -> p h e", e=hd))]))
        for t in range(SC // P):
            tok = slice(b * SC + t * P, b * SC + (t + 1) * P)
            products = []
            for c, rows in ((0, P), (1, DC - P)):
                products.append((chip.ctx[:rows, c, tok], chip.w_in[:rows, c, D:3 * D], 0, c == 0,
                                 c == 1 and not biased))
            if biased:
                products.append((chip.ones[:, 0:P], chip.w_bias[:, D:3 * D], 0, False, True))
            jobs.append((products, [
                (at.k[:, t].rearrange("p b (h w) -> p (b h) w", w=at.slot)[:, :, 0:hd],
                 lambda ps: ps[:, 0:D].rearrange("p (h e) -> p h e", e=hd)),
                (at.v[:, t, :, 0:hd],
                 lambda ps: ps[:, D:2 * D].rearrange("p (h e) -> p h e", e=hd))]))
        project_stage(chip, at, loads, jobs)
        attention_core(chip, at, g * D, clip=clip)

    for b in range(B):
        if heads_wide == D:
            group(b, 0)
        else:
            with chip.nc.Fori(0, heads_wide // D) as g:
                group(b, g)
        out_stages(chip, at, b, heads_wide, [], bo, chip.state, chip.inner)
    norm_stage(chip, chip.inner, chip.state, (P, P), B * S, 1e-5)


def shift_stage(chip, src, dst, add=None):
    nc, sig = chip.nc, chip.stage("small")
    with nc.Block() as block:
        @block.gpsimd
        def _(pool):
            chip.reset_others(pool, sig)

        @block.vector
        def _(dve):
            for b in range(B):
                dve.memset(dst[:, 1, b * S:b * S + 1], 0.0)
                dve.tensor_copy(dst[:, 1, b * S + 1:(b + 1) * S], src[:, 1, b * S:(b + 1) * S - 1])
            dve.tensor_copy(dst[:, 0, :], src[:, 0, :]).then_inc(sig["dve_done"], 1)


def copy_stage(chip, src, dst):
    nc, sig = chip.nc, chip.stage("small")
    with nc.Block() as block:
        @block.gpsimd
        def _(pool):
            chip.reset_others(pool, sig)

        @block.vector
        def _(dve):
            dve.tensor_copy(dst[:, :, :], src[:, :, :]).then_inc(sig["dve_done"], 1)


def gated_stage(chip, x, tiles, act_func, dst, addend, bias_loads=(), bias=None, out_bias=None,
                spread=None):
    nc, sig = chip.nc, chip.stage("gated")
    RING, halves = 4, B * S // BANK
    gate_up = chip.carve(0, RING, 2, 2 * P)
    down = chip.carve(2048, RING, D)
    acted = chip.carve(3072, 2, BANK)
    hidden = chip.carve(4096, 2, BANK)
    weighted = chip.carve(5120, 2, BANK)
    units = [(f, h) for f in range(len(tiles)) for h in range(halves)]
    gate_ps, up_ps, spread_ps = chip.psum[:, 4], chip.psum[:, 5], chip.psum[:, 6]
    sums = [[chip.psum[:, 2 * m + h] for h in range(halves)] for m in range(2)]
    made = hidden if spread is None else weighted
    with nc.Block() as block:
        @block.gpsimd
        def _(pool):
            chip.reset_others(pool, sig)

        @block.sync
        def _(sp):
            for to, frm in bias_loads:
                sp.dma_start(to, frm).then_inc(sig["bias_loaded"], 16)
            for f, (rows, loads) in enumerate(tiles):
                if f >= RING:
                    sp.wait_ge(sig["tile_done"], f - RING + 1)
                for to, frm in loads(gate_up[:, f % RING], down[:, f % RING]):
                    sp.dma_start(to, frm).then_inc(sig[f"slot{f % RING}_loaded"], 16)

        @block.tensor
        def _(pe):
            def down_products(u):
                f, h = units[u]
                rows = tiles[f][0]
                pe.wait_ge(sig["hidden_ready"], u + 1)
                for m in range(2):
                    mm = pe.matmul(sums[m][h], down[:rows, f % RING, m * P:(m + 1) * P],
                                   made[:rows, u % 2], start=f == 0, stop=f == len(tiles) - 1)
                if h == halves - 1:
                    mm.then_inc(sig["tile_done"], 1)

            for u, (f, h) in enumerate(units):
                rows, loads = tiles[f]
                if h == 0:
                    n = len(loads(gate_up[:, 0], down[:, 0]))
                    pe.wait_ge(sig[f"slot{f % RING}_loaded"], 16 * n * (f // RING + 1))
                cols = slice(h * BANK, (h + 1) * BANK)
                if u >= 1:
                    pe.wait_ge(sig["gate_acted"], u)
                for c in range(2):
                    mm = pe.matmul(gate_ps[:rows], gate_up[:, f % RING, c, 0:rows], x[:, c, cols],
                                   start=c == 0, stop=c == 1)
                mm.then_inc(sig["gate_ready"], 1)
                if u >= 1:
                    pe.wait_ge(sig["hidden_ready"], u)
                for c in range(2):
                    mm = pe.matmul(up_ps[:rows], gate_up[:, f % RING, c, P:P + rows],
                                   x[:, c, cols], start=c == 0, stop=c == 1)
                if spread is not None:
                    sel, combine = spread(f, cols)
                    mm = pe.matmul(spread_ps[:rows], sel, combine, start=True, stop=True)
                mm.then_inc(sig["up_ready"], 1)
                if u >= 1:
                    down_products(u - 1)
            down_products(len(units) - 1)

        @block.scalar
        def _(act):
            if bias_loads:
                act.wait_ge(sig["bias_loaded"], 16 * len(bias_loads))
            for u, (f, h) in enumerate(units):
                rows = tiles[f][0]
                act.wait_ge(sig["gate_ready"], u + 1)
                if u >= 2:
                    act.wait_ge(sig["hidden_ready"], u - 1)
                act.activation(acted[:rows, u % 2], gate_ps[:rows], act_func,
                               bias=0.0 if bias is None else bias[0][:rows, f:f + 1]
                               ).then_inc(sig["gate_acted"], 1)

        @block.vector
        def _(dve):
            order = Order(dve, sig["order"])
            if bias_loads:
                dve.wait_ge(sig["bias_loaded"], 16 * len(bias_loads))
            for u, (f, h) in enumerate(units):
                rows = tiles[f][0]
                dve.wait_ge(sig["up_ready"], u + 1)
                dve.wait_ge(sig["gate_acted"], u + 1)
                if u >= 2 * halves:
                    dve.wait_ge(sig["tile_done"], (u - 2) // halves)
                if bias is None:
                    ins = dve.tensor_tensor(hidden[:rows, u % 2], up_ps[:rows],
                                            acted[:rows, u % 2], ALU.mult)
                else:
                    ins = dve.scalar_tensor_tensor(hidden[:rows, u % 2], up_ps[:rows],
                                                   bias[1][:rows, f:f + 1], acted[:rows, u % 2],
                                                   ALU.add, ALU.mult)
                if spread is not None:
                    order(ins)
                    ins = dve.tensor_tensor(weighted[:rows, u % 2], spread_ps[:rows],
                                            hidden[:rows, u % 2], ALU.mult)
                ins.then_inc(sig["hidden_ready"], 1)
            dve.wait_ge(sig["tile_done"], len(tiles))
            for m in range(2):
                for h in range(halves):
                    cols = slice(h * BANK, (h + 1) * BANK)
                    if addend is None:
                        dve.tensor_copy(dst[:, m, cols], sums[m][h])
                    elif out_bias is None:
                        dve.tensor_tensor(dst[:, m, cols], sums[m][h], addend[:, m, cols], ALU.add)
                    else:
                        dve.scalar_tensor_tensor(dst[:, m, cols], sums[m][h],
                                                 out_bias[:, m:m + 1], addend[:, m, cols],
                                                 ALU.add, ALU.add)


def layer0_ffn(chip, a):
    depth, inner = 6, 1024
    hidden = 682
    at = Attention(chip, 64, 64, NT, 8.0, "band")
    (q_cos, q_sin), (k_cos, k_sin) = chip.tables(64, 0), chip.tables(64, 1)
    tables = [(q_cos, "xpos_q_cos"), (q_sin, "xpos_q_sin"), (k_cos, "xpos_k_cos"),
              (k_sin, "xpos_k_sin")]
    copy_stage(chip, chip.state, chip.inner)
    load_stage(chip, [(t, a[n].rearrange("p (t e) -> p t e", t=NT)) for t, n in tables]
               + [(chip.masks[:, :], a["mask_band65"])])
    masks = (chip.masks[:, 0:256], chip.masks[:, 256:512])
    h = chip.inner
    q_gain, k_gain = chip.gains[:, 0:64], chip.gains[:, 64:128]
    b2, b1 = chip.gains[:, 128:130], chip.gains[:, 130:142]
    ln_g, ln_b = chip.gains[:, 142:144], chip.gains[:, 144:146]
    with chip.nc.Fori(0, depth) as d:
        shift_stage(chip, h, chip.normed)
        load_stage(chip, [
            (chip.w_out[:, :, :], a["L0_ffn_Wo"][bass.ds(d, 1)].rearrange(
                "o (c p) n -> p (o c) n", p=P)),
            (q_gain, a["L0_ffn_q_scale"][bass.ds(d, 1)].partition_broadcast(P)),
            (k_gain, a["L0_ffn_k_scale"][bass.ds(d, 1)].partition_broadcast(P)),
            (b2, a["L0_ffn_b2_col"][:, bass.ds(2 * d, 2)]),
            (ln_g, a["L0_ffn_ln_g_col"][:, bass.ds(2 * d, 2)]),
            (ln_b, a["L0_ffn_ln_b_col"][:, bass.ds(2 * d, 2)]),
            (b1, a["L0_ffn_b1_col"][:, bass.ds(12 * d, 12)])])
        fill_slots_stage(chip, at)
        for b in range(B):
            with chip.nc.Fori(0, inner // D) as g:
                jobs = []
                for t in range(NT):
                    tok = slice(b * S + t * P, b * S + (t + 1) * P)
                    products = []
                    for lo, hi in ((0, BANK), (BANK, 3 * D)):
                        products += [(chip.normed[:, c, tok], chip.w_in[:, c, lo:hi], lo, c == 0,
                                      c == 1) for c in range(2)]
                    jobs.append((products, [
                        (at.raw_q[:, t * D:(t + 1) * D], lambda ps: ps[:, 0:D]),
                        (at.raw_k[:, t * D:(t + 1) * D], lambda ps: ps[:, D:2 * D]),
                        (at.v[:, t, :, 0:64], lambda ps: ps[:, 2 * D:3 * D].rearrange(
                            "p (h e) -> p h e", e=64))]))
                norm = (1.0, 0.0, 1e-12, 1.0)
                q_post = HeadPost(chip, at, at.raw_q, at.q, NT, 4, norm, q_gain, q_cos, q_sin)
                k_post = HeadPost(chip, at, at.raw_k, at.k, NT, 4, norm, k_gain, k_cos, k_sin)
                w = a["L0_ffn_Wqkv_groups"][bass.ds(d * 4 + g, 1)].rearrange(
                    "o (c p) n -> p (o c) n", p=P)
                project_stage(chip, at, [(chip.w_in[:, :, :], w)], jobs, q_post, k_post)
                attention_core(chip, at, g * D, masks)
            out_stages(chip, at, b, inner, [], None, h, h)
        shift_stage(chip, h, chip.normed)
        norm_stage(chip, chip.normed, chip.normed, (P, P), B * S, 1e-5, gain=ln_g, shift=ln_b)
        tiles = []
        for f in range(6):
            rows = min(P, hidden - f * P)
            w1 = a["L0_ffn_W1"][bass.ds(d, 1)].rearrange("o (c p) n -> p (o c) n", p=P)
            w2 = a["L0_ffn_W2"][bass.ds(d, 1), f * P:f * P + rows].rearrange("o p n -> p (o n)")

            def loads(gate_up, down, f=f, rows=rows, w1=w1, w2=w2):
                return [(gate_up[:, :, 0:rows], w1[:, :, hidden + f * P:hidden + f * P + rows]),
                        (gate_up[:, :, P:P + rows], w1[:, :, f * P:f * P + rows]),
                        (down[:rows], w2)]

            tiles.append((rows, loads))
        gated_stage(chip, chip.normed, tiles, ACT.Gelu, h, h, bias=(b1[:, 6:12], b1[:, 0:6]),
                    out_bias=b2)
    norm_stage(chip, chip.state, chip.state, (P, P), B * S, 1e-5, add=h)


def build(nc, a, out, upto=12):
    chip = Chip(nc)
    start_stage(chip, [(chip.state[:, :, :], a["x_fm"].rearrange("(c p) n -> p c n", p=P)),
                       (chip.ident[:, :], a["ident"]), (chip.ident_bf[:, :], a["ident_bf"]),
                       (chip.pick_max[:, :], a["pick_max"])]
                + ctx_loads(chip.ctx, a["ctx_fm"]))
    for layer in LAYERS[:upto]:
        layer(chip, a)
    store_stage(chip, out)


def store_stage(chip, out):
    nc, sig = chip.nc, chip.stage("small")
    with nc.Block() as block:
        @block.gpsimd
        def _(pool):
            chip.reset_others(pool, sig)

        @block.sync
        def _(sp):
            sp.dma_start(out.rearrange("(c p) n -> p c n", p=P),
                         chip.state[:, :, :]).then_inc(sig["weights_loaded"], 16)
            sp.wait_ge(sig["weights_loaded"], 16)


def layer0_cross(chip, a):
    cross_attention(chip, a, "L0_xattn_", 16, True)


def layer1_cross(chip, a):
    cross_attention(chip, a, "L1_xattn_", 64, False)


def layer1_linear_attention(chip, a):
    pre, feats = "L1_attn_", 64
    at = Attention(chip, 16, 16, NT, 1.0)
    bo = chip.gains[:, 0:2]
    qkT = chip.carve(0, 4, BANK)
    sq = chip.carve(2048, 4, BANK)
    v = chip.carve(4096, NT, 16 * 17).rearrange("p t (h e) -> p t h e", e=17)
    phi = chip.carve(5184, 2, NT * 16, feats)
    shifted = chip.carve(13376, 2, 8, feats)
    phi_qT = chip.carve(14400, 8, BANK)
    kv = chip.carve(18496, 8, 34)
    proj = chip.carve(18768, 2, BANK)
    top = chip.cols[:, 0:16].rearrange("p (n h) -> p n h", h=8)
    down = chip.cols[:, 16:32].rearrange("p (n h) -> p n h", h=8)
    head_sum = chip.cols[:, 32:40]
    nc = chip.nc
    load_stage(chip, [(chip.w_in[:, :, i * D:(i + 1) * D], fm(a[pre + n + "_t"]))
                      for i, n in enumerate(("Wq", "Wk", "Wv"))]
               + [(chip.w_out[:, 0:2, :], fm(a[pre + "Wo_t"])), (bo, a[pre + "bo_col"]),
                  (proj, a["L1_attn_proj_diag"].rearrange("c p n -> p c n")),
                  (head_sum, a["head_sum"])])

    def features_stage():
        sig = chip.stage("features")
        units = [(i, t, c) for i in range(2) for t in range(NT) for c in range(2)]
        with nc.Block() as block:
            @block.gpsimd
            def _(pool):
                chip.reset_others(pool, sig)
                pool.memset(kv, 0.0).then_inc(sig["cleared"], 1)

            @block.tensor
            def _(pe):
                pe.wait_ge(sig["squares_ready"], 4)
                for u, (i, t, c) in enumerate(units):
                    if u >= 4:
                        pe.wait_ge(sig["shifted_ready"], u - 3)
                    tok = slice(t * P, (t + 1) * P)
                    pe.matmul(chip.psum[:, 4 + u % 4, 0:8], sq[:, 2 * i + c, tok], head_sum,
                              start=True, stop=True)
                    pe.matmul(chip.psum[:, u % 4], qkT[:, 2 * i + c, tok], proj[:, c],
                              start=True, stop=True).then_inc(sig["logits_ready"], 1)

            @block.scalar
            def _(act):
                for n in range(4):
                    act.activation(sq[:, n], qkT[:, n], ACT.Square
                                   ).then_inc(sig["squares_ready"], 1)
                for u, (i, t, c) in enumerate(units):
                    act.wait_ge(sig["shifted_ready"], u + 1)
                    out = phi[:, i, t * 16 + c * 8:t * 16 + c * 8 + 8]
                    act.activation(out, shifted[:, u % 2], ACT.Exp,
                                   scale=0.25).then_inc(sig["exp_ready"], 1)

            @block.vector
            def _(dve):
                order = Order(dve, sig["order"])
                for u, (i, t, c) in enumerate(units):
                    dve.wait_ge(sig["logits_ready"], u + 1)
                    logits = chip.psum[:, u % 4].rearrange("p (h m) -> p h m", m=feats)
                    if u >= 2:
                        dve.wait_ge(sig["exp_ready"], u - 1)
                    order(dve.tensor_reduce(top[:, u % 2], logits, AX, ALU.max))
                    order(dve.scalar_tensor_tensor(down[:, u % 2], chip.psum[:, 4 + u % 4, 0:8],
                                                   0.125, top[:, u % 2], ALU.mult, ALU.add))
                    dve.tensor_tensor(shifted[:, u % 2], logits,
                                      down[:, u % 2].unsqueeze(2).to_broadcast([P, 8, feats]),
                                      ALU.subtract).then_inc(sig["shifted_ready"], 1)
                dve.wait_ge(sig["exp_ready"], len(units))
                dve.tensor_scalar(phi, phi, 1e-6, 0.125, ALU.add,
                                  ALU.mult).then_inc(sig["phi_ready"], 1)

    def sums_stage():
        sig = chip.stage("small")
        with nc.Block() as block:
            @block.gpsimd
            def _(pool):
                chip.reset_others(pool, sig)

            @block.tensor
            def _(pe):
                for p in range(8):
                    for t in range(NT):
                        lhs = phi[:, 1, t * 16 + 2 * p:t * 16 + 2 * p + 2].rearrange(
                            "p h m -> p (h m)")
                        mm = pe.matmul(chip.psum[:, 0, p * 34:(p + 1) * 34], lhs,
                                       v[:, t, 2 * p:2 * p + 2].rearrange("p h e -> p (h e)"),
                                       start=t == 0, stop=t == NT - 1)
                mm.then_inc(sig["pe_done"], 1)

            @block.vector
            def _(dve):
                dve.wait_ge(sig["pe_done"], 1)
                made = chip.psum[:, 0, 0:8 * 34].rearrange("p (n e) -> p n e", e=34)
                for i in range(2):
                    r, c = slice(64 * i, 64 * i + 64), slice(17 * i, 17 * i + 17)
                    dve.tensor_copy(kv[r, :, c], made[r, :, c]).then_inc(sig["dve_done"], 1)

    def values_stage():
        sig = chip.stage("small")
        sums = chip.roots[:, 0:16].unsqueeze(2)
        with nc.Block() as block:
            @block.gpsimd
            def _(pool):
                chip.reset_others(pool, sig)

            @block.tensor
            def _(pe):
                for t in range(NT):
                    for p in range(8):
                        mm = pe.matmul(chip.psum[:, t, p * 34:(p + 1) * 34],
                                       phi_qT[:, p, t * P:(t + 1) * P], kv[:, p],
                                       start=True, stop=True)
                    mm.then_inc(sig["pe_done"], 1)

            @block.vector
            def _(dve):
                order = Order(dve, sig["order"])
                for t in range(NT):
                    dve.wait_ge(sig["pe_done"], t + 1)
                    made = chip.psum[:, t, 0:16 * 17].rearrange("p (h e) -> p h e", e=17)
                    order(dve.tensor_scalar(sums, made[:, :, 16:17], 1e-6, None, ALU.add))
                    order(dve.reciprocal(sums, sums))
                    out = at.out[:, t, 0:D].rearrange("p (h e) -> p h e", e=16)
                    order(dve.tensor_tensor(out, made[:, :, 0:16],
                                            sums.to_broadcast([P, 16, 16]), ALU.mult))

    for b in range(B):
        cols = slice(b * S, (b + 1) * S)
        linear_stage(chip, [], [
            (qkT[:, 2 * i + m], [(chip.w_in[:, c, i * D + m * P:i * D + (m + 1) * P],
                                  chip.state[:, c, cols]) for c in range(2)], None, None)
            for i in range(2) for m in range(2)])
        ones_stage(chip, v)
        jobs = []
        for t in range(NT):
            tok = slice(b * S + t * P, b * S + (t + 1) * P)
            jobs.append(([(chip.state[:, c, tok], chip.w_in[:, c, 2 * D:3 * D], 0, c == 0, c == 1)
                          for c in range(2)],
                         [(v[:, t, :, 0:16], lambda ps: ps[:, 0:D].rearrange(
                             "p (h e) -> p h e", e=16))]))
        project_stage(chip, at, [], jobs)
        features_stage()
        turn_stage(chip, [([(phi[:, 0, t * 16 + 2 * p:t * 16 + 2 * p + 2].rearrange(
            "p h m -> p (h m)"), t * P) for t in range(NT)], phi_qT[:, p]) for p in range(8)])
        sums_stage()
        values_stage()
        out_stages(chip, at, b, D, [], bo, chip.state, chip.inner)
    norm_stage(chip, chip.inner, chip.state, (P, P), B * S, 1e-5)


def ones_stage(chip, v):
    nc, sig = chip.nc, chip.stage("small")
    with nc.Block() as block:
        @block.gpsimd
        def _(pool):
            chip.reset_others(pool, sig)
            pool.memset(v, 1.0).then_inc(sig["pool_done"], 1)


ROUND = 1.5 * 2 ** 23


def quantize_steps(order, dve, out, t, inverse, scale, low, high):
    order(dve.tensor_scalar(out, t, inverse, ROUND, ALU.mult, ALU.add))
    order(dve.tensor_scalar(out, out, ROUND, high, ALU.subtract, ALU.min))
    order(dve.tensor_scalar(out, out, low, scale, ALU.max, ALU.mult))


def quantize_activation_stage(chip, src, dst, times=None, then=None):
    nc, sig = chip.nc, chip.stage("quantize")
    top, inverse, scale = (chip.cols[:, i:i + 1] for i in range(3))
    with nc.Block() as block:
        @block.gpsimd
        def _(pool):
            chip.reset_others(pool, sig)
            pool.wait_ge(sig["row_max"], 1)
            pool.partition_all_reduce(scale, top, P, bass.bass_isa.ReduceOp.max
                                      ).then_inc(sig["all_max"], 1)

        @block.vector
        def _(dve):
            order = Order(dve, sig["order"])
            if times is not None:
                order(dve.tensor_tensor(src, src, times, ALU.mult))
            dve.tensor_reduce(top, src, mybir.AxisListType.XY, ALU.max,
                              apply_absolute_value=True).then_inc(sig["row_max"], 1)
            dve.wait_ge(sig["all_max"], 1)
            order(dve.tensor_scalar(scale, scale, 1.0 / 32767.0, 1e-12, ALU.mult, ALU.max))
            order(dve.reciprocal(inverse, scale))
            quantize_steps(order, dve, dst, src, inverse, scale, -32768.0, 32767.0)
            if then is not None:
                sigmoid = then
                dve.wait_ge(sig["sigmoid_ready"], 1)
                order(dve.tensor_scalar(sigmoid, sigmoid, 65536.0, ROUND, ALU.mult, ALU.add))
                order(dve.tensor_scalar(sigmoid, sigmoid, ROUND, 65535.0, ALU.subtract, ALU.min))
                order(dve.tensor_scalar(sigmoid, sigmoid, 0.0, 2.0 ** -16, ALU.max, ALU.mult))
                order(dve.tensor_tensor(dst, dst, sigmoid, ALU.mult))

        @block.scalar
        def _(act):
            if then is not None:
                act.wait_ge(sig["order"], 5 + (times is not None))
                act.activation(then, dst, ACT.Sigmoid).then_inc(sig["sigmoid_ready"], 1)


def layer1_ffn(chip, a):
    wide, blk = 768, 32
    w_raw = chip.carve(0, 6, D)
    w_gate_t, w_up_t = chip.carve(1536, 2, wide), chip.carve(3072, 2, wide)
    w_down_t = chip.carve(4608, 6, D)
    gate, up, sigmoid = (chip.carve(6144 + 6144 * i, 6, B * S) for i in range(3))
    steps = chip.cols[:, 0:48].unsqueeze(2)
    inverse = chip.roots[:, 0:48].unsqueeze(2)
    nc = chip.nc

    def weight_stage(name):
        sig = chip.stage("small")
        w = a["L1_ffn_" + name].rearrange("(c p) n -> p c n", p=P)
        raw = w_raw.rearrange("p a b -> p (a b)")[:, 0:6 * D].rearrange(
            "p (c n) -> p c n", n=w.shape[2])
        blocks = w_raw.rearrange("p a (n e) -> p (a n) e", e=blk)
        with nc.Block() as block:
            @block.gpsimd
            def _(pool):
                chip.reset_others(pool, sig)

            @block.sync
            def _(sp):
                sp.dma_start(raw, w).then_inc(sig["weights_loaded"], 16)

            @block.vector
            def _(dve):
                order = Order(dve, sig["order"])
                dve.wait_ge(sig["weights_loaded"], 16)
                order(dve.tensor_reduce(steps, blocks, AX, ALU.max, apply_absolute_value=True))
                order(dve.tensor_scalar(steps, steps, 1.0 / 7.0, 1e-12, ALU.mult, ALU.max))
                order(dve.reciprocal(inverse, steps))
                order(dve.tensor_tensor(blocks, blocks, inverse.to_broadcast([P, 48, blk]),
                                        ALU.mult))
                order(dve.tensor_scalar(blocks, blocks, ROUND, ROUND, ALU.add, ALU.subtract))
                order(dve.tensor_scalar(blocks, blocks, -8.0, 7.0, ALU.max, ALU.min))
                order(dve.tensor_tensor(blocks, blocks, steps.to_broadcast([P, 48, blk]),
                                        ALU.mult))
        return raw

    for name, dst in (("w_gate", w_gate_t), ("w_up", w_up_t)):
        raw = weight_stage(name)
        turn_stage(chip, [([(raw[:, o, c * P:(c + 1) * P], (o % 3) * P)
                            for o in range(o0, o0 + 3)], dst[:, c, o0 * P:(o0 + 3) * P])
                          for c in range(2) for o0 in (0, 3)])
    raw = weight_stage("w_down")
    turn_stage(chip, [([(raw[:, o, c * P:(c + 1) * P], o * P) for o in range(2)], w_down_t[:, c])
                      for c in range(6)])
    quantize_activation_stage(chip, chip.state[:, :, :], chip.normed[:, :, :])
    for w, dst in ((w_gate_t, gate), (w_up_t, up)):
        linear_stage(chip, [], [(dst[:, f, h * BANK:(h + 1) * BANK],
                                 [(w[:, c, f * P:(f + 1) * P],
                                   chip.normed[:, c, h * BANK:(h + 1) * BANK]) for c in range(2)],
                                 None, None) for f in range(6) for h in range(2)])
        quantize_activation_stage(chip, dst, dst, then=sigmoid if dst is gate else None)
    quantize_activation_stage(chip, gate, gate)
    quantize_activation_stage(chip, gate, gate, times=up)
    linear_stage(chip, [], [(chip.inner[:, m, h * BANK:(h + 1) * BANK],
                             [(w_down_t[:, f, m * P:(m + 1) * P],
                               gate[:, f, h * BANK:(h + 1) * BANK]) for f in range(6)],
                             None, chip.state[:, m, h * BANK:(h + 1) * BANK])
                            for m in range(2) for h in range(2)])
    norm_stage(chip, chip.inner, chip.state, (P, P), B * S, 1e-5)


def layer2_attention(chip, a):
    pre, virtual = "L2_attn_", 16
    at = Attention(chip, 32, 16, NT + 1, 32 ** -0.5, "ahead", virtual)
    cos, sin = chip.tables(32)
    fill_slots_stage(chip, at)
    load_stage(chip, [(cos, a["rope_l2_cos"].rearrange("p (t e) -> p t e", t=NT)),
                      (sin, a["rope_l2_sin"].rearrange("p (t e) -> p t e", t=NT)),
                      (chip.masks[:, :], a["mask_ahead"]),
                      (chip.w_out[:, 0:4, :], fm(a[pre + "W_O_flat"]))])
    masks = (chip.masks[:, 0:256], chip.masks[:, 256:512])
    for b in range(B):
        with chip.nc.Fori(0, 4) as g:
            virtual_k = at.k[0:virtual, NT].rearrange("p b (h w) -> p (b h) w",
                                                      w=at.slot)[:, :, 0:32]
            loads = [
                (chip.w_in[:, :, 0:640], a[pre + "W_groups"][bass.ds(g, 1)].rearrange(
                    "o (c p) n -> p (o c) n", p=P)),
                (chip.w_bias[:, 0:640], a[pre + "b_groups"][bass.ds(g, 1)]),
                (virtual_k, a[pre + "virtual_k"][:, bass.ds(g * 8, 8), :]),
                (at.v[0:virtual, NT, :, 0:16], a[pre + "virtual_v"].rearrange(
                    "k (h e) o -> k h (e o)", e=16)[:, bass.ds(g * 8, 8), :])]
            jobs = []
            for t in range(NT):
                tok = slice(b * S + t * P, b * S + (t + 1) * P)
                products = []
                for lo, hi in ((0, BANK), (BANK, 640)):
                    products += [(chip.state[:, c, tok], chip.w_in[:, c, lo:hi], lo, c == 0,
                                  False) for c in range(2)]
                    products.append((chip.ones[:, 0:P], chip.w_bias[:, lo:hi], lo, False, True))
                jobs.append((products, [
                    (at.raw_q[:, t * D:(t + 1) * D], lambda ps: ps[:, 0:D]),
                    (at.raw_k[:, t * D:(t + 1) * D], lambda ps: ps[:, D:2 * D]),
                    (at.v[:, t, :, 0:16], lambda ps: ps[:, 2 * D:2 * D + P].rearrange(
                        "p (h e) -> p h e", e=16))]))
            q_post = HeadPost(chip, at, at.raw_q, at.q, NT, 8, None, None, cos, sin)
            k_post = HeadPost(chip, at, at.raw_k, at.k, NT, 8, None, None, cos, sin)
            project_stage(chip, at, loads, jobs, q_post, k_post)
            attention_core(chip, at, g * P, masks)
        out_stages(chip, at, b, 512, [], None, chip.state, chip.inner)
    norm_stage(chip, chip.inner, chip.state, (P, P), B * S, 1e-5)


def layer2_cross(chip, a):
    pre = "L2_xattn_"
    tiles = SC // P + NT
    g = chip.gains
    norm_stage(chip, chip.ctx, chip.ctx, (P, DC - P), B * SC, 1e-5, gain=g[:, 0:2],
               shift=g[:, 2:4], loads=[(g[:, 0:2], a[pre + "ln_x_g_col"]),
                                       (g[:, 2:4], a[pre + "ln_x_b_col"])])
    at = Attention(chip, 64, 64, tiles, 1.0)
    bo, q_gain, k_gain = g[:, 0:2], g[:, 6:70], g[:, 70:134]
    key_cols = g[:, 134:146]
    fill_slots_stage(chip, at)
    norm_stage(chip, chip.state, chip.normed, (P, P), B * S, 1e-5, gain=g[:, 2:4],
               shift=g[:, 4:6], loads=[(g[:, 2:4], a[pre + "ln_l_g_col"]),
                                       (g[:, 4:6], a[pre + "ln_l_b_col"])])
    fill_slots_stage(chip, at)
    w_ctx = chip.w_out[:, 4:8, :].rearrange("p a b -> p (a b)").rearrange("p (c n) -> p c n", c=2)
    load_stage(chip, [(chip.w_in[:, :, 0:D], fm(a[pre + "Wq_t"])),
                      (chip.w_in[:, :, D:3 * D], fm(a[pre + "Wlkv_t"])),
                      (chip.w_out[:, 0:2, :], fm(a[pre + "Wo_t"])),
                      (bo, a[pre + "bo_col"]),
                      (q_gain, a[pre + "qn_g"].unsqueeze(0).partition_broadcast(P)),
                      (k_gain, a[pre + "kn_g"].unsqueeze(0).partition_broadcast(P)),
                      (chip.mask_row[:, :], a["mask_row"].unsqueeze(0)),
                      (chip.mask_cols[:, :], a["mask_cols"])] + ctx_loads(w_ctx, a[pre + "Wkv_t"]))
    nc = chip.nc

    def key_bias_stage(b):
        sig = chip.stage("small")
        with nc.Block() as block:
            @block.gpsimd
            def _(pool):
                chip.reset_others(pool, sig)

            @block.vector
            def _(dve):
                order = Order(dve, sig["order"])
                dve.memset(key_cols[:, 8:12], 0.0)
                dve.tensor_scalar(key_cols[:, 0:8], chip.mask_cols[:, b * 8:(b + 1) * 8], BIG,
                                  -BIG, ALU.mult, ALU.add)
                order(dve.tensor_scalar(chip.w_bias[:, :], chip.mask_row[:, b * SC:(b + 1) * SC],
                                        BIG, -BIG, ALU.mult, ALU.add))

    for b in range(B):
        key_bias_stage(b)
        for part in range(3):
            jobs = []
            for t in range(NT):
                if part < 2:
                    tok = slice(b * SC + (part * NT + t) * P, b * SC + (part * NT + t + 1) * P)
                    products = [(chip.ctx[:r, c, tok], w_ctx[:r, c], 0, c == 0, c == 1)
                                for c, r in ((0, P), (1, DC - P))]
                else:
                    tok = slice(b * S + t * P, b * S + (t + 1) * P)
                    products = [(chip.normed[:, c, tok], chip.w_in[:, c, D:3 * D], 0, c == 0,
                                 c == 1) for c in range(2)]
                    products += [(chip.normed[:, c, tok], chip.w_in[:, c, 0:D], BANK, c == 0,
                                  c == 1) for c in range(2)]
                copies = [(at.raw_k[:, t * D:(t + 1) * D], lambda ps: ps[:, 0:D]),
                          (at.v[:, part * NT + t, :, 0:64], lambda ps: ps[:, D:2 * D].rearrange(
                              "p (h e) -> p h e", e=64))]
                if part == 2:
                    copies.append((at.raw_q[:, t * D:(t + 1) * D],
                                   lambda ps: ps[:, BANK:BANK + D]))
                jobs.append((products, copies))
            q_post = HeadPost(chip, at, at.raw_q, at.q, NT, 4, (1.0 / 64, 0.0, 1e-8, 0.125),
                              q_gain) if part == 2 else None
            k_post = HeadPost(chip, at, at.raw_k, at.k[:, part * NT:(part + 1) * NT], NT, 4,
                              (1.0 / 64, 0.0, 1e-8, 1.0), k_gain)
            project_stage(chip, at, [], jobs, q_post, k_post)
        attention_core(chip, at, 0, None, chip.w_bias, key_cols)
        out_stages(chip, at, b, D, [], bo, chip.state, chip.inner)
    norm_stage(chip, chip.inner, chip.state, (P, P), B * S, 1e-5)
    load_stage(chip, ctx_loads(chip.ctx, a["ctx_fm"]))


def rank_steps(order, dve, values, work, work2, ties, rank, n):
    tiles = B * NT
    for t in range(tiles):
        v = values[:, t]
        mine = v.unsqueeze(2).to_broadcast([P, n, n])
        other = v.unsqueeze(1).to_broadcast([P, n, n])
        w = work[:, t * n * n:(t + 1) * n * n].rearrange("p (i j) -> p i j", j=n)
        w2 = work2[:, t * n * n:(t + 1) * n * n].rearrange("p (i j) -> p i j", j=n)
        dve.tensor_tensor(w, other, mine, ALU.is_gt)
        ins = dve.tensor_tensor(w2, other, mine, ALU.is_equal)
    order(ins)
    m = tiles * n * n
    tie = ties.unsqueeze(1).to_broadcast([P, tiles, n * n])
    order(dve.tensor_tensor(work2[:, :m].rearrange("p (t e) -> p t e", t=tiles),
                            work2[:, :m].rearrange("p (t e) -> p t e", t=tiles), tie, ALU.mult))
    order(dve.tensor_tensor(work[:, :m], work[:, :m], work2[:, :m], ALU.add))
    order(dve.tensor_reduce(rank, work[:, :m].rearrange("p (t j) -> p t j", j=n), AX, ALU.add))


def router_logits_stage(chip, logits, router, loads, n):
    nc, sig = chip.nc, chip.stage("small")
    with nc.Block() as block:
        @block.gpsimd
        def _(pool):
            chip.reset_others(pool, sig)

        @block.sync
        def _(sp):
            for dst, src in loads:
                sp.dma_start(dst, src).then_inc(sig["weights_loaded"], 16)

        @block.tensor
        def _(pe):
            pe.wait_ge(sig["weights_loaded"], 16 * len(loads))
            for t in range(B * NT):
                for c in range(2):
                    mm = pe.matmul(chip.psum[:, 0, t * n:(t + 1) * n],
                                   chip.state[:, c, t * P:(t + 1) * P], router[:, c],
                                   start=c == 0, stop=c == 1)
            mm.then_inc(sig["pe_done"], 1)

        @block.vector
        def _(dve):
            dve.wait_ge(sig["pe_done"], 1)
            dve.tensor_copy(logits, chip.psum[:, 0, 0:B * NT * n].rearrange(
                "p (t e) -> p t e", e=n)).then_inc(sig["dve_done"], 1)


def turn_combine(chip, combine, combine_t, n):
    turn_stage(chip, [([(combine[:, 4 * q + t, :], t * P) for t in range(4)],
                       combine_t[:n, q * BANK:(q + 1) * BANK]) for q in range(2)])


def layer2_ffn(chip, a):
    pre, n, groups, tiles = "L2_ffn_", 16, 4, B * NT
    router = chip.carve(8192, 2, n)
    logits, scores, biased = (chip.carve(8224 + i * tiles * n, tiles, n) for i in range(3))
    bias = chip.carve(8608, n)
    ties = chip.carve(8624, n * n)
    ties4 = chip.carve(8880, groups * groups)
    sel = chip.carve(8896, 12, P)
    combine = chip.carve(10432, tiles, n + 1)
    combine_t = chip.carve(10568, B * S)
    group_score, group_rank = (chip.carve(11592 + 32 * i, tiles, groups) for i in range(2))
    pair = chip.carve(11656, tiles * groups)
    rank = chip.carve(11688, tiles * n)
    work, work2 = chip.carve(11816, 2048), chip.carve(13864, 2048)
    total = chip.carve(15912, tiles, 1)
    router_logits_stage(chip, logits, router, [
        (router, fm(a[pre + "router_w_t"])),
        (bias, a[pre + "correction_bias"].unsqueeze(0).partition_broadcast(P)),
        (ties, a["ties16"].partition_broadcast(P)), (ties4, a["ties4"].partition_broadcast(P)),
        (sel[:n + 1], a["sel_l2"])], n)
    nc, sig = chip.nc, chip.stage("route")
    with nc.Block() as block:
        @block.gpsimd
        def _(pool):
            chip.reset_others(pool, sig)

        @block.scalar
        def _(act):
            act.activation(scores, logits, ACT.Sigmoid).then_inc(sig["scores_ready"], 1)

        @block.vector
        def _(dve):
            order = Order(dve, sig["order"])
            dve.wait_ge(sig["scores_ready"], 1)
            order(dve.tensor_tensor(biased, scores,
                                    bias.unsqueeze(1).to_broadcast([P, tiles, n]), ALU.add))
            quads = biased.rearrange("p t (g e) -> p (t g) e", e=4)
            best = group_score.rearrange("p t g -> p (t g)").unsqueeze(2)
            one = pair.unsqueeze(2)
            order(dve.tensor_tensor(best, quads[:, :, 0:1], quads[:, :, 1:2], ALU.add))
            for i, j in ((0, 2), (0, 3), (1, 2), (1, 3), (2, 3)):
                order(dve.tensor_tensor(one, quads[:, :, i:i + 1], quads[:, :, j:j + 1], ALU.add))
                order(dve.tensor_tensor(best, best, one, ALU.max))
            rank_steps(order, dve, group_score, work, work2, ties4,
                       group_rank.rearrange("p t g -> p (t g)"), groups)
            order(dve.tensor_scalar(group_rank, group_rank, 2.0, -BIG, ALU.is_ge, ALU.mult))
            order(dve.tensor_tensor(quads, quads, group_rank.rearrange(
                "p t g -> p (t g)").unsqueeze(2).to_broadcast([P, tiles * groups, 4]), ALU.add))
            rank_steps(order, dve, biased, work, work2, ties, rank, n)
            order(dve.tensor_scalar(rank, rank, 4.0, None, ALU.is_lt))
            dve.memset(combine[:, :, n:n + 1], 1.0)
            order(dve.tensor_tensor(logits, scores, rank.rearrange("p (t e) -> p t e", e=n),
                                    ALU.mult))
            order(dve.tensor_reduce(total, logits, AX, ALU.add))
            order(dve.tensor_scalar(total, total, 1e-20, None, ALU.add))
            order(dve.reciprocal(total, total))
            order(dve.tensor_tensor(combine[:, :, 0:n], logits, total.to_broadcast([P, tiles, n]),
                                    ALU.mult))
    turn_combine(chip, combine, combine_t, n + 1)
    expert_stage(chip, a, pre, 12, lambda f, cols: (sel[:n + 1, f], combine_t[:n + 1, cols]),
                 chip.state)
    norm_stage(chip, chip.inner, chip.state, (P, P), B * S, 1e-5)


def expert_stage(chip, a, pre, tiles, spread, addend):
    gate_up, down = a[pre + "gate_up_tiles"], a[pre + "down_tiles"]

    def tile(f):
        def loads(to_gate_up, to_down):
            return [(to_gate_up, fm(gate_up[f])), (to_down, down[f])]
        return P, loads

    gated_stage(chip, chip.state, [tile(f) for f in range(tiles)], ACT.Silu, chip.inner, addend,
                spread=spread)


def layer3_attention(chip, a):
    pre = "L3_attn_"
    at = Attention(chip, 16, 16, NT, 0.25, "band")
    cos, sin = chip.tables(16)
    fill_slots_stage(chip, at)
    load_stage(chip, [(cos, a["rope_l3_cos"].rearrange("p (t e) -> p t e", t=NT)),
                      (sin, a["rope_l3_sin"].rearrange("p (t e) -> p t e", t=NT)),
                      (chip.masks[:, :], a["mask_band128"]),
                      (chip.w_in[:, :, :], fm(a[pre + "Wqkv"])),
                      (chip.w_out[:, 0:2, :], fm(a[pre + "Wout"]))])
    masks = (chip.masks[:, 0:256], chip.masks[:, 256:512])
    for b in range(B):
        jobs = []
        for t in range(NT):
            tok = slice(b * S + t * P, b * S + (t + 1) * P)
            products = []
            for lo, hi in ((0, BANK), (BANK, 3 * D)):
                products += [(chip.state[:, c, tok], chip.w_in[:, c, lo:hi], lo, c == 0, c == 1)
                             for c in range(2)]
            jobs.append((products, [
                (at.raw_q[:, t * D:(t + 1) * D], lambda ps: ps[:, 0:D]),
                (at.raw_k[:, t * D:(t + 1) * D], lambda ps: ps[:, D:2 * D]),
                (at.v[:, t, :, 0:16], lambda ps: ps[:, 2 * D:3 * D].rearrange(
                    "p (h e) -> p h e", e=16))]))
        q_post = HeadPost(chip, at, at.raw_q, at.q, NT, 16, None, None, cos, sin)
        k_post = HeadPost(chip, at, at.raw_k, at.k, NT, 16, None, None, cos, sin)
        project_stage(chip, at, [], jobs, q_post, k_post)
        attention_core(chip, at, 0, masks)
        out_stages(chip, at, b, D, [], None, chip.state, chip.inner)
    norm_stage(chip, chip.inner, chip.state, (P, P), B * S, 1e-5)


def layer3_cross(chip, a):
    cross_attention(chip, a, "L3_xattn_", 16, True, clip=40000.0)


def layer3_ffn(chip, a):
    pre, n, real, tiles = "L3_ffn_", 40, 32, B * NT
    router = chip.carve(8192, 2, n)
    logits, scores, biased = (chip.carve(8272 + i * tiles * n, tiles, n) for i in range(3))
    bias = chip.carve(9232, n)
    total = chip.carve(9272, tiles, 1)
    rank = chip.carve(9280, tiles * n)
    combine_t = chip.carve(9600, B * S)
    sel = chip.carve(10624, real + 1, P)
    ties = chip.carve(14848, n * n)
    router_logits_stage(chip, logits, router, [
        (router, fm(a[pre + "classifier_weight_t"])),
        (bias, a[pre + "e_score_correction_bias"].unsqueeze(0).partition_broadcast(P)),
        (ties, a["ties40"].partition_broadcast(P)), (sel[:n], a["sel_l3"])], n)
    nc, sig = chip.nc, chip.stage("route")
    larger, equal = chip.carve(16448, n * n), chip.carve(18048, n * n)
    with nc.Block() as block:
        @block.gpsimd
        def _(pool):
            chip.reset_others(pool, sig)

        @block.scalar
        def _(act):
            act.wait_ge(sig["shifted_ready"], 1)
            act.activation(scores, logits, ACT.Exp).then_inc(sig["scores_ready"], 1)

        @block.vector
        def _(dve):
            order = Order(dve, sig["order"])
            order(dve.tensor_reduce(total, logits, AX, ALU.max))
            dve.tensor_tensor(logits, logits, total.to_broadcast([P, tiles, n]),
                              ALU.subtract).then_inc(sig["shifted_ready"], 1)
            dve.wait_ge(sig["scores_ready"], 1)
            order(dve.tensor_reduce(total, scores, AX, ALU.add))
            order(dve.reciprocal(total, total))
            order(dve.tensor_tensor(scores, scores, total.to_broadcast([P, tiles, n]), ALU.mult))
            order(dve.tensor_tensor(biased, scores,
                                    bias.unsqueeze(1).to_broadcast([P, tiles, n]), ALU.add))
            for t in range(tiles):
                v = biased[:, t]
                mine = v.unsqueeze(2).to_broadcast([P, n, n])
                other = v.unsqueeze(1).to_broadcast([P, n, n])
                dve.tensor_tensor(larger.rearrange("p (i j) -> p i j", j=n), other, mine,
                                  ALU.is_gt)
                order(dve.tensor_tensor(equal.rearrange("p (i j) -> p i j", j=n), other, mine,
                                        ALU.is_equal))
                order(dve.tensor_tensor(equal, equal, ties, ALU.mult))
                order(dve.tensor_tensor(larger, larger, equal, ALU.add))
                order(dve.tensor_reduce(rank[:, t * n:(t + 1) * n],
                                        larger.rearrange("p (i j) -> p i j", j=n), AX, ALU.add))
            order(dve.tensor_scalar(rank, rank, 6.0, 2.5, ALU.is_lt, ALU.mult))
            order(dve.tensor_tensor(biased, scores, rank.rearrange("p (t e) -> p t e", e=n),
                                    ALU.mult))
    turn_combine(chip, biased, combine_t, n)
    sig = chip.stage("small")
    with nc.Block() as block:
        @block.gpsimd
        def _(pool):
            chip.reset_others(pool, sig)

        @block.tensor
        def _(pe):
            for h in range(2):
                mm = pe.matmul(chip.psum[:, h], sel[:n, real],
                               combine_t[:n, h * BANK:(h + 1) * BANK], start=True, stop=True)
            mm.then_inc(sig["pe_done"], 1)

        @block.vector
        def _(dve):
            dve.wait_ge(sig["pe_done"], 1)
            for m in range(2):
                for h in range(2):
                    cols = slice(h * BANK, (h + 1) * BANK)
                    dve.scalar_tensor_tensor(chip.normed[:, m, cols], chip.psum[:, h], 1.0,
                                             chip.state[:, m, cols], ALU.add,
                                             ALU.mult).then_inc(sig["dve_done"], 1)
    expert_stage(chip, a, pre, real, lambda f, cols: (sel[:n, f], combine_t[:n, cols]),
                 chip.normed)
    norm_stage(chip, chip.inner, chip.state, (P, P), B * S, 1e-5)


LAYERS = [layer0_attention, layer0_cross, layer0_ffn, layer1_linear_attention, layer1_cross,
          layer1_ffn, layer2_attention, layer2_cross, layer2_ffn, layer3_attention, layer3_cross,
          layer3_ffn]


COLUMNS = ("w", "g", "b", "bo", "b2")


def host_arrays(inputs):
    import numpy as np
    lay = np.ascontiguousarray
    a = {n: lay(v) for n, v in inputs.items() if n not in ("x", "ctx_768", "mask_BxS2_bk0")}
    a["x_fm"] = lay(inputs["x"].reshape(B * S, D).T)
    a["ctx_fm"] = lay(inputs["ctx_768"].reshape(B * SC, DC).T)
    for n, v in inputs.items():
        if n.split("_")[-1] in COLUMNS and v.shape[-1] == D:
            v = v.reshape(-1, 2, P).transpose(2, 0, 1)
            a[n + "_col"] = lay(v.reshape(P, -1))
    w = inputs["L0_ffn_Wqkv"].reshape(6, D, 3, 4, D).transpose(0, 3, 1, 2, 4)
    a["L0_ffn_Wqkv_groups"] = lay(w.reshape(24, D, 3 * D))
    b1 = inputs["L0_ffn_b1"].reshape(6, 2, 682)
    b1 = np.concatenate([b1, np.zeros((6, 2, 768 - 682), b1.dtype)], -1)
    a["L0_ffn_b1_col"] = lay(b1.reshape(6 * 12, P).T)
    for n in ("L1_attn_Wq", "L1_attn_Wk", "L1_attn_Wv", "L1_attn_Wo", "L2_xattn_Wq",
              "L2_xattn_Wlkv", "L2_xattn_Wkv", "L2_xattn_Wo", "L2_ffn_router_w",
              "L3_ffn_classifier_weight"):
        a[n + "_t"] = lay(inputs[n].T)
    proj = inputs["L1_attn_proj"]
    diag = np.zeros((2, 8, 16, 8, 64), proj.dtype)
    for h in range(16):
        diag[h // 8, h % 8, :, h % 8, :] = proj[h].T
    a["L1_attn_proj_diag"] = diag.reshape(2, P, 512)
    pre = "L2_attn_"
    w_q, w_k = (inputs[pre + n].transpose(1, 0, 2).reshape(D, 4, D) for n in ("W_Q", "W_K"))
    w_v = inputs[pre + "W_V"].reshape(4, P, D).transpose(2, 0, 1)
    a[pre + "W_groups"] = lay(np.concatenate([w_q, w_k, w_v], 2).transpose(1, 0, 2))
    a[pre + "b_groups"] = lay(np.concatenate(
        [inputs[pre + "b_Q"].reshape(4, D), inputs[pre + "b_K"].reshape(4, D),
         inputs[pre + "b_V"].reshape(4, P)], 1))
    a[pre + "W_O_flat"] = lay(inputs[pre + "W_O"].reshape(512, D))
    for n in ("ln_x_g", "ln_x_b"):
        v = inputs["L2_xattn_" + n]
        a[f"L2_xattn_{n}_col"] = lay(np.concatenate([v, v[:D - DC]]).reshape(2, P).T)
    mask = inputs["mask_BxS2_bk0"]
    a["mask_row"] = lay(mask.reshape(-1))
    a["mask_cols"] = lay(mask.reshape(B * SC // P, P).T)
    pre = "L2_ffn_"
    routed = [inputs[pre + n].reshape(8, 2, D, 64).transpose(0, 2, 1, 3).reshape(8, D, P)
              for n in ("gate_w", "up_w")]
    shared = [inputs[pre + n].reshape(4, P, D).transpose(0, 2, 1)
              for n in ("shared_gate_w", "shared_up_w")]
    a[pre + "gate_up_tiles"] = lay(np.concatenate(
        [np.concatenate(routed, 2), np.concatenate(shared, 2)], 0))
    a[pre + "down_tiles"] = lay(np.concatenate(
        [inputs[pre + "down_w"].reshape(8, P, D),
         inputs[pre + "shared_down_w"].T.reshape(4, P, D)], 0))
    a["L3_ffn_gate_up_tiles"] = lay(inputs["L3_ffn_gate_up_proj"][:32].transpose(0, 2, 1))
    a["L3_ffn_down_tiles"] = lay(inputs["L3_ffn_down_proj"].transpose(0, 2, 1))
    a.update(constants())
    return a


def kernel(**inputs):
    import concourse.bacc as bacc
    from concourse.bass_utils import run_bass_kernel_spmd

    arrays = host_arrays(inputs)
    nc = bacc.Bacc("TRN2", target_bir_lowering=False, num_devices=1)
    a = {n: nc.dram_tensor("in_" + n, v.shape, mybir.dt.from_np(v.dtype),
                           kind="ExternalInput").ap() for n, v in arrays.items()}
    out = nc.dram_tensor("out_fm", (D, B * S), F32, kind="ExternalOutput").ap()
    build(nc, a, out)
    r = run_bass_kernel_spmd(nc, [{"in_" + n: v for n, v in arrays.items()}], core_ids=[0])
    import numpy as np
    return np.ascontiguousarray(r.results[0]["out_fm"].T).reshape(B, S, D)
```

```python
import concourse.bass as bass
from concourse import mybir
from concourse.alu_op_type import AluOpType as ALU

F32 = mybir.dt.float32
BF16 = mybir.dt.bfloat16
U8 = mybir.dt.uint8
ACT = mybir.ActivationFunctionType
AX = mybir.AxisListType.X

P = 128
B, S, D = 2, 512, 256
SC, DC = 1024, 192
NT = S // P
BANK = 512
BIG = 1.0e30
CLIP = 10000.0

STAGES = {
    "start": ["inputs_loaded", "constants_set"],
    "norm": ["gains_loaded", "summed", "mean_ready", "centered", "squared", "var_ready", "var_kept",
             "root_ready", "order"],
    "linear": ["weights_loaded", "product_ready", "product_used"],
    "project": ["weights_loaded", "product_ready", "product_kept", "sums_ready", "roots_ready", "order"],
    "turn": ["turned", "kept_by_dve", "kept_by_act"],
    "split": ["part_ready", "repeated", "order"],
    "attend": ["shift_cleared", "turned", "turn_kept", "scores_ready", "max_taken",
               "shift_ready", "shifted_ready", "exp_ready", "probs_ready", "values_ready",
               "group_kept", "sums_spread", "heads_kept", "order"],
    "gated": ["bias_loaded", "slot0_loaded", "slot1_loaded", "slot2_loaded", "slot3_loaded",
              "gate_ready", "up_ready", "gate_acted", "hidden_ready", "tile_done", "sum_ready",
              "order"],
    "features": ["cleared", "squares_ready", "logits_ready", "shifted_ready", "exp_ready",
                 "phi_ready", "order"],
    "quantize": ["row_max", "all_max", "sigmoid_ready", "order"],
    "route": ["shifted_ready", "scores_ready", "order"],
    "small": ["weights_loaded", "pe_done", "act_done", "dve_done", "pool_done", "order"],
}


class Signals:

    def __init__(self, nc, names, stage):
        self.of = {n: nc.alloc_semaphore(f"{stage}_{n}") for n in names}
        nums = [s.num for s in self.of.values()]
        self.lo, self.hi = min(nums), max(nums) + 1

    def __getitem__(self, name):
        return self.of[name]


class Order:

    def __init__(self, eng, sem):
        self.eng, self.sem, self.n = eng, sem, 0

    def __call__(self, ins):
        self.n += 1
        ins.then_inc(self.sem, 1)
        self.eng.wait_ge(self.sem, self.n)


class Chip:

    def __init__(self, nc):
        self.nc = nc
        self.signals = {k: Signals(nc, v, k) for k, v in STAGES.items()}
        self.lo = min(s.lo for s in self.signals.values())
        self.hi = max(s.hi for s in self.signals.values())
        self.last = None
        self.psum = nc.alloc_psum_tensor("psum", [P, 8, BANK], F32)
        sb = nc.alloc_sbuf_tensor
        self.state = sb("state", [P, 2, B * S], F32)
        self.inner = sb("inner", [P, 2, B * S], F32)
        self.normed = sb("normed", [P, 2, B * S], F32)
        self.ctx = sb("ctx", [P, 2, B * SC], F32)
        self.ident = sb("ident", [P, P], F32)
        self.ident_bf = sb("ident_bf", [P, P], BF16)
        self.mean_w = sb("mean_w", [P, 2, P], F32)
        self.ones = sb("ones", [1, P], F32)
        self.masks = sb("masks", [P, 2 * 256], BF16)
        self.w_in = sb("w_in", [P, 2, 768], F32)
        self.w_bias = sb("w_bias", [1, SC], F32)
        self.virtual_k = sb("virtual_k", [16, D], F32)
        self.w_out = sb("w_out", [P, 8, D], F32)
        self.cols = sb("cols", [P, 64], F32)
        self.roots = sb("roots", [P, 64], F32)
        self.pick_sum = sb("pick_sum", [P, P], F32)
        self.pick_shift = sb("pick_shift", [P, P], BF16)
        self.clip_col = sb("clip_col", [P, 1], F32)
        self.gains = sb("gains", [P, 160], F32)
        self.mask_cols = sb("mask_cols", [P, B * SC // P], U8)
        self.table_mem = sb("table_mem", [P, 4 * NT * 64], F32)
        self.arena = sb("arena", [P, 35712], F32)

    def carve(self, at, *shape):
        n = 1
        for s in shape:
            n *= s
        assert at + n <= self.arena.shape[1], (at, n)
        v = self.arena[:, at:at + n]
        if len(shape) == 1:
            return v
        if len(shape) == 2:
            return v.rearrange("p (a b) -> p a b", b=shape[1])
        return v.rearrange("p (a b c) -> p a b c", b=shape[1], c=shape[2])

    def tables(self, hd, n=0):
        at = n * 2 * NT * 64
        return [self.table_mem[:, at + i * NT * hd:at + (i + 1) * NT * hd].rearrange(
            "p (t e) -> p t e", e=hd) for i in range(2)]

    def stage(self, kind):
        if self.last == kind:
            with self.nc.Block() as block:
                @block.gpsimd
                def _(pool):
                    pool.sem_clear(range(self.lo, self.hi))
        self.last = kind
        return self.signals[kind]

    def reset_others(self, pool, own):
        if own.lo > self.lo:
            pool.sem_clear(range(self.lo, own.lo))
        if own.hi < self.hi:
            pool.sem_clear(range(own.hi, self.hi))


def start_stage(chip, loads):
    nc, sig = chip.nc, chip.stage("start")
    with nc.Block() as block:
        @block.sync
        def _(sp):
            for dst, src in loads:
                sp.dma_start(dst, src).then_inc(sig["inputs_loaded"], 16)
            sp.wait_ge(sig["inputs_loaded"], 16 * len(loads))

        @block.vector
        def _(dve):
            dve.memset(chip.ones[:, :], 1.0)
            dve.memset(chip.clip_col[:, :], -CLIP)
            dve.memset(chip.mean_w[:, 0, :], 1.0 / D)
            dve.memset(chip.mean_w[:, 1, :], 1.0 / DC).then_inc(sig["constants_set"], 1)
            dve.wait_ge(sig["constants_set"], 1)


def load_stage(chip, loads):
    nc, sig = chip.nc, chip.stage("start")
    with nc.Block() as block:
        @block.gpsimd
        def _(pool):
            chip.reset_others(pool, sig)

        @block.sync
        def _(sp):
            for dst, src in loads:
                sp.dma_start(dst, src).then_inc(sig["inputs_loaded"], 16)
            sp.wait_ge(sig["inputs_loaded"], 16 * len(loads))


def norm_stage(chip, src, dst, sizes, width, eps, center=True, gain=None, shift=None, add=None,
               loads=()):
    nc, sig = chip.nc, chip.stage("norm")
    halves = width // BANK
    mean_w = chip.mean_w[:, 0 if sum(sizes) == D else 1, :]
    work = chip.carve(0, 2, 2, BANK)
    centred = chip.carve(2048, 2, 2, BANK)
    squares = chip.carve(4096, 2, 2, BANK)
    spread = chip.carve(6144, 2, BANK)
    root = chip.carve(7168, 2, BANK)
    mean_ps, var_ps = chip.psum[:, 0:2, :], chip.psum[:, 2:4, :]
    chunks = list(enumerate(sizes))
    with nc.Block() as block:
        @block.gpsimd
        def _(pool):
            chip.reset_others(pool, sig)

        @block.sync
        def _(sp):
            for to, frm in loads:
                sp.dma_start(to, frm).then_inc(sig["gains_loaded"], 16)

        @block.vector
        def _(dve):
            order = Order(dve, sig["order"])

            def begin(h):
                n, cols = h % 2, slice(h * BANK, (h + 1) * BANK)
                if h >= 2:
                    dve.wait_ge(sig["squared"], h - 1)
                for c, rows in chunks:
                    if add is not None:
                        ins = dve.tensor_tensor(work[:rows, n, c], src[:rows, c, cols],
                                                add[:rows, c, cols], ALU.add)
                    else:
                        ins = dve.tensor_copy(work[:rows, n, c], src[:rows, c, cols])
                    ins.then_inc(sig["summed"], 1)
                if center:
                    dve.wait_ge(sig["mean_ready"], h + 1)
                dve.wait_ge(sig["summed"], 2 * h + 2)
                for c, rows in chunks:
                    if center:
                        ins = dve.tensor_tensor(centred[:rows, n, c], work[:rows, n, c],
                                                mean_ps[:rows, n], ALU.subtract)
                    else:
                        ins = dve.tensor_copy(centred[:rows, n, c], work[:rows, n, c])
                    ins.then_inc(sig["centered"], 1)

            def end(h):
                n = h % 2
                dve.wait_ge(sig["var_ready"], h + 1)
                dve.tensor_scalar(spread[:, n], var_ps[:, n], eps, None,
                                  ALU.add).then_inc(sig["var_kept"], 1)
                dve.wait_ge(sig["root_ready"], h + 1)
                order(dve.reciprocal(spread[:, n], root[:, n]))
                for c, rows in chunks:
                    out = dst[:rows, c, h * BANK:(h + 1) * BANK]
                    order(dve.tensor_tensor(out, centred[:rows, n, c], spread[:rows, n], ALU.mult))
                    if gain is not None and shift is None:
                        order(dve.tensor_scalar(out, out, gain[:rows, c:c + 1], None, ALU.mult))
                    elif gain is not None:
                        order(dve.tensor_scalar(out, out, gain[:rows, c:c + 1],
                                                shift[:rows, c:c + 1], ALU.mult, ALU.add))

            if loads:
                dve.wait_ge(sig["gains_loaded"], 16 * len(loads))
            begin(0)
            for h in range(halves):
                if h + 1 < halves:
                    begin(h + 1)
                end(h)

        @block.scalar
        def _(act):
            for h in range(halves):
                n = h % 2
                act.wait_ge(sig["centered"], 2 * h + 2)
                if h >= 2:
                    act.wait_ge(sig["var_ready"], h - 1)
                for c, rows in chunks:
                    ins = act.activation(squares[:rows, n, c], centred[:rows, n, c], ACT.Square)
                ins.then_inc(sig["squared"], 1)
                act.wait_ge(sig["var_kept"], h + 1)
                act.activation(root[:, n], spread[:, n], ACT.Sqrt).then_inc(sig["root_ready"], 1)

        @block.tensor
        def _(pe):
            def mean(h):
                if not center:
                    return
                n = h % 2
                pe.wait_ge(sig["summed"], 2 * h + 2)
                if h >= 2:
                    pe.wait_ge(sig["centered"], 2 * (h - 1))
                for c, rows in chunks:
                    mm = pe.matmul(mean_ps[:, n], mean_w[:rows, :], work[:rows, n, c],
                                   start=c == 0, stop=c == 1)
                mm.then_inc(sig["mean_ready"], 1)

            mean(0)
            for h in range(halves):
                if h + 1 < halves:
                    mean(h + 1)
                n = h % 2
                pe.wait_ge(sig["squared"], h + 1)
                if h >= 2:
                    pe.wait_ge(sig["var_kept"], h - 1)
                for c, rows in chunks:
                    mm = pe.matmul(var_ps[:, n], mean_w[:rows, :], squares[:rows, n, c],
                                   start=c == 0, stop=c == 1)
                mm.then_inc(sig["var_ready"], 1)


def linear_stage(chip, loads, jobs):
    nc, sig = chip.nc, chip.stage("linear")
    with nc.Block() as block:
        @block.gpsimd
        def _(pool):
            chip.reset_others(pool, sig)

        @block.sync
        def _(sp):
            for dst, src in loads:
                sp.dma_start(dst, src).then_inc(sig["weights_loaded"], 16)

        @block.tensor
        def _(pe):
            if loads:
                pe.wait_ge(sig["weights_loaded"], 16 * len(loads))
            for j, (out, pairs, bias, addend) in enumerate(jobs):
                if j >= 8:
                    pe.wait_ge(sig["product_used"], j - 7)
                rows, cols = out.shape
                for i, (lhs, rhs) in enumerate(pairs):
                    mm = pe.matmul(chip.psum[:rows, j % 8, :cols], lhs, rhs, start=i == 0,
                                   stop=i == len(pairs) - 1)
                mm.then_inc(sig["product_ready"], 1)

        @block.vector
        def _(dve):
            if loads:
                dve.wait_ge(sig["weights_loaded"], 16 * len(loads))
            for j, (out, pairs, bias, addend) in enumerate(jobs):
                rows, cols = out.shape
                made = chip.psum[:rows, j % 8, :cols]
                dve.wait_ge(sig["product_ready"], j + 1)
                if addend is not None and bias is not None:
                    ins = dve.scalar_tensor_tensor(out, made, bias, addend, ALU.add, ALU.add)
                elif addend is not None:
                    ins = dve.tensor_tensor(out, made, addend, ALU.add)
                elif bias is not None:
                    ins = dve.tensor_scalar(out, made, bias, None, ALU.add)
                else:
                    ins = dve.tensor_copy(out, made)
                ins.then_inc(sig["product_used"], 1)


def turn_stage(chip, groups):
    nc, sig = chip.nc, chip.stage("turn")

    def kept(eng, g):
        eng.wait_ge(sig["kept_by_act" if g % 2 else "kept_by_dve"], g // 2 + 1)

    with nc.Block() as block:
        @block.gpsimd
        def _(pool):
            chip.reset_others(pool, sig)

        @block.tensor
        def _(pe):
            for g, (parts, dst) in enumerate(groups):
                if g >= 8:
                    kept(pe, g - 8)
                for src, at in parts:
                    rows, cols = src.shape
                    mm = pe.transpose(chip.psum[:cols, g % 8, at:at + rows], src,
                                      chip.ident[:rows, :rows])
                mm.then_inc(sig["turned"], 1)

        @block.vector
        def _(dve):
            for g, (parts, dst) in enumerate(groups):
                if g % 2 == 0:
                    dve.wait_ge(sig["turned"], g + 1)
                    dve.tensor_copy(dst, chip.psum[:dst.shape[0], g % 8, :dst.shape[1]]
                                    ).then_inc(sig["kept_by_dve"], 1)

        @block.scalar
        def _(act):
            for g, (parts, dst) in enumerate(groups):
                if g % 2 == 1:
                    act.wait_ge(sig["turned"], g + 1)
                    act.copy(dst, chip.psum[:dst.shape[0], g % 8, :dst.shape[1]]
                             ).then_inc(sig["kept_by_act"], 1)


class Attention:

    Q_PARTS, K_PARTS = (0, 0, 0, 1, 1, 2), (0, 1, 2, 0, 1, 0)

    def __init__(self, chip, hd, vd, key_tiles, scale, mask=None, last_keys=P, heads=None, rep=1):
        self.hd, self.vd, self.scale, self.mask, self.rep = hd, vd, scale, mask, rep
        self.heads = D // hd if heads is None else heads
        self.kv_heads = self.heads // rep
        self.split = hd < 64
        self.shift_at = 6 * hd if self.split else hd
        self.shifts = 3 if self.split else 1
        self.bias_at = self.shift_at + self.shifts
        self.passes = -(-(self.shift_at + self.shifts) // P)
        self.slot = self.passes * P
        self.key_tiles, self.last_keys = key_tiles, last_keys
        self.keys = (key_tiles - 1) * P + last_keys
        self.v_slot = 2 * vd
        self.per_bank = P // self.v_slot if vd == 16 else 1
        self.bank_cols = 2 * BANK if self.split else BANK
        self.ident = chip.ident_bf if self.split else chip.ident
        at = 0

        def take(n):
            nonlocal at
            at += n
            return at - n

        def operand(*shape):
            n = 1
            for v in shape:
                n *= v
            v = chip.carve(take(n // 2 if self.split else n), n // 2 if self.split else n)
            if self.split:
                v = v.bitcast(BF16)
            if len(shape) == 3:
                return v.rearrange("p (a b c) -> p a b c", b=shape[1], c=shape[2])
            return v.rearrange("p (a b) -> p a b", b=shape[1])

        self.q = operand(NT, self.heads, self.slot)
        self.k = operand(key_tiles, self.kv_heads, self.slot)
        self.v = chip.carve(take(key_tiles * self.kv_heads * self.v_slot), key_tiles,
                            self.kv_heads, self.v_slot)
        self.qT = [operand(self.passes, S) for i in range(3)]
        self.kT = [operand(self.passes, key_tiles * P) for i in range(3)]
        self.unscaled = chip.carve(take(BANK), BANK) if vd == 16 else None
        self.inverse = chip.carve(take(BANK), BANK)
        chunks = 4 if hd == 16 or key_tiles > 8 else 8
        self.outT = chip.carve(take(chunks * BANK), chunks, BANK)
        probs = take(0)
        self.probs = [chip.carve(take(key_tiles * BANK), key_tiles, BANK) for i in range(2)]
        self.floor_rows = None
        if self.mask is None and self.split:
            self.floor_rows = chip.carve(take(2 * BANK), 2, BANK)
        self.raw_q = chip.carve(probs, NT * D)
        self.raw_k = chip.carve(probs + 1024, 2048)
        self.tmp, self.tmp2 = (chip.carve(probs + n, 1024) for n in ((3072, 4096)
                               if self.mask is None else (2048, 3072)))

    def slots(self, t, tiles):
        return t[:, :tiles].rearrange("p t h w -> p (t h) w")

    def values(self, t, rows=P):
        return self.v[:rows, t, :, 0:self.vd]

    def value_parts(self, t):
        if self.vd == 16:
            return [(self.v[:, t, :, 0:16], slice(0, self.kv_heads))]
        return [(self.v[:, t, 0:self.kv_heads:2, 0:64], slice(0, self.kv_heads, 2)),
                (self.v[:, t, 1:self.kv_heads:2, 64:128], slice(1, self.kv_heads, 2))]

    def width(self, kt):
        return self.last_keys if kt == self.key_tiles - 1 else P

    def keys_of(self, qt):
        if self.mask == "causal":
            return 0, qt + 1
        if self.mask == "band":
            return max(qt - 1, 0), qt + 1
        if self.mask == "ahead":
            return 0, qt + 2
        return 0, self.key_tiles

    def masks_of(self, qt, lo, hi):
        if self.mask is None:
            return []
        if self.mask == "causal":
            found = [(0, P, qt * P)]
        elif self.mask == "band":
            found = [(0, P, (qt - 1) * P)] * (qt > 0) + [(P, 2 * P, qt * P)]
        else:
            found = [(0, P, qt * P), (P, P + self.width(qt + 1), (qt + 1) * P)]
        return [m for m in found if lo <= m[2] < hi]

    def masks_of_keys(self, kt):
        if self.mask is None:
            return []
        if self.mask == "causal":
            return [(0, P, 0)]
        if self.mask == "band":
            return [(0, P, 0)] + [(P, 2 * P, P)] * (kt + 1 < NT)
        if kt == 0:
            return [(P, 2 * P, 0)]
        return [(0, P, 0)] + [(P, 2 * P, P)] * (kt < NT)

    def queries_of(self, kt):
        seen = [qt for qt in range(NT) if self.keys_of(qt)[0] <= kt < self.keys_of(qt)[1]]
        return seen[0], seen[-1] + 1

    def maxima_units(self):
        units = []
        for qt in range(NT):
            k0, k1 = self.keys_of(qt)
            first, end = k0 * P, min(k1 * P, self.keys)
            for i, lo in enumerate(range(first, end, BANK)):
                units.append((qt, lo, min(BANK, end - lo), i))
        return units

    def turn_units(self, h):
        def unit(src, dst, blocks):
            parts, end = [], 0
            for p, t, w in blocks:
                parts.append((src(p, t, w), end))
                end += w
            return parts, dst

        qT, kT, kv = self.qT[h % 3], self.kT[(h // self.rep) % 3], h // self.rep
        units = [self.query_unit(h)]
        if h % self.rep == 0:
            step = self.bank_cols // P
            for p in range(self.passes):
                for t0 in range(0, self.key_tiles, step):
                    tiles = range(t0, min(t0 + step, self.key_tiles))
                    n = sum(self.width(t) for t in tiles)
                    units.append(unit(
                        lambda p, t, w: self.k[:w, t, kv, p * P:(p + 1) * P],
                        kT[:, p, t0 * P:t0 * P + n], [(p, t, self.width(t)) for t in tiles]))
        return units

    def query_unit(self, h):
        parts = [(self.q[:, t, h, p * P:(p + 1) * P], (p * NT + t) * P)
                 for p in range(self.passes) for t in range(NT)]
        return parts, self.qT[h % 3].rearrange("p a b -> p (a b)")

    def value_pieces(self, kt):
        q0, q1 = self.queries_of(kt)
        pieces = []
        for qt in range(q0, q1):
            k0, k1 = self.keys_of(qt) if self.mask == "band" else (0, self.key_tiles)
            flags = (kt == k0, kt == k1 - 1)
            if pieces and pieces[-1][2:] == flags:
                pieces[-1] = (pieces[-1][0], qt + 1, *flags)
            else:
                pieces.append((qt, qt + 1, *flags))
        return pieces


def fill_slots_stage(chip, at):
    nc, sig = chip.nc, chip.stage("small")
    with nc.Block() as block:
        @block.gpsimd
        def _(pool):
            chip.reset_others(pool, sig)
            pool.memset(at.v, 1.0).then_inc(sig["pool_done"], 1)

        @block.vector
        def _(dve):
            order = Order(dve, sig["order"])
            order(dve.memset(at.k, 0.0))
            ins = dve.memset(at.slots(at.k, at.key_tiles)[:, :, at.shift_at:at.bias_at], 1.0)
            order(ins)
            order(dve.memset(at.q, 0.0))
            if not at.split:
                order(dve.memset(at.slots(at.q, NT)[:, :, at.bias_at:at.bias_at + 1], 1.0))


def project_stage(chip, loads, jobs, q_post=None, k_post=None):
    nc, sig = chip.nc, chip.stage("project")
    posts = [p for p in (q_post, k_post) if p is not None]
    biased = any(len(c) == 3 for _, copies in jobs for c in copies)
    with nc.Block() as block:
        @block.gpsimd
        def _(pool):
            chip.reset_others(pool, sig)

        @block.sync
        def _(sp):
            for dst, src in loads:
                sp.dma_start(dst, src).then_inc(sig["weights_loaded"], 16)

        @block.tensor
        def _(pe):
            if loads:
                pe.wait_ge(sig["weights_loaded"], 16 * len(loads))
            for j, (products, copies) in enumerate(jobs):
                if j >= 4:
                    pe.wait_ge(sig["product_kept"], j - 3)
                two = chip.psum[:, 2 * (j % 4):2 * (j % 4) + 2, :].rearrange("p a b -> p (a b)")
                for lhs, rhs, first, start, stop in products:
                    mm = pe.matmul(two[:lhs.shape[1], first:first + rhs.shape[1]], lhs, rhs,
                                   start=start, stop=stop)
                mm.then_inc(sig["product_ready"], 1)

        @block.scalar
        def _(act):
            for j, (products, copies) in enumerate(jobs if not biased else []):
                act.wait_ge(sig["product_ready"], j + 1)
                two = chip.psum[:, 2 * (j % 4):2 * (j % 4) + 2, :].rearrange("p a b -> p (a b)")
                for dst, src in copies:
                    ins = act.copy(dst, src(two))
                ins.then_inc(sig["product_kept"], 1)
            n = 0
            for post in posts:
                if post.norm:
                    n += 1
                    act.wait_ge(sig["sums_ready"], n)
                    act.activation(post.root, post.sums, ACT.Sqrt).then_inc(sig["roots_ready"], 1)

        @block.vector
        def _(dve):
            order = Order(dve, sig["order"])
            if loads:
                dve.wait_ge(sig["weights_loaded"], 16 * len(loads))
            for j, (products, copies) in enumerate(jobs if biased else []):
                dve.wait_ge(sig["product_ready"], j + 1)
                two = chip.psum[:, 2 * (j % 4):2 * (j % 4) + 2, :].rearrange("p a b -> p (a b)")
                for dst, src, row in copies:
                    ins = dve.tensor_tensor(dst, src(two), row, ALU.add)
                ins.then_inc(sig["product_kept"], 1)
            if not posts:
                return
            dve.wait_ge(sig["product_kept"], len(jobs))
            n = 0
            for post in posts:
                t, tmp = post.raw, post.tmp
                if post.norm:
                    mult, eps, floor, scale = post.norm
                    order(dve.tensor_tensor(tmp, t, t, ALU.mult))
                    order(dve.tensor_reduce(post.sums, tmp, AX, ALU.add))
                    dve.tensor_scalar(post.sums, post.sums, mult, eps, ALU.mult,
                                      ALU.add).then_inc(sig["sums_ready"], 1)
                    n += 1
                    dve.wait_ge(sig["roots_ready"], n)
                    order(dve.tensor_scalar(post.root, post.root, floor, 1.0 / scale, ALU.max,
                                            ALU.mult))
                    order(dve.reciprocal(post.root, post.root))
                    last = post.gain is None and post.cos is None
                    order(dve.tensor_tensor(post.dst if last else t, t,
                                            post.root.to_broadcast(t.shape), ALU.mult))
                    if last:
                        continue
                if post.gain is not None:
                    out = post.dst if post.cos is None else t
                    order(dve.tensor_tensor(out, t, post.gain.unsqueeze(1).to_broadcast(t.shape), ALU.mult))
                    if post.cos is None:
                        continue
                order(dve.tensor_tensor(post.by_tile(tmp), post.by_tile(t), post.table(post.cos),
                                        ALU.mult))
                for dst_part, src_part in post.partners:
                    ins = dve.tensor_tensor(post.by_tile(post.tmp2)[:, :, :, dst_part],
                                            post.by_tile(t)[:, :, :, src_part],
                                            post.table(post.sin)[:, :, :, dst_part], ALU.mult)
                    order(ins)
                order(dve.tensor_tensor(post.dst, tmp, post.tmp2, ALU.add))


class HeadPost:

    def __init__(self, chip, at, raw, slots, tiles, heads, norm=None, gain=None, cos=None,
                 sin=None, pairs=False):
        hd = at.hd
        n = tiles * heads
        self.tiles, self.heads, self.hd = tiles, heads, hd
        self.raw = raw[:, :n * hd].rearrange("p (n e) -> p n e", e=hd)
        self.tmp = at.tmp[:, :n * hd].rearrange("p (n e) -> p n e", e=hd)
        self.tmp2 = at.tmp2[:, :n * hd].rearrange("p (n e) -> p n e", e=hd)
        self.sums = chip.cols[:, 0:n]
        self.root = chip.roots[:, 0:n]
        self.norm, self.cos, self.sin = norm, cos, sin
        self.gain = gain
        self.dst = self.raw if at.split else at.slots(slots, tiles)[:, :, :hd]
        if pairs:
            self.partners = [(slice(0, hd, 2), slice(1, hd, 2)), (slice(1, hd, 2), slice(0, hd, 2))]
        else:
            self.partners = [(slice(0, hd // 2), slice(hd // 2, hd)),
                             (slice(hd // 2, hd), slice(0, hd // 2))]

    def by_tile(self, t):
        return t.rearrange("p (t h) e -> p t h e", h=self.heads)

    def table(self, t):
        return t.unsqueeze(2).to_broadcast([P, self.tiles, self.heads, self.hd])


def split_stage(chip, at, jobs):
    nc, sig = chip.nc, chip.stage("split")
    with nc.Block() as block:
        @block.gpsimd
        def _(pool):
            chip.reset_others(pool, sig)

        @block.vector
        def _(dve):
            order = Order(dve, sig["order"])
            for j, (raw, slots, parts) in enumerate(jobs):
                first, second, third = (
                    slots[:, :, parts.index(i) * at.hd:(parts.index(i) + 1) * at.hd]
                    for i in range(3))
                dve.tensor_copy(first, raw).then_inc(sig["part_ready"], 1)
                dve.wait_ge(sig["part_ready"], 2 * j + 1)
                order(dve.tensor_tensor(raw, raw, first, ALU.subtract))
                dve.tensor_copy(second, raw).then_inc(sig["part_ready"], 1)
                dve.wait_ge(sig["part_ready"], 2 * j + 2)
                order(dve.tensor_tensor(third, raw, second, ALU.subtract))

        @block.scalar
        def _(act):
            for j, (raw, slots, parts) in enumerate(jobs):
                for i in range(2):
                    act.wait_ge(sig["part_ready"], 2 * j + i + 1)
                    places = [n for n, part in enumerate(parts) if part == i]
                    src = slots[:, :, places[0] * at.hd:(places[0] + 1) * at.hd]
                    for n in places[1:]:
                        act.copy(slots[:, :, n * at.hd:(n + 1) * at.hd],
                                 src).then_inc(sig["repeated"], 1)


def split_jobs(at, raw, slots, tiles, heads, parts):
    return [(raw[:, t * heads * at.hd:(t + 1) * heads * at.hd].rearrange(
        "p (n e) -> p n e", e=at.hd), slots[:, t], parts) for t in range(tiles)]


def attend_stage(chip, at, out_chunk, mask=None, clip=None):
    nc, sig = chip.nc, chip.stage("attend")
    heads, scale = at.heads, at.scale
    max_units = at.maxima_units()
    parts = max(u[3] for u in max_units) + 1
    turns = [at.turn_units(h) for h in range(heads)]
    S_LAG = 2
    steps = max(len(max_units), at.key_tiles + S_LAG, max(len(t) for t in turns))
    per_turn = 1 if clip is None else 2
    MAX_BANKS, SCORE_BANKS, TURN_BANKS, VALUE_BANKS = (0, 1), (2, 3), (4, 5), (6, 7)
    minus = at.slots(at.q, NT)[:, :, at.shift_at:at.shift_at + at.shifts]
    tops = chip.cols[:, 0:NT * parts].rearrange("p (t c) -> p t c", c=parts)
    shift = chip.roots[:, 0:NT].unsqueeze(2)
    rest = chip.roots[:, NT:2 * NT].unsqueeze(2)
    groups = heads // at.per_bank

    def turn_order():
        n, order = 0, {}
        for i in range(-2, heads + 1):
            for u in range(steps):
                if u == 1 and 0 <= i < heads:
                    order["shift", i] = n
                    n += per_turn
                if i + 2 < heads and u < len(turns[i + 2]):
                    order[i + 2, u] = n
                    n += 1
        return order

    turn_no = turn_order()

    def turned_by(h):
        return max(turn_no[h, u] for u in range(len(turns[h]))) + 1

    def turn_bank(n):
        bank = chip.psum[:, TURN_BANKS[n % 2], :]
        return bank.bitcast(BF16) if at.split else bank

    def value_bank(h):
        g = h // at.per_bank
        return chip.psum[:, VALUE_BANKS[g % 2], :]

    with nc.Block() as block:
        @block.gpsimd
        def _(pool):
            chip.reset_others(pool, sig)

        @block.tensor
        def _(pe):
            def turn(n, unit):
                if n >= 2:
                    pe.wait_ge(sig["turn_kept"], n - 1)
                for src, first in unit[0]:
                    rows = src.shape[0]
                    mm = pe.transpose(turn_bank(n)[:, first:first + rows], src,
                                      at.ident[:rows, :rows])
                mm.then_inc(sig["turned"], 1)

            def turn_shift(h):
                pe.wait_ge(sig["shift_ready"], h + 1)
                n = turn_no["shift", h]
                turn(n, at.query_unit(h))
                if clip is not None:
                    pe.wait_ge(sig["turn_kept"], n + 1)
                    pe.matmul(chip.psum[:, TURN_BANKS[(n + 1) % 2], :], chip.pick_shift[:, :],
                              at.qT[h % 3][:, 0, :], start=True,
                              stop=True).then_inc(sig["turned"], 1)

            def maxima(h, u):
                qt, lo, n, part = max_units[u]
                count = h * len(max_units) + u
                if u == 0:
                    pe.wait_ge(sig["turn_kept"], turned_by(h))
                if count >= 2:
                    pe.wait_ge(sig["max_taken"], count - 1)
                ps = chip.psum[:, MAX_BANKS[count % 2], :]
                masks = at.masks_of(qt, lo, lo + n)
                for p in range(at.passes):
                    mm = pe.matmul(ps[:, :n], at.qT[h % 3][:, p, qt * P:(qt + 1) * P],
                                   at.kT[(h // at.rep) % 3][:, p, lo:lo + n], start=p == 0,
                                   stop=p == at.passes - 1 and not masks)
                for i, (m0, m1, col) in enumerate(masks):
                    mm = pe.matmul(ps[:, col - lo:col - lo + m1 - m0], chip.ident_bf[:, :],
                                   mask[0][:, m0:m1], start=False, stop=i == len(masks) - 1)
                mm.then_inc(sig["scores_ready"], 1)

            def shifted(h, kt):
                count = h * at.key_tiles + kt
                if kt == 0:
                    pe.wait_ge(sig["turn_kept"], turn_no["shift", h] + 1)
                if count >= 2:
                    pe.wait_ge(sig["exp_ready"], count - 1)
                q0, q1 = at.queries_of(kt)
                w = at.width(kt)
                ps = chip.psum[:w, SCORE_BANKS[count % 2], :(q1 - q0) * P]
                masks = at.masks_of_keys(kt)
                for p in range(at.passes):
                    mm = pe.matmul(ps, at.kT[(h // at.rep) % 3][:, p, kt * P:kt * P + w],
                                   at.qT[h % 3][:, p, q0 * P:q1 * P], start=p == 0,
                                   stop=p == at.passes - 1 and not masks)
                for i, (m0, m1, col) in enumerate(masks):
                    mm = pe.matmul(ps[:, col:col + m1 - m0], chip.ident_bf[:, :w],
                                   mask[1][:, m0:m1], start=False, stop=i == len(masks) - 1)
                mm.then_inc(sig["shifted_ready"], 1)

            def values(h, kt):
                if kt == 0 and h % at.per_bank == 0 and h // at.per_bank >= 2:
                    pe.wait_ge(sig["heads_kept"], h // at.per_bank - 1)
                pe.wait_ge(sig["exp_ready" if clip is None else "probs_ready"],
                           h * at.key_tiles + kt + 1)
                r = slice((h % at.per_bank) * at.v_slot, (h % at.per_bank + 1) * at.v_slot)
                w = at.width(kt)
                for q0, q1, starts, stops in at.value_pieces(kt):
                    mm = pe.matmul(value_bank(h)[r, q0 * P:q1 * P], at.v[:w, kt, h // at.rep, :],
                                   at.probs[h % 2][:w, kt, q0 * P:q1 * P], start=starts,
                                   stop=stops)
                if kt == at.key_tiles - 1:
                    mm.then_inc(sig["values_ready"], 1)

            def spread_sums(g):
                pe.wait_ge(sig["group_kept"], g + 1)
                pe.matmul(chip.psum[:, VALUE_BANKS[g % 2], :], chip.pick_sum[:, :],
                          at.unscaled, start=True, stop=True).then_inc(sig["sums_spread"], 1)

            pe.wait_ge(sig["shift_cleared"], 1)
            for i in range(-2, heads + 1):
                for u in range(steps):
                    if 0 <= i + 1 < heads and u < len(max_units):
                        maxima(i + 1, u)
                    if 0 <= i - 1 < heads and u < at.key_tiles:
                        values(i - 1, u)
                    if u == 1 and 0 <= i < heads:
                        turn_shift(i)
                    if u == 1 and at.vd == 16 and i - 2 >= 0 and (i - 1) % at.per_bank == 0:
                        spread_sums((i - 2) // at.per_bank)
                    if 0 <= i < heads and 0 <= u - S_LAG < at.key_tiles:
                        shifted(i, u - S_LAG)
                    if i + 2 < heads and u < len(turns[i + 2]):
                        turn(turn_no[i + 2, u], turns[i + 2][u])
            if at.vd == 16:
                spread_sums(groups - 1)

        @block.scalar
        def _(act):
            def keep(n, dst):
                act.wait_ge(sig["turned"], n + 1)
                act.copy(dst, turn_bank(n)[:, :dst.shape[1]]).then_inc(sig["turn_kept"], 1)

            def exp(h, kt):
                count = h * at.key_tiles + kt
                if kt == 0 and h >= 2:
                    act.wait_ge(sig["values_ready"], h - 1)
                act.wait_ge(sig["shifted_ready"], count + 1)
                q0, q1 = at.queries_of(kt)
                w = at.width(kt)
                ins = act.activation(at.probs[h % 2][:w, kt, q0 * P:q1 * P],
                                     chip.psum[:w, SCORE_BANKS[count % 2], :(q1 - q0) * P],
                                     ACT.Exp, scale=scale)
                ins.then_inc(sig["exp_ready"], 1)

            for i in range(-2, heads + 1):
                for u in range(steps):
                    if u == 1 and 0 <= i < heads:
                        n = turn_no["shift", i]
                        keep(n, at.query_unit(i)[1])
                        if clip is not None:
                            act.wait_ge(sig["turned"], n + 2)
                            if i >= 2:
                                act.wait_ge(sig["probs_ready"], (i - 1) * at.key_tiles)
                            act.activation(at.floor_rows[:, i % 2],
                                           chip.psum[:, TURN_BANKS[(n + 1) % 2], :], ACT.Exp,
                                           bias=chip.clip_col[:, 0:1],
                                           scale=scale).then_inc(sig["turn_kept"], 1)
                    if 0 <= i < heads and 0 <= u - S_LAG < at.key_tiles:
                        exp(i, u - S_LAG)
                    if i + 2 < heads and u < len(turns[i + 2]):
                        keep(turn_no[i + 2, u], turns[i + 2][u][1])
                if at.vd == 16 and i - 1 >= 0 and i % at.per_bank == 0:
                    g = (i - 1) // at.per_bank
                    act.wait_ge(sig["values_ready"], i)
                    if g >= 1:
                        act.wait_ge(sig["heads_kept"], g)
                    act.copy(at.unscaled, chip.psum[:, VALUE_BANKS[g % 2], :]
                             ).then_inc(sig["group_kept"], 1)

        @block.vector
        def _(dve):
            order = Order(dve, sig["order"])
            dve.memset(minus, 0.0).then_inc(sig["shift_cleared"], 1)
            if parts > 1:
                order(dve.memset(tops, -BIG))

            def take(h, u):
                qt, lo, n, part = max_units[u]
                count = h * len(max_units) + u
                dve.wait_ge(sig["scores_ready"], count + 1)
                bank = chip.psum[:, MAX_BANKS[count % 2], :n]
                dst = shift[:, qt] if parts == 1 else tops[:, qt, part:part + 1]
                dve.tensor_reduce(dst, bank, AX, ALU.max,
                                  negate=parts == 1).then_inc(sig["max_taken"], 1)

            def write_shift(h):
                dve.wait_ge(sig["max_taken"], (h + 1) * len(max_units))
                if parts > 1:
                    order(dve.tensor_reduce(shift, tops, AX, ALU.max, negate=True))
                if clip is not None:
                    order(dve.tensor_scalar(shift, shift, -clip, clip, ALU.max, ALU.min))
                col = [at.q[:, :, h, at.shift_at + i:at.shift_at + i + 1]
                       for i in range(at.shifts)]
                if at.split:
                    order(dve.tensor_copy(col[0], shift))
                    order(dve.tensor_tensor(rest, shift, col[0], ALU.subtract))
                    order(dve.tensor_copy(col[1], rest))
                    dve.tensor_tensor(col[2], rest, col[1],
                                      ALU.subtract).then_inc(sig["shift_ready"], 1)
                else:
                    dve.tensor_copy(col[0], shift).then_inc(sig["shift_ready"], 1)
                dve.wait_ge(sig["shift_ready"], h + 1)

            def bound(h, kt):
                dve.wait_ge(sig["exp_ready"], h * at.key_tiles + kt + 1)
                if kt == 0:
                    dve.wait_ge(sig["turn_kept"], turn_no["shift", h] + 2)
                probs = at.probs[h % 2][:, kt, :]
                dve.scalar_tensor_tensor(probs, probs, 1.0, at.floor_rows[:, h % 2], ALU.min,
                                         ALU.max).then_inc(sig["probs_ready"], 1)

            def divide_group(g):
                dve.wait_ge(sig["sums_spread"], g + 1)
                order(dve.reciprocal(at.inverse, chip.psum[:, VALUE_BANKS[g % 2], :]))
                dve.tensor_tensor(at.outT[:, bass.ds(out_chunk + g, 1), :].rearrange(
                    "p a n -> p (a n)"), at.unscaled, at.inverse,
                    ALU.mult).then_inc(sig["heads_kept"], 1)
                dve.wait_ge(sig["heads_kept"], g + 1)

            def divide_head(h):
                dve.wait_ge(sig["values_ready"], h + 1)
                r, other = slice(0, 64), slice(64, P)
                if h % 2:
                    r, other = other, r
                bank = value_bank(h)
                order(dve.reciprocal(at.inverse[r], bank[other]))
                dve.tensor_tensor(at.outT[r, bass.ds(out_chunk + h // 2, 1), :].rearrange(
                    "p a n -> p (a n)"), bank[r], at.inverse[r],
                    ALU.mult).then_inc(sig["heads_kept"], 1)
                dve.wait_ge(sig["heads_kept"], h + 1)

            for i in range(-2, heads + 1):
                for u in range(steps):
                    if 0 <= i + 1 < heads and u < len(max_units):
                        take(i + 1, u)
                    if clip is not None and 0 <= i < heads and 0 <= u - S_LAG < at.key_tiles:
                        bound(i, u - S_LAG)
                    if u == 3 and at.vd == 16 and i - 2 >= 0 and (i - 1) % at.per_bank == 0:
                        divide_group((i - 2) // at.per_bank)
                    if u == 0 and at.vd == 64 and i - 2 >= 0:
                        divide_head(i - 2)
                if 0 <= i + 1 < heads:
                    write_shift(i + 1)
            if at.vd == 16:
                divide_group(groups - 1)
            else:
                divide_head(heads - 1)


def out_stage(chip, outT, b, chunks, bias, addend, dst):
    cols = slice(b * S, (b + 1) * S)
    jobs = [(dst[:, m, cols], [(chip.w_out[:, c, m * P:(m + 1) * P], outT[:, c])
                               for c in range(chunks)],
             None if bias is None else bias[:, m:m + 1],
             None if addend is None else addend[:, m, cols]) for m in range(2)]
    linear_stage(chip, [], jobs)


def rope_tables(hd, base, pairs, theta=None):
    import numpy as np
    half = hd // 2
    f32 = np.float32
    if theta is None:
        theta = f32(1.0) / (f32(base) ** (np.arange(0, hd, 2, dtype=f32) / f32(hd)))
    angle = np.arange(S, dtype=f32)[:, None] * theta[None, :].astype(f32)
    c, s = np.cos(angle), np.sin(angle)
    if pairs:
        cos, sin = np.repeat(c, 2, -1), np.repeat(s, 2, -1)
        sin[:, 0::2] *= -1
    else:
        cos, sin = np.concatenate([c, c], -1), np.concatenate([-s, s], -1)
    return cos.astype(f32), sin.astype(f32)


def by_partition(table):
    import numpy as np
    return np.ascontiguousarray(table.reshape(NT, P, -1).transpose(1, 0, 2).reshape(P, -1))


def band_masks(lowest, highest, other):
    import numpy as np
    i, j = np.arange(P)[:, None], np.arange(P)[None, :]

    def tile(distance):
        return np.where((distance >= lowest) & (distance <= highest), 0.0, -BIG)

    diag_q, diag_k = tile(i - j), tile(j - i)
    side_q, side_k = tile(i - j - other * P), tile(j - i - other * P)
    if other == -1:
        return np.concatenate([side_q, diag_q, diag_k, side_k], 1)
    if other == 1:
        return np.concatenate([diag_q, side_q, side_k, diag_k], 1)
    return np.concatenate([diag_q, diag_q, diag_k, diag_k], 1)


def constants():
    import numpy as np
    bf16 = mybir.dt.np(BF16)
    out = {"ident": np.eye(P, dtype=np.float32), "ident_bf": np.eye(P).astype(bf16)}
    for name, args in (("causal", (0, 10 ** 6, 0)), ("band64", (0, 63, -1)), ("band65", (0, 64, -1)),
                       ("band128", (0, 127, -1)), ("ahead", (-16, 10 ** 6, 1))):
        out["mask_" + name] = band_masks(*args).astype(bf16)
    for name, args in (("rope_l0g", (16, 1e6, True)), ("rope_l0l", (16, 1e4, True)),
                       ("rope_l2", (32, 1e4, False)), ("rope_l3", (16, 1e4, False))):
        cos, sin = rope_tables(*args)
        out[name + "_cos"], out[name + "_sin"] = by_partition(cos), by_partition(sin)
    out["pick_sum"] = np.zeros((P, P), np.float32)
    for i in range(0, P, 32):
        out["pick_sum"][i + 16, i:i + 32] = 1.0
    out["pick_shift"] = np.zeros((P, P), np.float32)
    out["pick_shift"][96:99] = 1.0
    out["pick_shift"] = out["pick_shift"].astype(bf16)
    out["head_sum"] = np.repeat(np.eye(8, dtype=np.float32), 16, 0)
    for n in (4, 16, 40):
        out[f"ties{n}"] = np.tril(np.ones((n, n), np.float32), -1).reshape(1, n * n)
    sel = np.zeros((17, 12, P), np.float32)
    for f in range(8):
        sel[2 * f, f, :64] = 1.0
        sel[2 * f + 1, f, 64:] = 1.0
    sel[16, 8:] = 1.0
    out["sel_l2"] = sel
    sel = np.zeros((40, 33, P), np.float32)
    for f in range(32):
        sel[f, f] = 1.0
    sel[32:, 32] = 1.0
    out["sel_l3"] = sel
    cos, sin = rope_tables(64, 1e4, False)
    f32 = np.float32
    half = np.arange(0, 64, 2, dtype=f32)
    base = (half + f32(0.4 * 64)) / f32(1.4 * 64)
    power = (np.arange(S, dtype=f32) - S // 2) / f32(32)
    scale = base[None, :] ** power[:, None]
    scale = np.concatenate([scale, scale], -1).astype(f32)
    for name, s in (("xpos_q", scale), ("xpos_k", f32(1.0) / scale)):
        out[name + "_cos"], out[name + "_sin"] = by_partition(cos * s), by_partition(sin * s)
    return out


def fm(w):
    return w.rearrange("(c p) n -> p c n", p=P)


def ctx_loads(dst, w, cols=slice(None)):
    return [(dst[:, 0], w[0:P, cols]), (dst[:DC - P, 1], w[P:DC, cols])]


def layer0_attention(chip, a):
    h = chip.inner
    for kind, table, mask_name in (("g", "rope_l0g", "causal"), ("l", "rope_l0l", "band64")):
        src = chip.state if kind == "g" else h
        gains = chip.gains[:, 0:2]
        norm_name = "L0_attn_norm1_w" if kind == "g" else "L0_attn_norm2_w"
        norm_stage(chip, src, chip.normed, (P, P), B * S, 1e-6, center=False, gain=gains,
                   loads=[(gains, a[norm_name + "_col"])])
        at = Attention(chip, 16, 16, NT, 0.25, "causal" if kind == "g" else "band", rep=4)
        fill_slots_stage(chip, at)
        cos, sin = chip.tables(16)
        load_stage(chip, [(cos, a[table + "_cos"].rearrange("p (t e) -> p t e", t=NT)),
                          (sin, a[table + "_sin"].rearrange("p (t e) -> p t e", t=NT)),
                          (chip.masks[:, :], a["mask_" + mask_name]),
                          (chip.w_in[:, :, 0:D], fm(a[f"L0_attn_{kind}_wq"])),
                          (chip.w_out[:, 0:4, :], fm(a[f"L0_attn_{kind}_wo_slots"]))]
                   + ([(chip.w_in[:, :, 256:320], fm(a["L0_attn_g_kv_down"])),
                       (chip.w_in[:64, 0, 384:448], a["L0_attn_g_k_up"]),
                       (chip.w_in[:64, 0, 448:512], a["L0_attn_g_v_up"])] if kind == "g" else
                      [(chip.w_in[:, :, 256:320], fm(a["L0_attn_l_wk"])),
                       (chip.w_in[:, :, 320:384], fm(a["L0_attn_l_wv"]))]))
        masks = (chip.masks[:, 0:256], chip.masks[:, 256:512])
        latent = chip.carve(30000, BANK)[:64]
        for b in range(B):
            cols = slice(b * S, (b + 1) * S)
            if kind == "g":
                linear_stage(chip, [], [(latent, [(chip.w_in[:, c, 256:320],
                                                   chip.normed[:, c, cols]) for c in range(2)],
                                         None, None)])
            jobs = []
            for t in range(NT):
                tok = slice(b * S + t * P, b * S + (t + 1) * P)
                x = [chip.normed[:, c, tok] for c in range(2)]
                if kind == "g":
                    products = [(x[0], chip.w_in[:, 0, 0:D], 0, True, False),
                                (x[1], chip.w_in[:, 1, 0:D], 0, False, True),
                                (latent[:, t * P:(t + 1) * P], chip.w_in[:64, 0, 384:512], BANK,
                                 True, True)]
                    k_at = BANK
                else:
                    products = [(x[0], chip.w_in[:, 0, 0:384], 0, True, False),
                                (x[1], chip.w_in[:, 1, 0:384], 0, False, True)]
                    k_at = D
                copies = [(at.raw_q[:, t * D:(t + 1) * D], lambda ps: ps[:, 0:D]),
                          (at.raw_k[:, t * 64:(t + 1) * 64],
                           lambda ps, k=k_at: ps[:, k:k + 64]),
                          (at.v[:, t, :, 0:16], lambda ps, k=k_at: ps[:, k + 64:k + 128].rearrange(
                              "p (n e) -> p n e", e=16))]
                jobs.append((products, copies))
            norm = (1.0 / 16, 1e-6, 0.0, 1.0)
            q_post = HeadPost(chip, at, at.raw_q, at.q, NT, 16, norm, None, cos, sin, True)
            k_post = HeadPost(chip, at, at.raw_k, at.k, NT, 4, norm, None, cos, sin, True)
            project_stage(chip, [], jobs, q_post, k_post)
            split_stage(chip, at, split_jobs(at, at.raw_q, at.q, NT, 16, at.Q_PARTS)
                        + split_jobs(at, at.raw_k, at.k, NT, 4, at.K_PARTS))
            attend_stage(chip, at, 0, masks)
            out_stage(chip, at.outT, b, 4, None, src, h)
    norm_stage(chip, chip.state, chip.state, (P, P), B * S, 1e-5, add=h)


def cross_attention(chip, a, pre, hd, clip=None):
    at = Attention(chip, hd, hd, SC // P, hd ** -0.5)
    biased = at.split
    chunks = 4 if hd == 16 else 8
    fill_slots_stage(chip, at)
    bo = chip.gains[:, 0:2]
    rows = chip.table_mem[:, 0:3 * D]
    loads = [(chip.w_out[:, 0:chunks, :], fm(a[pre + ("Wo_slots" if biased else "Wo")])),
             (bo, a[pre + "bo_col"])]
    if biased:
        for i, n in enumerate("qkv"):
            loads.append((rows[:, i * D:(i + 1) * D],
                          a[pre + "b" + n].unsqueeze(0).partition_broadcast(P)))
    load_stage(chip, loads)

    def group(b, g):
        cols = bass.ds(g * D, D)
        w_q, w_k, w_v = (chip.w_in[:, :, i * D:(i + 1) * D] for i in range(3))
        loads = ([(w_q, fm(a[pre + "Wq"])[:, :, cols])] + ctx_loads(w_k, a[pre + "Wk"], cols)
                 + ctx_loads(w_v, a[pre + "Wv"], cols))

        def heads_of(ps, first, which=slice(None)):
            return ps[:, first:first + D].rearrange("p (h e) -> p h e", e=hd)[:, which]

        jobs = []
        for t in range(NT):
            tok = slice(b * S + t * P, b * S + (t + 1) * P)
            products = [(chip.state[:, c, tok], w_q[:, c], 0, c == 0, c == 1) for c in range(2)]
            if biased:
                copies = [(at.raw_q[:, t * D:(t + 1) * D], lambda ps: ps[:, 0:D], rows[:, 0:D])]
            else:
                copies = [(at.q[:, t, :, 0:hd], lambda ps: heads_of(ps, 0))]
            jobs.append((products, copies))
        for t in range(SC // P):
            tok = slice(b * SC + t * P, b * SC + (t + 1) * P)
            products = [(chip.ctx[:r, c, tok], chip.w_in[:r, c, D:3 * D], 0, c == 0, c == 1)
                        for c, r in ((0, P), (1, DC - P))]
            if biased:
                copies = [(at.raw_k[:, t * D:(t + 1) * D], lambda ps: ps[:, 0:D], rows[:, D:2 * D])]
                copies += [(dst, lambda ps, which=which: heads_of(ps, D, which),
                            heads_of(rows, 2 * D, which)) for dst, which in at.value_parts(t)]
            else:
                copies = [(at.k[:, t, :, 0:hd], lambda ps: heads_of(ps, 0))]
                copies += [(dst, lambda ps, which=which: heads_of(ps, D, which))
                           for dst, which in at.value_parts(t)]
            jobs.append((products, copies))
        project_stage(chip, loads, jobs)
        if at.split:
            split_stage(chip, at, split_jobs(at, at.raw_q, at.q, NT, at.heads, at.Q_PARTS)
                        + split_jobs(at, at.raw_k, at.k, SC // P, at.heads, at.K_PARTS))
        attend_stage(chip, at, g * 2, clip=clip)

    for b in range(B):
        if hd == 16:
            group(b, 0)
        else:
            with chip.nc.Fori(0, 4) as g:
                group(b, g)
        out_stage(chip, at.outT, b, chunks, bo, chip.state, chip.inner)
    norm_stage(chip, chip.inner, chip.state, (P, P), B * S, 1e-5)


def shift_stage(chip, src, dst, add=None):
    nc, sig = chip.nc, chip.stage("small")
    with nc.Block() as block:
        @block.gpsimd
        def _(pool):
            chip.reset_others(pool, sig)

        @block.vector
        def _(dve):
            for b in range(B):
                dve.memset(dst[:, 1, b * S:b * S + 1], 0.0)
                dve.tensor_copy(dst[:, 1, b * S + 1:(b + 1) * S], src[:, 1, b * S:(b + 1) * S - 1])
            dve.tensor_copy(dst[:, 0, :], src[:, 0, :]).then_inc(sig["dve_done"], 1)


def copy_stage(chip, src, dst):
    nc, sig = chip.nc, chip.stage("small")
    with nc.Block() as block:
        @block.gpsimd
        def _(pool):
            chip.reset_others(pool, sig)

        @block.vector
        def _(dve):
            dve.tensor_copy(dst[:, :, :], src[:, :, :]).then_inc(sig["dve_done"], 1)


def gated_stage(chip, x, tiles, act_func, dst, addend, bias_loads=(), bias=None, out_bias=None,
                spread=None):
    nc, sig = chip.nc, chip.stage("gated")
    RING, halves = 4, B * S // BANK
    gate_up = chip.carve(0, RING, 2, 2 * P)
    down = chip.carve(2048, RING, D)
    acted = chip.carve(3072, 2, BANK)
    hidden = chip.carve(4096, 2, BANK)
    weighted = chip.carve(5120, 2, BANK)
    units = [(f, h) for f in range(len(tiles)) for h in range(halves)]
    gate_ps, up_ps, spread_ps = chip.psum[:, 4], chip.psum[:, 5], chip.psum[:, 6]
    sums = [[chip.psum[:, 2 * m + h] for h in range(halves)] for m in range(2)]
    made = hidden if spread is None else weighted
    with nc.Block() as block:
        @block.gpsimd
        def _(pool):
            chip.reset_others(pool, sig)

        @block.sync
        def _(sp):
            for to, frm in bias_loads:
                sp.dma_start(to, frm).then_inc(sig["bias_loaded"], 16)
            for f, (rows, loads) in enumerate(tiles):
                if f >= RING:
                    sp.wait_ge(sig["tile_done"], f - RING + 1)
                for to, frm in loads(gate_up[:, f % RING], down[:, f % RING]):
                    sp.dma_start(to, frm).then_inc(sig[f"slot{f % RING}_loaded"], 16)

        @block.tensor
        def _(pe):
            def down_products(u):
                f, h = units[u]
                rows = tiles[f][0]
                pe.wait_ge(sig["hidden_ready"], u + 1)
                for m in range(2):
                    mm = pe.matmul(sums[m][h], down[:rows, f % RING, m * P:(m + 1) * P],
                                   made[:rows, u % 2], start=f == 0, stop=f == len(tiles) - 1)
                if h == halves - 1:
                    mm.then_inc(sig["tile_done"], 1)

            for u, (f, h) in enumerate(units):
                rows, loads = tiles[f]
                if h == 0:
                    n = len(loads(gate_up[:, 0], down[:, 0]))
                    pe.wait_ge(sig[f"slot{f % RING}_loaded"], 16 * n * (f // RING + 1))
                cols = slice(h * BANK, (h + 1) * BANK)
                if u >= 1:
                    pe.wait_ge(sig["gate_acted"], u)
                for c in range(2):
                    mm = pe.matmul(gate_ps[:rows], gate_up[:, f % RING, c, 0:rows], x[:, c, cols],
                                   start=c == 0, stop=c == 1)
                mm.then_inc(sig["gate_ready"], 1)
                if u >= 1:
                    pe.wait_ge(sig["hidden_ready"], u)
                for c in range(2):
                    mm = pe.matmul(up_ps[:rows], gate_up[:, f % RING, c, P:P + rows],
                                   x[:, c, cols], start=c == 0, stop=c == 1)
                if spread is not None:
                    sel, combine = spread(f, cols)
                    mm = pe.matmul(spread_ps[:rows], sel, combine, start=True, stop=True)
                mm.then_inc(sig["up_ready"], 1)
                if u >= 1:
                    down_products(u - 1)
            down_products(len(units) - 1)

        @block.scalar
        def _(act):
            if bias_loads:
                act.wait_ge(sig["bias_loaded"], 16 * len(bias_loads))
            for u, (f, h) in enumerate(units):
                rows = tiles[f][0]
                act.wait_ge(sig["gate_ready"], u + 1)
                if u >= 2:
                    act.wait_ge(sig["hidden_ready"], u - 1)
                act.activation(acted[:rows, u % 2], gate_ps[:rows], act_func,
                               bias=0.0 if bias is None else bias[0][:rows, f:f + 1]
                               ).then_inc(sig["gate_acted"], 1)

        @block.vector
        def _(dve):
            order = Order(dve, sig["order"])
            if bias_loads:
                dve.wait_ge(sig["bias_loaded"], 16 * len(bias_loads))
            for u, (f, h) in enumerate(units):
                rows = tiles[f][0]
                dve.wait_ge(sig["up_ready"], u + 1)
                dve.wait_ge(sig["gate_acted"], u + 1)
                if u >= 2 * halves:
                    dve.wait_ge(sig["tile_done"], (u - 2) // halves)
                if bias is None:
                    ins = dve.tensor_tensor(hidden[:rows, u % 2], up_ps[:rows],
                                            acted[:rows, u % 2], ALU.mult)
                else:
                    ins = dve.scalar_tensor_tensor(hidden[:rows, u % 2], up_ps[:rows],
                                                   bias[1][:rows, f:f + 1], acted[:rows, u % 2],
                                                   ALU.add, ALU.mult)
                if spread is not None:
                    order(ins)
                    ins = dve.tensor_tensor(weighted[:rows, u % 2], spread_ps[:rows],
                                            hidden[:rows, u % 2], ALU.mult)
                ins.then_inc(sig["hidden_ready"], 1)
            dve.wait_ge(sig["tile_done"], len(tiles))
            for m in range(2):
                for h in range(halves):
                    cols = slice(h * BANK, (h + 1) * BANK)
                    if addend is None:
                        dve.tensor_copy(dst[:, m, cols], sums[m][h])
                    elif out_bias is None:
                        dve.tensor_tensor(dst[:, m, cols], sums[m][h], addend[:, m, cols], ALU.add)
                    else:
                        dve.scalar_tensor_tensor(dst[:, m, cols], sums[m][h],
                                                 out_bias[:, m:m + 1], addend[:, m, cols],
                                                 ALU.add, ALU.add)


def layer0_ffn(chip, a):
    depth, inner = 6, 1024
    hidden = 682
    at = Attention(chip, 64, 64, NT, 8.0, "band")
    (q_cos, q_sin), (k_cos, k_sin) = chip.tables(64, 0), chip.tables(64, 1)
    tables = [(q_cos, "xpos_q_cos"), (q_sin, "xpos_q_sin"), (k_cos, "xpos_k_cos"),
              (k_sin, "xpos_k_sin")]
    copy_stage(chip, chip.state, chip.inner)
    load_stage(chip, [(t, a[n].rearrange("p (t e) -> p t e", t=NT)) for t, n in tables]
               + [(chip.masks[:, :], a["mask_band65"])])
    masks = (chip.masks[:, 0:256], chip.masks[:, 256:512])
    h = chip.inner
    q_gain, k_gain = chip.gains[:, 0:64], chip.gains[:, 64:128]
    b2, b1 = chip.gains[:, 128:130], chip.gains[:, 130:142]
    ln_g, ln_b = chip.gains[:, 142:144], chip.gains[:, 144:146]
    with chip.nc.Fori(0, depth) as d:
        shift_stage(chip, h, chip.normed)
        load_stage(chip, [
            (chip.w_out[:, :, :], a["L0_ffn_Wo"][bass.ds(d, 1)].rearrange(
                "o (c p) n -> p (o c) n", p=P)),
            (q_gain, a["L0_ffn_q_scale"][bass.ds(d, 1)].partition_broadcast(P)),
            (k_gain, a["L0_ffn_k_scale"][bass.ds(d, 1)].partition_broadcast(P)),
            (b2, a["L0_ffn_b2_col"][:, bass.ds(2 * d, 2)]),
            (ln_g, a["L0_ffn_ln_g_col"][:, bass.ds(2 * d, 2)]),
            (ln_b, a["L0_ffn_ln_b_col"][:, bass.ds(2 * d, 2)]),
            (b1, a["L0_ffn_b1_col"][:, bass.ds(12 * d, 12)])])
        fill_slots_stage(chip, at)
        for b in range(B):
            with chip.nc.Fori(0, inner // D) as g:
                jobs = []
                for t in range(NT):
                    tok = slice(b * S + t * P, b * S + (t + 1) * P)
                    products = []
                    for lo, hi in ((0, BANK), (BANK, 3 * D)):
                        products += [(chip.normed[:, c, tok], chip.w_in[:, c, lo:hi], lo, c == 0,
                                      c == 1) for c in range(2)]
                    jobs.append((products, [
                        (at.raw_q[:, t * D:(t + 1) * D], lambda ps: ps[:, 0:D]),
                        (at.raw_k[:, t * D:(t + 1) * D], lambda ps: ps[:, D:2 * D])]
                        + [(dst, lambda ps, which=which: ps[:, 2 * D:3 * D].rearrange(
                            "p (h e) -> p h e", e=64)[:, which])
                           for dst, which in at.value_parts(t)]))
                norm = (1.0, 0.0, 1e-12, 1.0)
                q_post = HeadPost(chip, at, at.raw_q, at.q, NT, 4, norm, q_gain, q_cos, q_sin)
                k_post = HeadPost(chip, at, at.raw_k, at.k, NT, 4, norm, k_gain, k_cos, k_sin)
                w = a["L0_ffn_Wqkv_groups"][bass.ds(d * 4 + g, 1)].rearrange(
                    "o (c p) n -> p (o c) n", p=P)
                project_stage(chip, [(chip.w_in[:, :, :], w)], jobs, q_post, k_post)
                attend_stage(chip, at, g * 2, masks)
            out_stage(chip, at.outT, b, 8, None, h, h)
        shift_stage(chip, h, chip.normed)
        norm_stage(chip, chip.normed, chip.normed, (P, P), B * S, 1e-5, gain=ln_g, shift=ln_b)
        tiles = []
        for f in range(6):
            rows = min(P, hidden - f * P)
            w1 = a["L0_ffn_W1"][bass.ds(d, 1)].rearrange("o (c p) n -> p (o c) n", p=P)
            w2 = a["L0_ffn_W2"][bass.ds(d, 1), f * P:f * P + rows].rearrange("o p n -> p (o n)")

            def loads(gate_up, down, f=f, rows=rows, w1=w1, w2=w2):
                return [(gate_up[:, :, 0:rows], w1[:, :, hidden + f * P:hidden + f * P + rows]),
                        (gate_up[:, :, P:P + rows], w1[:, :, f * P:f * P + rows]),
                        (down[:rows], w2)]

            tiles.append((rows, loads))
        gated_stage(chip, chip.normed, tiles, ACT.Gelu, h, h, bias=(b1[:, 6:12], b1[:, 0:6]),
                    out_bias=b2)
    norm_stage(chip, chip.state, chip.state, (P, P), B * S, 1e-5, add=h)


def build(nc, a, out, upto=12):
    chip = Chip(nc)
    start_stage(chip, [(chip.state[:, :, :], a["x_fm"].rearrange("(c p) n -> p c n", p=P)),
                       (chip.ident[:, :], a["ident"]), (chip.ident_bf[:, :], a["ident_bf"]),
                       (chip.pick_sum[:, :], a["pick_sum"]),
                       (chip.pick_shift[:, :], a["pick_shift"])]
                + ctx_loads(chip.ctx, a["ctx_fm"]))
    for layer in LAYERS[:upto]:
        layer(chip, a)
    store_stage(chip, out)


def store_stage(chip, out):
    nc, sig = chip.nc, chip.stage("small")
    with nc.Block() as block:
        @block.gpsimd
        def _(pool):
            chip.reset_others(pool, sig)

        @block.sync
        def _(sp):
            sp.dma_start(out.rearrange("(c p) n -> p c n", p=P),
                         chip.state[:, :, :]).then_inc(sig["weights_loaded"], 16)
            sp.wait_ge(sig["weights_loaded"], 16)


def layer0_cross(chip, a):
    cross_attention(chip, a, "L0_xattn_", 16)


def layer1_cross(chip, a):
    cross_attention(chip, a, "L1_xattn_", 64)


def layer1_linear_attention(chip, a):
    pre, feats = "L1_attn_", 64
    bo = chip.gains[:, 0:2]
    heads_out = chip.carve(19800, NT, D)
    outT = chip.carve(21000, 2, BANK)
    qkT = chip.carve(0, 4, BANK)
    sq = chip.carve(2048, 4, BANK)
    v = chip.carve(4096, NT, 16 * 17).rearrange("p t (h e) -> p t h e", e=17)
    phi = chip.carve(5184, 2, NT * 16, feats)
    shifted = chip.carve(13376, 2, 8, feats)
    phi_qT = chip.carve(14400, 8, BANK)
    kv = chip.carve(18496, 8, 34)
    proj = chip.carve(18768, 2, BANK)
    top = chip.cols[:, 0:16].rearrange("p (n h) -> p n h", h=8)
    down = chip.cols[:, 16:32].rearrange("p (n h) -> p n h", h=8)
    head_sum = chip.cols[:, 32:40]
    nc = chip.nc
    load_stage(chip, [(chip.w_in[:, :, i * D:(i + 1) * D], fm(a[pre + n + "_t"]))
                      for i, n in enumerate(("Wq", "Wk", "Wv"))]
               + [(chip.w_out[:, 0:2, :], fm(a[pre + "Wo_t"])), (bo, a[pre + "bo_col"]),
                  (proj, a["L1_attn_proj_diag"].rearrange("c p n -> p c n")),
                  (head_sum, a["head_sum"])])

    def features_stage():
        sig = chip.stage("features")
        units = [(i, t, c) for i in range(2) for t in range(NT) for c in range(2)]
        with nc.Block() as block:
            @block.gpsimd
            def _(pool):
                chip.reset_others(pool, sig)
                pool.memset(kv, 0.0).then_inc(sig["cleared"], 1)

            @block.tensor
            def _(pe):
                pe.wait_ge(sig["squares_ready"], 4)
                for u, (i, t, c) in enumerate(units):
                    if u >= 4:
                        pe.wait_ge(sig["shifted_ready"], u - 3)
                    tok = slice(t * P, (t + 1) * P)
                    pe.matmul(chip.psum[:, 4 + u % 4, 0:8], sq[:, 2 * i + c, tok], head_sum,
                              start=True, stop=True)
                    pe.matmul(chip.psum[:, u % 4], qkT[:, 2 * i + c, tok], proj[:, c],
                              start=True, stop=True).then_inc(sig["logits_ready"], 1)

            @block.scalar
            def _(act):
                for n in range(4):
                    act.activation(sq[:, n], qkT[:, n], ACT.Square
                                   ).then_inc(sig["squares_ready"], 1)
                for u, (i, t, c) in enumerate(units):
                    act.wait_ge(sig["shifted_ready"], u + 1)
                    out = phi[:, i, t * 16 + c * 8:t * 16 + c * 8 + 8]
                    act.activation(out, shifted[:, u % 2], ACT.Exp,
                                   scale=0.25).then_inc(sig["exp_ready"], 1)

            @block.vector
            def _(dve):
                order = Order(dve, sig["order"])
                for u, (i, t, c) in enumerate(units):
                    dve.wait_ge(sig["logits_ready"], u + 1)
                    logits = chip.psum[:, u % 4].rearrange("p (h m) -> p h m", m=feats)
                    if u >= 2:
                        dve.wait_ge(sig["exp_ready"], u - 1)
                    order(dve.tensor_reduce(top[:, u % 2], logits, AX, ALU.max))
                    order(dve.scalar_tensor_tensor(down[:, u % 2], chip.psum[:, 4 + u % 4, 0:8],
                                                   0.125, top[:, u % 2], ALU.mult, ALU.add))
                    dve.tensor_tensor(shifted[:, u % 2], logits,
                                      down[:, u % 2].unsqueeze(2).to_broadcast([P, 8, feats]),
                                      ALU.subtract).then_inc(sig["shifted_ready"], 1)
                dve.wait_ge(sig["exp_ready"], len(units))
                dve.tensor_scalar(phi, phi, 1e-6, 0.125, ALU.add,
                                  ALU.mult).then_inc(sig["phi_ready"], 1)

    def sums_stage():
        sig = chip.stage("small")
        with nc.Block() as block:
            @block.gpsimd
            def _(pool):
                chip.reset_others(pool, sig)

            @block.tensor
            def _(pe):
                for p in range(8):
                    for t in range(NT):
                        lhs = phi[:, 1, t * 16 + 2 * p:t * 16 + 2 * p + 2].rearrange(
                            "p h m -> p (h m)")
                        mm = pe.matmul(chip.psum[:, 0, p * 34:(p + 1) * 34], lhs,
                                       v[:, t, 2 * p:2 * p + 2].rearrange("p h e -> p (h e)"),
                                       start=t == 0, stop=t == NT - 1)
                mm.then_inc(sig["pe_done"], 1)

            @block.vector
            def _(dve):
                dve.wait_ge(sig["pe_done"], 1)
                made = chip.psum[:, 0, 0:8 * 34].rearrange("p (n e) -> p n e", e=34)
                for i in range(2):
                    r, c = slice(64 * i, 64 * i + 64), slice(17 * i, 17 * i + 17)
                    dve.tensor_copy(kv[r, :, c], made[r, :, c]).then_inc(sig["dve_done"], 1)

    def values_stage():
        sig = chip.stage("small")
        sums = chip.roots[:, 0:16].unsqueeze(2)
        with nc.Block() as block:
            @block.gpsimd
            def _(pool):
                chip.reset_others(pool, sig)

            @block.tensor
            def _(pe):
                for t in range(NT):
                    for p in range(8):
                        mm = pe.matmul(chip.psum[:, t, p * 34:(p + 1) * 34],
                                       phi_qT[:, p, t * P:(t + 1) * P], kv[:, p],
                                       start=True, stop=True)
                    mm.then_inc(sig["pe_done"], 1)

            @block.vector
            def _(dve):
                order = Order(dve, sig["order"])
                for t in range(NT):
                    dve.wait_ge(sig["pe_done"], t + 1)
                    made = chip.psum[:, t, 0:16 * 17].rearrange("p (h e) -> p h e", e=17)
                    order(dve.tensor_scalar(sums, made[:, :, 16:17], 1e-6, None, ALU.add))
                    order(dve.reciprocal(sums, sums))
                    out = heads_out[:, t].rearrange("p (h e) -> p h e", e=16)
                    order(dve.tensor_tensor(out, made[:, :, 0:16],
                                            sums.to_broadcast([P, 16, 16]), ALU.mult))

    for b in range(B):
        cols = slice(b * S, (b + 1) * S)
        linear_stage(chip, [], [
            (qkT[:, 2 * i + m], [(chip.w_in[:, c, i * D + m * P:i * D + (m + 1) * P],
                                  chip.state[:, c, cols]) for c in range(2)], None, None)
            for i in range(2) for m in range(2)])
        ones_stage(chip, v)
        jobs = []
        for t in range(NT):
            tok = slice(b * S + t * P, b * S + (t + 1) * P)
            jobs.append(([(chip.state[:, c, tok], chip.w_in[:, c, 2 * D:3 * D], 0, c == 0, c == 1)
                          for c in range(2)],
                         [(v[:, t, :, 0:16], lambda ps: ps[:, 0:D].rearrange(
                             "p (h e) -> p h e", e=16))]))
        project_stage(chip, [], jobs)
        features_stage()
        turn_stage(chip, [([(phi[:, 0, t * 16 + 2 * p:t * 16 + 2 * p + 2].rearrange(
            "p h m -> p (h m)"), t * P) for t in range(NT)], phi_qT[:, p]) for p in range(8)])
        sums_stage()
        values_stage()
        turn_stage(chip, [([(heads_out[:, t, c * P:(c + 1) * P], t * P) for t in range(NT)],
                           outT[:, c]) for c in range(2)])
        out_stage(chip, outT, b, 2, bo, chip.state, chip.inner)
    norm_stage(chip, chip.inner, chip.state, (P, P), B * S, 1e-5)


def ones_stage(chip, v):
    nc, sig = chip.nc, chip.stage("small")
    with nc.Block() as block:
        @block.gpsimd
        def _(pool):
            chip.reset_others(pool, sig)
            pool.memset(v, 1.0).then_inc(sig["pool_done"], 1)


ROUND = 1.5 * 2 ** 23


def quantize_steps(order, dve, out, t, inverse, scale, low, high):
    order(dve.tensor_scalar(out, t, inverse, ROUND, ALU.mult, ALU.add))
    order(dve.tensor_scalar(out, out, ROUND, high, ALU.subtract, ALU.min))
    order(dve.tensor_scalar(out, out, low, scale, ALU.max, ALU.mult))


def quantize_activation_stage(chip, src, dst, times=None, then=None):
    nc, sig = chip.nc, chip.stage("quantize")
    top, inverse, scale = (chip.cols[:, i:i + 1] for i in range(3))
    with nc.Block() as block:
        @block.gpsimd
        def _(pool):
            chip.reset_others(pool, sig)
            pool.wait_ge(sig["row_max"], 1)
            pool.partition_all_reduce(scale, top, P, bass.bass_isa.ReduceOp.max
                                      ).then_inc(sig["all_max"], 1)

        @block.vector
        def _(dve):
            order = Order(dve, sig["order"])
            if times is not None:
                order(dve.tensor_tensor(src, src, times, ALU.mult))
            dve.tensor_reduce(top, src, mybir.AxisListType.XY, ALU.max,
                              apply_absolute_value=True).then_inc(sig["row_max"], 1)
            dve.wait_ge(sig["all_max"], 1)
            order(dve.tensor_scalar(scale, scale, 1.0 / 32767.0, 1e-12, ALU.mult, ALU.max))
            order(dve.reciprocal(inverse, scale))
            quantize_steps(order, dve, dst, src, inverse, scale, -32768.0, 32767.0)
            if then is not None:
                sigmoid = then
                dve.wait_ge(sig["sigmoid_ready"], 1)
                order(dve.tensor_scalar(sigmoid, sigmoid, 65536.0, ROUND, ALU.mult, ALU.add))
                order(dve.tensor_scalar(sigmoid, sigmoid, ROUND, 65535.0, ALU.subtract, ALU.min))
                order(dve.tensor_scalar(sigmoid, sigmoid, 0.0, 2.0 ** -16, ALU.max, ALU.mult))
                order(dve.tensor_tensor(dst, dst, sigmoid, ALU.mult))

        @block.scalar
        def _(act):
            if then is not None:
                act.wait_ge(sig["order"], 5 + (times is not None))
                act.activation(then, dst, ACT.Sigmoid).then_inc(sig["sigmoid_ready"], 1)


def layer1_ffn(chip, a):
    wide, blk = 768, 32
    w_raw = chip.carve(0, 6, D)
    w_gate_t, w_up_t = chip.carve(1536, 2, wide), chip.carve(3072, 2, wide)
    w_down_t = chip.carve(4608, 6, D)
    gate, up, sigmoid = (chip.carve(6144 + 6144 * i, 6, B * S) for i in range(3))
    steps = chip.cols[:, 0:48].unsqueeze(2)
    inverse = chip.roots[:, 0:48].unsqueeze(2)
    nc = chip.nc

    def weight_stage(name):
        sig = chip.stage("small")
        w = a["L1_ffn_" + name].rearrange("(c p) n -> p c n", p=P)
        raw = w_raw.rearrange("p a b -> p (a b)")[:, 0:6 * D].rearrange(
            "p (c n) -> p c n", n=w.shape[2])
        blocks = w_raw.rearrange("p a (n e) -> p (a n) e", e=blk)
        with nc.Block() as block:
            @block.gpsimd
            def _(pool):
                chip.reset_others(pool, sig)

            @block.sync
            def _(sp):
                sp.dma_start(raw, w).then_inc(sig["weights_loaded"], 16)

            @block.vector
            def _(dve):
                order = Order(dve, sig["order"])
                dve.wait_ge(sig["weights_loaded"], 16)
                order(dve.tensor_reduce(steps, blocks, AX, ALU.max, apply_absolute_value=True))
                order(dve.tensor_scalar(steps, steps, 1.0 / 7.0, 1e-12, ALU.mult, ALU.max))
                order(dve.reciprocal(inverse, steps))
                order(dve.tensor_tensor(blocks, blocks, inverse.to_broadcast([P, 48, blk]),
                                        ALU.mult))
                order(dve.tensor_scalar(blocks, blocks, ROUND, ROUND, ALU.add, ALU.subtract))
                order(dve.tensor_scalar(blocks, blocks, -8.0, 7.0, ALU.max, ALU.min))
                order(dve.tensor_tensor(blocks, blocks, steps.to_broadcast([P, 48, blk]),
                                        ALU.mult))
        return raw

    for name, dst in (("w_gate", w_gate_t), ("w_up", w_up_t)):
        raw = weight_stage(name)
        turn_stage(chip, [([(raw[:, o, c * P:(c + 1) * P], (o % 3) * P)
                            for o in range(o0, o0 + 3)], dst[:, c, o0 * P:(o0 + 3) * P])
                          for c in range(2) for o0 in (0, 3)])
    raw = weight_stage("w_down")
    turn_stage(chip, [([(raw[:, o, c * P:(c + 1) * P], o * P) for o in range(2)], w_down_t[:, c])
                      for c in range(6)])
    quantize_activation_stage(chip, chip.state[:, :, :], chip.normed[:, :, :])
    for w, dst in ((w_gate_t, gate), (w_up_t, up)):
        linear_stage(chip, [], [(dst[:, f, h * BANK:(h + 1) * BANK],
                                 [(w[:, c, f * P:(f + 1) * P],
                                   chip.normed[:, c, h * BANK:(h + 1) * BANK]) for c in range(2)],
                                 None, None) for f in range(6) for h in range(2)])
        quantize_activation_stage(chip, dst, dst, then=sigmoid if dst is gate else None)
    quantize_activation_stage(chip, gate, gate)
    quantize_activation_stage(chip, gate, gate, times=up)
    linear_stage(chip, [], [(chip.inner[:, m, h * BANK:(h + 1) * BANK],
                             [(w_down_t[:, f, m * P:(m + 1) * P],
                               gate[:, f, h * BANK:(h + 1) * BANK]) for f in range(6)],
                             None, chip.state[:, m, h * BANK:(h + 1) * BANK])
                            for m in range(2) for h in range(2)])
    norm_stage(chip, chip.inner, chip.state, (P, P), B * S, 1e-5)


def layer2_attention(chip, a):
    pre, virtual = "L2_attn_", 16
    at = Attention(chip, 32, 16, NT + 1, 32 ** -0.5, "ahead", virtual)
    virtual_k = chip.virtual_k[:, 0:D]
    cos, sin = chip.tables(32)
    fill_slots_stage(chip, at)
    load_stage(chip, [(cos, a["rope_l2_cos"].rearrange("p (t e) -> p t e", t=NT)),
                      (sin, a["rope_l2_sin"].rearrange("p (t e) -> p t e", t=NT)),
                      (chip.masks[:, :], a["mask_ahead"]),
                      (chip.w_out[:, 0:8, :], fm(a[pre + "W_O_slots"]))])
    masks = (chip.masks[:, 0:256], chip.masks[:, 256:512])
    for b in range(B):
        with chip.nc.Fori(0, 4) as g:
            loads = [
                (chip.w_in[:, :, 0:640], a[pre + "W_groups"][bass.ds(g, 1)].rearrange(
                    "o (c p) n -> p (o c) n", p=P)),
                (chip.w_bias[:, 0:640], a[pre + "b_groups"][bass.ds(g, 1)]),
                (virtual_k.rearrange("p (h e) -> p h e", e=32),
                 a[pre + "virtual_k"][:, bass.ds(g * 8, 8), :]),
                (at.v[0:virtual, NT, :, 0:16], a[pre + "virtual_v"].rearrange(
                    "k (h e) o -> k h (e o)", e=16)[:, bass.ds(g * 8, 8), :])]
            jobs = []
            for t in range(NT):
                tok = slice(b * S + t * P, b * S + (t + 1) * P)
                products = []
                for lo, hi in ((0, BANK), (BANK, 640)):
                    products += [(chip.state[:, c, tok], chip.w_in[:, c, lo:hi], lo, c == 0,
                                  False) for c in range(2)]
                    products.append((chip.ones[:, 0:P], chip.w_bias[:, lo:hi], lo, False, True))
                jobs.append((products, [
                    (at.raw_q[:, t * D:(t + 1) * D], lambda ps: ps[:, 0:D]),
                    (at.raw_k[:, t * D:(t + 1) * D], lambda ps: ps[:, D:2 * D]),
                    (at.v[:, t, :, 0:16], lambda ps: ps[:, 2 * D:2 * D + P].rearrange(
                        "p (h e) -> p h e", e=16))]))
            q_post = HeadPost(chip, at, at.raw_q, at.q, NT, 8, None, None, cos, sin)
            k_post = HeadPost(chip, at, at.raw_k, at.k, NT, 8, None, None, cos, sin)
            project_stage(chip, loads, jobs, q_post, k_post)
            split_stage(chip, at, split_jobs(at, at.raw_q, at.q, NT, 8, at.Q_PARTS)
                        + split_jobs(at, at.raw_k, at.k, NT, 8, at.K_PARTS)
                        + [(virtual_k.rearrange("p (h e) -> p h e", e=32), at.k[:virtual, NT],
                            at.K_PARTS)])
            attend_stage(chip, at, g * 2, masks)
        out_stage(chip, at.outT, b, 8, None, chip.state, chip.inner)
    norm_stage(chip, chip.inner, chip.state, (P, P), B * S, 1e-5)


def layer2_cross(chip, a):
    pre = "L2_xattn_"
    tiles = SC // P + NT
    g = chip.gains
    norm_stage(chip, chip.ctx, chip.ctx, (P, DC - P), B * SC, 1e-5, gain=g[:, 0:2],
               shift=g[:, 2:4], loads=[(g[:, 0:2], a[pre + "ln_x_g_col"]),
                                       (g[:, 2:4], a[pre + "ln_x_b_col"])])
    at = Attention(chip, 64, 64, tiles, 1.0)
    bo, q_gain, k_gain = g[:, 0:2], g[:, 6:70], g[:, 70:134]
    key_cols = g[:, 134:146]
    norm_stage(chip, chip.state, chip.normed, (P, P), B * S, 1e-5, gain=g[:, 2:4],
               shift=g[:, 4:6], loads=[(g[:, 2:4], a[pre + "ln_l_g_col"]),
                                       (g[:, 4:6], a[pre + "ln_l_b_col"])])
    fill_slots_stage(chip, at)
    w_ctx = chip.w_out[:, 4:8, :].rearrange("p a b -> p (a b)").rearrange("p (c n) -> p c n", c=2)
    load_stage(chip, [(chip.w_in[:, :, 0:D], fm(a[pre + "Wq_t"])),
                      (chip.w_in[:, :, D:3 * D], fm(a[pre + "Wlkv_t"])),
                      (chip.w_out[:, 0:2, :], fm(a[pre + "Wo_t"])),
                      (bo, a[pre + "bo_col"]),
                      (q_gain, a[pre + "qn_g"].unsqueeze(0).partition_broadcast(P)),
                      (k_gain, a[pre + "kn_g"].unsqueeze(0).partition_broadcast(P)),
                      (chip.mask_cols[:, :], a["mask_cols"])] + ctx_loads(w_ctx, a[pre + "Wkv_t"]))
    nc = chip.nc

    def key_bias_stage(b):
        sig = chip.stage("small")
        with nc.Block() as block:
            @block.gpsimd
            def _(pool):
                chip.reset_others(pool, sig)

            @block.vector
            def _(dve):
                order = Order(dve, sig["order"])
                order(dve.tensor_scalar(key_cols[:, 0:8], chip.mask_cols[:, b * 8:(b + 1) * 8],
                                        BIG, -BIG, ALU.mult, ALU.add))
                order(dve.tensor_copy(
                    at.k[:, 0:8, :, at.bias_at],
                    key_cols[:, 0:8].unsqueeze(2).to_broadcast([P, 8, at.heads])))

    for b in range(B):
        key_bias_stage(b)
        for part in range(3):
            jobs = []
            for t in range(NT):
                if part < 2:
                    tok = slice(b * SC + (part * NT + t) * P, b * SC + (part * NT + t + 1) * P)
                    products = [(chip.ctx[:r, c, tok], w_ctx[:r, c], 0, c == 0, c == 1)
                                for c, r in ((0, P), (1, DC - P))]
                else:
                    tok = slice(b * S + t * P, b * S + (t + 1) * P)
                    products = [(chip.normed[:, c, tok], chip.w_in[:, c, D:3 * D], 0, c == 0,
                                 c == 1) for c in range(2)]
                    products += [(chip.normed[:, c, tok], chip.w_in[:, c, 0:D], BANK, c == 0,
                                  c == 1) for c in range(2)]
                copies = [(at.raw_k[:, t * D:(t + 1) * D], lambda ps: ps[:, 0:D]),
                          ] + [(dst, lambda ps, which=which: ps[:, D:2 * D].rearrange(
                              "p (h e) -> p h e", e=64)[:, which])
                               for dst, which in at.value_parts(part * NT + t)]
                if part == 2:
                    copies.append((at.raw_q[:, t * D:(t + 1) * D],
                                   lambda ps: ps[:, BANK:BANK + D]))
                jobs.append((products, copies))
            q_post = HeadPost(chip, at, at.raw_q, at.q, NT, 4, (1.0 / 64, 0.0, 1e-8, 0.125),
                              q_gain) if part == 2 else None
            k_post = HeadPost(chip, at, at.raw_k, at.k[:, part * NT:(part + 1) * NT], NT, 4,
                              (1.0 / 64, 0.0, 1e-8, 1.0), k_gain)
            project_stage(chip, [], jobs, q_post, k_post)
        attend_stage(chip, at, 0)
        out_stage(chip, at.outT, b, 2, bo, chip.state, chip.inner)
    norm_stage(chip, chip.inner, chip.state, (P, P), B * S, 1e-5)
    load_stage(chip, ctx_loads(chip.ctx, a["ctx_fm"]))


def rank_steps(order, dve, values, work, work2, ties, rank, n):
    tiles = B * NT
    for t in range(tiles):
        v = values[:, t]
        mine = v.unsqueeze(2).to_broadcast([P, n, n])
        other = v.unsqueeze(1).to_broadcast([P, n, n])
        w = work[:, t * n * n:(t + 1) * n * n].rearrange("p (i j) -> p i j", j=n)
        w2 = work2[:, t * n * n:(t + 1) * n * n].rearrange("p (i j) -> p i j", j=n)
        dve.tensor_tensor(w, other, mine, ALU.is_gt)
        ins = dve.tensor_tensor(w2, other, mine, ALU.is_equal)
    order(ins)
    m = tiles * n * n
    tie = ties.unsqueeze(1).to_broadcast([P, tiles, n * n])
    order(dve.tensor_tensor(work2[:, :m].rearrange("p (t e) -> p t e", t=tiles),
                            work2[:, :m].rearrange("p (t e) -> p t e", t=tiles), tie, ALU.mult))
    order(dve.tensor_tensor(work[:, :m], work[:, :m], work2[:, :m], ALU.add))
    order(dve.tensor_reduce(rank, work[:, :m].rearrange("p (t j) -> p t j", j=n), AX, ALU.add))


def router_logits_stage(chip, logits, router, loads, n):
    nc, sig = chip.nc, chip.stage("small")
    with nc.Block() as block:
        @block.gpsimd
        def _(pool):
            chip.reset_others(pool, sig)

        @block.sync
        def _(sp):
            for dst, src in loads:
                sp.dma_start(dst, src).then_inc(sig["weights_loaded"], 16)

        @block.tensor
        def _(pe):
            pe.wait_ge(sig["weights_loaded"], 16 * len(loads))
            for t in range(B * NT):
                for c in range(2):
                    mm = pe.matmul(chip.psum[:, 0, t * n:(t + 1) * n],
                                   chip.state[:, c, t * P:(t + 1) * P], router[:, c],
                                   start=c == 0, stop=c == 1)
            mm.then_inc(sig["pe_done"], 1)

        @block.vector
        def _(dve):
            dve.wait_ge(sig["pe_done"], 1)
            dve.tensor_copy(logits, chip.psum[:, 0, 0:B * NT * n].rearrange(
                "p (t e) -> p t e", e=n)).then_inc(sig["dve_done"], 1)


def turn_combine(chip, combine, combine_t, n):
    turn_stage(chip, [([(combine[:, 4 * q + t, :], t * P) for t in range(4)],
                       combine_t[:n, q * BANK:(q + 1) * BANK]) for q in range(2)])


def layer2_ffn(chip, a):
    pre, n, groups, tiles = "L2_ffn_", 16, 4, B * NT
    router = chip.carve(8192, 2, n)
    logits, scores, biased = (chip.carve(8224 + i * tiles * n, tiles, n) for i in range(3))
    bias = chip.carve(8608, n)
    ties = chip.carve(8624, n * n)
    ties4 = chip.carve(8880, groups * groups)
    sel = chip.carve(8896, 12, P)
    combine = chip.carve(10432, tiles, n + 1)
    combine_t = chip.carve(10568, B * S)
    group_score, group_rank = (chip.carve(11592 + 32 * i, tiles, groups) for i in range(2))
    pair = chip.carve(11656, tiles * groups)
    rank = chip.carve(11688, tiles * n)
    work, work2 = chip.carve(11816, 2048), chip.carve(13864, 2048)
    total = chip.carve(15912, tiles, 1)
    router_logits_stage(chip, logits, router, [
        (router, fm(a[pre + "router_w_t"])),
        (bias, a[pre + "correction_bias"].unsqueeze(0).partition_broadcast(P)),
        (ties, a["ties16"].partition_broadcast(P)), (ties4, a["ties4"].partition_broadcast(P)),
        (sel[:n + 1], a["sel_l2"])], n)
    nc, sig = chip.nc, chip.stage("route")
    with nc.Block() as block:
        @block.gpsimd
        def _(pool):
            chip.reset_others(pool, sig)

        @block.scalar
        def _(act):
            act.activation(scores, logits, ACT.Sigmoid).then_inc(sig["scores_ready"], 1)

        @block.vector
        def _(dve):
            order = Order(dve, sig["order"])
            dve.wait_ge(sig["scores_ready"], 1)
            order(dve.tensor_tensor(biased, scores,
                                    bias.unsqueeze(1).to_broadcast([P, tiles, n]), ALU.add))
            quads = biased.rearrange("p t (g e) -> p (t g) e", e=4)
            best = group_score.rearrange("p t g -> p (t g)").unsqueeze(2)
            one = pair.unsqueeze(2)
            order(dve.tensor_tensor(best, quads[:, :, 0:1], quads[:, :, 1:2], ALU.add))
            for i, j in ((0, 2), (0, 3), (1, 2), (1, 3), (2, 3)):
                order(dve.tensor_tensor(one, quads[:, :, i:i + 1], quads[:, :, j:j + 1], ALU.add))
                order(dve.tensor_tensor(best, best, one, ALU.max))
            rank_steps(order, dve, group_score, work, work2, ties4,
                       group_rank.rearrange("p t g -> p (t g)"), groups)
            order(dve.tensor_scalar(group_rank, group_rank, 2.0, -BIG, ALU.is_ge, ALU.mult))
            order(dve.tensor_tensor(quads, quads, group_rank.rearrange(
                "p t g -> p (t g)").unsqueeze(2).to_broadcast([P, tiles * groups, 4]), ALU.add))
            rank_steps(order, dve, biased, work, work2, ties, rank, n)
            order(dve.tensor_scalar(rank, rank, 4.0, None, ALU.is_lt))
            dve.memset(combine[:, :, n:n + 1], 1.0)
            order(dve.tensor_tensor(logits, scores, rank.rearrange("p (t e) -> p t e", e=n),
                                    ALU.mult))
            order(dve.tensor_reduce(total, logits, AX, ALU.add))
            order(dve.tensor_scalar(total, total, 1e-20, None, ALU.add))
            order(dve.reciprocal(total, total))
            order(dve.tensor_tensor(combine[:, :, 0:n], logits, total.to_broadcast([P, tiles, n]),
                                    ALU.mult))
    turn_combine(chip, combine, combine_t, n + 1)
    expert_stage(chip, a, pre, 12, lambda f, cols: (sel[:n + 1, f], combine_t[:n + 1, cols]),
                 chip.state)
    norm_stage(chip, chip.inner, chip.state, (P, P), B * S, 1e-5)


def expert_stage(chip, a, pre, tiles, spread, addend):
    gate_up, down = a[pre + "gate_up_tiles"], a[pre + "down_tiles"]

    def tile(f):
        def loads(to_gate_up, to_down):
            return [(to_gate_up, fm(gate_up[f])), (to_down, down[f])]
        return P, loads

    gated_stage(chip, chip.state, [tile(f) for f in range(tiles)], ACT.Silu, chip.inner, addend,
                spread=spread)


def layer3_attention(chip, a):
    pre = "L3_attn_"
    at = Attention(chip, 16, 16, NT, 0.25, "band")
    cos, sin = chip.tables(16)
    fill_slots_stage(chip, at)
    load_stage(chip, [(cos, a["rope_l3_cos"].rearrange("p (t e) -> p t e", t=NT)),
                      (sin, a["rope_l3_sin"].rearrange("p (t e) -> p t e", t=NT)),
                      (chip.masks[:, :], a["mask_band128"]),
                      (chip.w_in[:, :, :], fm(a[pre + "Wqkv"])),
                      (chip.w_out[:, 0:4, :], fm(a[pre + "Wout_slots"]))])
    masks = (chip.masks[:, 0:256], chip.masks[:, 256:512])
    for b in range(B):
        jobs = []
        for t in range(NT):
            tok = slice(b * S + t * P, b * S + (t + 1) * P)
            products = []
            for lo, hi in ((0, BANK), (BANK, 3 * D)):
                products += [(chip.state[:, c, tok], chip.w_in[:, c, lo:hi], lo, c == 0, c == 1)
                             for c in range(2)]
            jobs.append((products, [
                (at.raw_q[:, t * D:(t + 1) * D], lambda ps: ps[:, 0:D]),
                (at.raw_k[:, t * D:(t + 1) * D], lambda ps: ps[:, D:2 * D]),
                (at.v[:, t, :, 0:16], lambda ps: ps[:, 2 * D:3 * D].rearrange(
                    "p (h e) -> p h e", e=16))]))
        q_post = HeadPost(chip, at, at.raw_q, at.q, NT, 16, None, None, cos, sin)
        k_post = HeadPost(chip, at, at.raw_k, at.k, NT, 16, None, None, cos, sin)
        project_stage(chip, [], jobs, q_post, k_post)
        split_stage(chip, at, split_jobs(at, at.raw_q, at.q, NT, 16, at.Q_PARTS)
                    + split_jobs(at, at.raw_k, at.k, NT, 16, at.K_PARTS))
        attend_stage(chip, at, 0, masks)
        out_stage(chip, at.outT, b, 4, None, chip.state, chip.inner)
    norm_stage(chip, chip.inner, chip.state, (P, P), B * S, 1e-5)


def layer3_cross(chip, a):
    cross_attention(chip, a, "L3_xattn_", 16, clip=CLIP / 16 ** -0.5)


def layer3_ffn(chip, a):
    pre, n, real, tiles = "L3_ffn_", 40, 32, B * NT
    router = chip.carve(8192, 2, n)
    logits, scores, biased = (chip.carve(8272 + i * tiles * n, tiles, n) for i in range(3))
    bias = chip.carve(9232, n)
    total = chip.carve(9272, tiles, 1)
    rank = chip.carve(9280, tiles * n)
    combine_t = chip.carve(9600, B * S)
    sel = chip.carve(10624, real + 1, P)
    ties = chip.carve(14848, n * n)
    router_logits_stage(chip, logits, router, [
        (router, fm(a[pre + "classifier_weight_t"])),
        (bias, a[pre + "e_score_correction_bias"].unsqueeze(0).partition_broadcast(P)),
        (ties, a["ties40"].partition_broadcast(P)), (sel[:n], a["sel_l3"])], n)
    nc, sig = chip.nc, chip.stage("route")
    larger, equal = chip.carve(16448, n * n), chip.carve(18048, n * n)
    with nc.Block() as block:
        @block.gpsimd
        def _(pool):
            chip.reset_others(pool, sig)

        @block.scalar
        def _(act):
            act.wait_ge(sig["shifted_ready"], 1)
            act.activation(scores, logits, ACT.Exp).then_inc(sig["scores_ready"], 1)

        @block.vector
        def _(dve):
            order = Order(dve, sig["order"])
            order(dve.tensor_reduce(total, logits, AX, ALU.max))
            dve.tensor_tensor(logits, logits, total.to_broadcast([P, tiles, n]),
                              ALU.subtract).then_inc(sig["shifted_ready"], 1)
            dve.wait_ge(sig["scores_ready"], 1)
            order(dve.tensor_reduce(total, scores, AX, ALU.add))
            order(dve.reciprocal(total, total))
            order(dve.tensor_tensor(scores, scores, total.to_broadcast([P, tiles, n]), ALU.mult))
            order(dve.tensor_tensor(biased, scores,
                                    bias.unsqueeze(1).to_broadcast([P, tiles, n]), ALU.add))
            for t in range(tiles):
                v = biased[:, t]
                mine = v.unsqueeze(2).to_broadcast([P, n, n])
                other = v.unsqueeze(1).to_broadcast([P, n, n])
                dve.tensor_tensor(larger.rearrange("p (i j) -> p i j", j=n), other, mine,
                                  ALU.is_gt)
                order(dve.tensor_tensor(equal.rearrange("p (i j) -> p i j", j=n), other, mine,
                                        ALU.is_equal))
                order(dve.tensor_tensor(equal, equal, ties, ALU.mult))
                order(dve.tensor_tensor(larger, larger, equal, ALU.add))
                order(dve.tensor_reduce(rank[:, t * n:(t + 1) * n],
                                        larger.rearrange("p (i j) -> p i j", j=n), AX, ALU.add))
            order(dve.tensor_scalar(rank, rank, 6.0, 2.5, ALU.is_lt, ALU.mult))
            order(dve.tensor_tensor(biased, scores, rank.rearrange("p (t e) -> p t e", e=n),
                                    ALU.mult))
    turn_combine(chip, biased, combine_t, n)
    sig = chip.stage("small")
    with nc.Block() as block:
        @block.gpsimd
        def _(pool):
            chip.reset_others(pool, sig)

        @block.tensor
        def _(pe):
            for h in range(2):
                mm = pe.matmul(chip.psum[:, h], sel[:n, real],
                               combine_t[:n, h * BANK:(h + 1) * BANK], start=True, stop=True)
            mm.then_inc(sig["pe_done"], 1)

        @block.vector
        def _(dve):
            dve.wait_ge(sig["pe_done"], 1)
            for m in range(2):
                for h in range(2):
                    cols = slice(h * BANK, (h + 1) * BANK)
                    dve.scalar_tensor_tensor(chip.normed[:, m, cols], chip.psum[:, h], 1.0,
                                             chip.state[:, m, cols], ALU.add,
                                             ALU.mult).then_inc(sig["dve_done"], 1)
    expert_stage(chip, a, pre, real, lambda f, cols: (sel[:n, f], combine_t[:n, cols]),
                 chip.normed)
    norm_stage(chip, chip.inner, chip.state, (P, P), B * S, 1e-5)


LAYERS = [layer0_attention, layer0_cross, layer0_ffn, layer1_linear_attention, layer1_cross,
          layer1_ffn, layer2_attention, layer2_cross, layer2_ffn, layer3_attention, layer3_cross,
          layer3_ffn]


COLUMNS = ("w", "g", "b", "bo", "b2")


def host_arrays(inputs):
    import numpy as np
    lay = np.ascontiguousarray
    a = {n: lay(v) for n, v in inputs.items() if n not in ("x", "ctx_768", "mask_BxS2_bk0")}
    a["x_fm"] = lay(inputs["x"].reshape(B * S, D).T)
    a["ctx_fm"] = lay(inputs["ctx_768"].reshape(B * SC, DC).T)
    for n, v in inputs.items():
        if n.split("_")[-1] in COLUMNS and v.shape[-1] == D:
            v = v.reshape(-1, 2, P).transpose(2, 0, 1)
            a[n + "_col"] = lay(v.reshape(P, -1))
    w = inputs["L0_ffn_Wqkv"].reshape(6, D, 3, 4, D).transpose(0, 3, 1, 2, 4)
    a["L0_ffn_Wqkv_groups"] = lay(w.reshape(24, D, 3 * D))
    b1 = inputs["L0_ffn_b1"].reshape(6, 2, 682)
    b1 = np.concatenate([b1, np.zeros((6, 2, 768 - 682), b1.dtype)], -1)
    a["L0_ffn_b1_col"] = lay(b1.reshape(6 * 12, P).T)
    for n in ("L1_attn_Wq", "L1_attn_Wk", "L1_attn_Wv", "L1_attn_Wo", "L2_xattn_Wq",
              "L2_xattn_Wlkv", "L2_xattn_Wkv", "L2_xattn_Wo", "L2_ffn_router_w",
              "L3_ffn_classifier_weight"):
        a[n + "_t"] = lay(inputs[n].T)
    proj = inputs["L1_attn_proj"]
    diag = np.zeros((2, 8, 16, 8, 64), proj.dtype)
    for h in range(16):
        diag[h // 8, h % 8, :, h % 8, :] = proj[h].T
    a["L1_attn_proj_diag"] = diag.reshape(2, P, 512)
    pre = "L2_attn_"
    w_q, w_k = (inputs[pre + n].transpose(1, 0, 2).reshape(D, 4, D) for n in ("W_Q", "W_K"))
    w_v = inputs[pre + "W_V"].reshape(4, P, D).transpose(2, 0, 1)
    a[pre + "W_groups"] = lay(np.concatenate([w_q, w_k, w_v], 2).transpose(1, 0, 2))
    a[pre + "b_groups"] = lay(np.concatenate(
        [inputs[pre + "b_Q"].reshape(4, D), inputs[pre + "b_K"].reshape(4, D),
         inputs[pre + "b_V"].reshape(4, P)], 1))
    for n in ("L0_attn_g_wo", "L0_attn_l_wo", "L0_xattn_Wo", "L2_attn_W_O", "L3_attn_Wout",
              "L3_xattn_Wo"):
        w = inputs[n].reshape(-1, 16, D)
        a[n + "_slots"] = lay(np.concatenate([w, np.zeros_like(w)], 1).reshape(-1, D))
    for n in ("ln_x_g", "ln_x_b"):
        v = inputs["L2_xattn_" + n]
        a[f"L2_xattn_{n}_col"] = lay(np.concatenate([v, v[:D - DC]]).reshape(2, P).T)
    mask = inputs["mask_BxS2_bk0"]
    a["mask_cols"] = lay(mask.reshape(B * SC // P, P).T)
    pre = "L2_ffn_"
    routed = [inputs[pre + n].reshape(8, 2, D, 64).transpose(0, 2, 1, 3).reshape(8, D, P)
              for n in ("gate_w", "up_w")]
    shared = [inputs[pre + n].reshape(4, P, D).transpose(0, 2, 1)
              for n in ("shared_gate_w", "shared_up_w")]
    a[pre + "gate_up_tiles"] = lay(np.concatenate(
        [np.concatenate(routed, 2), np.concatenate(shared, 2)], 0))
    a[pre + "down_tiles"] = lay(np.concatenate(
        [inputs[pre + "down_w"].reshape(8, P, D),
         inputs[pre + "shared_down_w"].T.reshape(4, P, D)], 0))
    a["L3_ffn_gate_up_tiles"] = lay(inputs["L3_ffn_gate_up_proj"][:32].transpose(0, 2, 1))
    a["L3_ffn_down_tiles"] = lay(inputs["L3_ffn_down_proj"].transpose(0, 2, 1))
    a.update(constants())
    return a


def kernel(**inputs):
    import concourse.bacc as bacc
    from concourse.bass_utils import run_bass_kernel_spmd

    arrays = host_arrays(inputs)
    nc = bacc.Bacc("TRN2", target_bir_lowering=False, num_devices=1)
    a = {n: nc.dram_tensor("in_" + n, v.shape, mybir.dt.from_np(v.dtype),
                           kind="ExternalInput").ap() for n, v in arrays.items()}
    out = nc.dram_tensor("out_fm", (D, B * S), F32, kind="ExternalOutput").ap()
    build(nc, a, out)
    r = run_bass_kernel_spmd(nc, [{"in_" + n: v for n, v in arrays.items()}], core_ids=[0])
    import numpy as np
    return np.ascontiguousarray(r.results[0]["out_fm"].T).reshape(B, S, D)
```
